# Optimizing a Trainium2 kernel written in Bass

```python
import numpy as np
import jax
import jax.numpy as jnp

def _softmax(x, axis=-1):
    return jax.nn.softmax(x, axis=axis)

def _gelu(x):
    return jax.nn.gelu(x, approximate=True)

def _silu(x):
    return jax.nn.silu(x)

def _sigmoid(x):
    return jax.nn.sigmoid(x)

def _layernorm(x, axis=-1, eps=1e-05):
    m = jnp.mean(x, axis=axis, keepdims=True)
    v = jnp.var(x, axis=axis, keepdims=True)
    return (x - m) / jnp.sqrt(v + eps)

def _scatter_add(tgt, idx, src, axis=0):
    return tgt.at[idx].add(src)

def _segment_sum(src, seg, n):
    return jax.ops.segment_sum(src, seg, n)
kernel_name = 'mk_flamingo_gated_d2_seqx_r8_1de002'

def setup_inputs(seed: int=0):
    np.random.seed(seed)
    _w = jnp.asarray

    def _rec_inputs():
        import jax
        import jax.numpy as jnp
        _rk = jax.random.key(seed)
        x = -0.0003929 + 0.9999 * jax.random.normal(jax.random.fold_in(_rk, 1), (32, 64, 512), jnp.float32)
        _lenS = 64 - jax.random.randint(jax.random.fold_in(_rk, 7), (32,), 0, max(1, 64 // 4) + 1, jnp.int32)
        _lenS2 = 64 - jax.random.randint(jax.random.fold_in(_rk, 8), (32,), 0, max(1, 64 // 4) + 1, jnp.int32)
        _ctx_4096P = jax.random.normal(jax.random.fold_in(_rk, 11), (32, 16, 512), jnp.float32)
        _ctx_4096c = jax.random.dirichlet(jax.random.fold_in(_rk, 511), 0.3 * jnp.ones((16,), jnp.float32), (32, 64))
        _ctx_4096t = jnp.einsum('bsk,bkd->bsd', _ctx_4096c, _ctx_4096P)
        _ctx_4096t = _ctx_4096t * jax.lax.rsqrt(jnp.mean(jnp.square(_ctx_4096t)) + 1e-12) * 0.953939
        ctx_4096 = 2.81802e-05 + 1.00001 * (_ctx_4096t + 0.3 * jax.random.normal(jax.random.fold_in(_rk, 611), (32, 64, 512), jnp.float32))
        _g = jax.random.normal(jax.random.fold_in(_rk, 9001), (2, 2), jnp.float32)
        _g = jnp.sign(_g) * jnp.maximum(jnp.abs(_g), 1.0) + (_g == 0) * 1.0
        g_xattn = _g[0]
        g_ffn = _g[1]
        return (x, ctx_4096, g_xattn, g_ffn)
    x, ctx_4096, g_xattn, g_ffn = _rec_inputs()

    def _L0_xattn_setup():
        import jax, jax.numpy as jnp
        import numpy as np
        DIM = 64
        HEADS = 8
        DIM_HEAD = 64
        HIDDEN = HEADS * DIM_HEAD
        SCALE = DIM_HEAD ** (-0.5)
        key = jax.random.key(seed)
        ks = jax.random.split(key, 9)
        b, n = (8, 512)
        std = 1.0 / np.sqrt(DIM)
        return {'q': jax.random.normal(ks[0], (b, DIM, n), jnp.float32), 'k': jax.random.normal(ks[1], (b, DIM, n), jnp.float32), 'v': jax.random.normal(ks[2], (b, DIM, n), jnp.float32), 'Wq': jax.random.normal(ks[3], (HIDDEN, DIM), jnp.float32) * std, 'Wk': jax.random.normal(ks[4], (HIDDEN, DIM), jnp.float32) * std, 'Wv': jax.random.normal(ks[5], (HIDDEN, DIM), jnp.float32) * std, 'Wo': jax.random.normal(ks[6], (DIM, HIDDEN), jnp.float32) * (1.0 / np.sqrt(HIDDEN)), 'bo': jax.random.normal(ks[7], (DIM,), jnp.float32) * 0.01, 'g': jnp.ones((1, DIM, 1), jnp.float32)}
    _L0_xattn_all = _L0_xattn_setup()
    _L0_xattn_in = {k: v for k, v in _L0_xattn_all.items() if k in ('Wq', 'Wk', 'Wv', 'Wo', 'bo', 'g')}
    del _L0_xattn_all

    def _L0_ffn_setup():
        import jax, jax.numpy as jnp
        import numpy as np
        N_STREAMS = 4
        DIM = 128
        SINKHORN_ITERS = 50
        SINKHORN_TAU = 0.1
        RMS_EPS = 1.1920929e-07

        def sinkhorn_log(logits, num_iters=SINKHORN_ITERS, tau=SINKHORN_TAU):
            Z = logits / tau
            u0 = jnp.zeros(Z.shape[:-1], Z.dtype)
            v0 = jnp.zeros_like(u0)

            def step(carry, _):
                u, v = carry
                u = -jax.nn.logsumexp(Z + v[..., None, :], axis=-1)
                v = -jax.nn.logsumexp(Z + u[..., :, None], axis=-2)
                return ((u, v), None)
            (u, v), _ = jax.lax.scan(step, (u0, v0), None, length=num_iters)
            return jnp.exp(Z + u[..., :, None] + v[..., None, :])
        key = jax.random.key(seed)
        ks = jax.random.split(key, 6)
        B, T = (4, 256)
        n, C = (N_STREAMS, DIM)
        wd = n * C
        x = jax.random.normal(ks[0], (B, T, wd), dtype=jnp.float32)
        W_res = 0.01 * jax.random.normal(ks[1], (n * n, wd), dtype=jnp.float32)
        W_pre = 0.01 * jax.random.normal(ks[2], (n, wd), dtype=jnp.float32)
        W_post = 0.01 * jax.random.normal(ks[3], (n, wd), dtype=jnp.float32)
        H_res_base = jnp.full((n, n), -0.5, dtype=jnp.float32)
        H_res_base = H_res_base.at[jnp.arange(n), jnp.arange(n)].set(0.0)
        H_pre_base = jnp.zeros((n,), dtype=jnp.float32).at[0].set(1.0)
        H_post_base = jnp.zeros((n,), dtype=jnp.float32)
        gate = jnp.array([5.0], dtype=jnp.float32)
        W_branch = 1.0 / np.sqrt(C) * jax.random.normal(ks[4], (C, C), dtype=jnp.float32)
        return {'x': x, 'W_res': W_res, 'W_pre': W_pre, 'W_post': W_post, 'H_res_base': H_res_base, 'H_pre_base': H_pre_base, 'H_post_base': H_post_base, 'gate': gate, 'W_branch': W_branch}
    _L0_ffn_all = _L0_ffn_setup()
    _L0_ffn_in = {k: v for k, v in _L0_ffn_all.items() if k in ('W_res', 'W_pre', 'W_post', 'H_res_base', 'H_pre_base', 'H_post_base', 'gate', 'W_branch')}
    del _L0_ffn_all

    def _L1_xattn_setup():
        import jax, jax.numpy as jnp
        import numpy as np
        EMB_DIM = 64
        HEADS = 8
        key = jax.random.key(seed)
        kq, kk, kv = jax.random.split(key, 3)
        B, C, N = (8, EMB_DIM, 512)
        q = jax.random.normal(kq, (B, C, N), dtype=jnp.float32)
        k = jax.random.normal(kk, (B, C, N), dtype=jnp.float32)
        v = jax.random.normal(kv, (B, C, N), dtype=jnp.float32)
        return {'q': q, 'k': k, 'v': v}
    _L1_xattn_all = _L1_xattn_setup()
    _L1_xattn_in = {k: v for k, v in _L1_xattn_all.items() if k in ()}
    del _L1_xattn_all

    def _L1_ffn_setup():
        import jax, jax.numpy as jnp
        import numpy as np
        H = 512
        I = 256
        E = 16
        TOPK = 4
        SI = 256
        key = jax.random.key(seed)
        ks = jax.random.split(key, 9)
        s = 0.02
        return {'hidden_states': jax.random.normal(ks[0], (2, 256, H), dtype=jnp.float32), 'gate_w': jax.random.normal(ks[1], (E, H), dtype=jnp.float32) * s, 'bias': jnp.zeros((E,), dtype=jnp.float32), 'Wg': jax.random.normal(ks[2], (E, I, H), dtype=jnp.float32) * s, 'Wu': jax.random.normal(ks[3], (E, I, H), dtype=jnp.float32) * s, 'Wd': jax.random.normal(ks[4], (E, H, I), dtype=jnp.float32) * s, 'Sg': jax.random.normal(ks[5], (SI, H), dtype=jnp.float32) * s, 'Su': jax.random.normal(ks[6], (SI, H), dtype=jnp.float32) * s, 'Sd': jax.random.normal(ks[7], (H, SI), dtype=jnp.float32) * s}
    _L1_ffn_all = _L1_ffn_setup()
    _L1_ffn_in = {k: v for k, v in _L1_ffn_all.items() if k in ('gate_w', 'bias', 'Wg', 'Wu', 'Wd', 'Sg', 'Su', 'Sd')}
    del _L1_ffn_all
    return {'x': x, 'ctx_4096': ctx_4096, 'g_xattn': g_xattn, 'g_ffn': g_ffn, 'L0_xattn_Wq': _L0_xattn_in['Wq'], 'L0_xattn_Wk': _L0_xattn_in['Wk'], 'L0_xattn_Wv': _L0_xattn_in['Wv'], 'L0_xattn_Wo': _L0_xattn_in['Wo'], 'L0_xattn_bo': _L0_xattn_in['bo'], 'L0_xattn_g': _L0_xattn_in['g'], 'L0_ffn_W_res': _L0_ffn_in['W_res'], 'L0_ffn_W_pre': _L0_ffn_in['W_pre'], 'L0_ffn_W_post': _L0_ffn_in['W_post'], 'L0_ffn_H_res_base': _L0_ffn_in['H_res_base'], 'L0_ffn_H_pre_base': _L0_ffn_in['H_pre_base'], 'L0_ffn_H_post_base': _L0_ffn_in['H_post_base'], 'L0_ffn_gate': _L0_ffn_in['gate'], 'L0_ffn_W_branch': _L0_ffn_in['W_branch'], 'L1_ffn_gate_w': _L1_ffn_in['gate_w'], 'L1_ffn_bias': _L1_ffn_in['bias'], 'L1_ffn_Wg': _L1_ffn_in['Wg'], 'L1_ffn_Wu': _L1_ffn_in['Wu'], 'L1_ffn_Wd': _L1_ffn_in['Wd'], 'L1_ffn_Sg': _L1_ffn_in['Sg'], 'L1_ffn_Su': _L1_ffn_in['Su'], 'L1_ffn_Sd': _L1_ffn_in['Sd']}

def reference(x, ctx_4096, g_xattn, g_ffn, L0_xattn_Wq, L0_xattn_Wk, L0_xattn_Wv, L0_xattn_Wo, L0_xattn_bo, L0_xattn_g, L0_ffn_W_res, L0_ffn_W_pre, L0_ffn_W_post, L0_ffn_H_res_base, L0_ffn_H_pre_base, L0_ffn_H_post_base, L0_ffn_gate, L0_ffn_W_branch, L1_ffn_gate_w, L1_ffn_bias, L1_ffn_Wg, L1_ffn_Wu, L1_ffn_Wd, L1_ffn_Sg, L1_ffn_Su, L1_ffn_Sd):
    import jax
    import jax.numpy as jnp

    def _L0_xattn_ref(q, k, v, Wq, Wk, Wv, Wo, bo, g):
        import jax, jax.numpy as jnp
        import numpy as np
        DIM = 64
        HEADS = 8
        DIM_HEAD = 64
        HIDDEN = HEADS * DIM_HEAD
        SCALE = DIM_HEAD ** (-0.5)
        b = q.shape[0]
        qh = jnp.einsum('bcn,oc->bon', q, Wq).reshape(b, HEADS, DIM_HEAD, -1)
        kh = jnp.einsum('bcn,oc->bon', k, Wk).reshape(b, HEADS, DIM_HEAD, -1)
        vh = jnp.einsum('bcn,oc->bon', v, Wv).reshape(b, HEADS, DIM_HEAD, -1)
        qh = jax.nn.softmax(qh, axis=-2) * SCALE
        kh = jax.nn.softmax(kh, axis=-1)
        context = jnp.einsum('bhdn,bhen->bhde', kh, vh)
        out = jnp.einsum('bhde,bhdn->bhen', context, qh)
        out = out.reshape(b, HIDDEN, -1)
        out = jnp.einsum('bcn,oc->bon', out, Wo) + bo[None, :, None]
        norm = jnp.maximum(jnp.sqrt(jnp.sum(out * out, axis=1, keepdims=True)), 1e-12)
        return out / norm * g * np.sqrt(DIM)

    def _L0_ffn_ref(x, W_res, W_pre, W_post, H_res_base, H_pre_base, H_post_base, gate, W_branch):
        import jax, jax.numpy as jnp
        import numpy as np
        N_STREAMS = 4
        DIM = 128
        SINKHORN_ITERS = 50
        SINKHORN_TAU = 0.1
        RMS_EPS = 1.1920929e-07

        def sinkhorn_log(logits, num_iters=SINKHORN_ITERS, tau=SINKHORN_TAU):
            Z = logits / tau
            u0 = jnp.zeros(Z.shape[:-1], Z.dtype)
            v0 = jnp.zeros_like(u0)

            def step(carry, _):
                u, v = carry
                u = -jax.nn.logsumexp(Z + v[..., None, :], axis=-1)
                v = -jax.nn.logsumexp(Z + u[..., :, None], axis=-2)
                return ((u, v), None)
            (u, v), _ = jax.lax.scan(step, (u0, v0), None, length=num_iters)
            return jnp.exp(Z + u[..., :, None] + v[..., None, :])
        B, T, nC = x.shape
        n = N_STREAMS
        C = nC // n
        x_norm = x * jax.lax.rsqrt(jnp.mean(x * x, axis=-1, keepdims=True) + RMS_EPS)
        H_res_logits = (x_norm @ W_res.T).reshape(B, T, n, n) + H_res_base
        H_pre_logits = x_norm @ W_pre.T + H_pre_base
        H_post_logits = x_norm @ W_post.T + H_post_base
        H_res = sinkhorn_log(H_res_logits)
        H_pre = jax.nn.softmax(H_pre_logits, axis=-1)
        H_post = jax.nn.softmax(H_post_logits, axis=-1)
        g = jax.nn.sigmoid(gate)[0]
        I = jnp.eye(n, dtype=H_res.dtype)
        H_res = (1.0 - g) * I + g * H_res
        x_streams = x.reshape(B, T, n, C)
        x_pre = jnp.einsum('btnc,btn->btc', x_streams, H_pre)
        y = x_pre @ W_branch
        x_mixed = jnp.einsum('btij,btjc->btic', H_res, x_streams)
        y_distributed = jnp.einsum('btc,btn->btnc', y, H_post)
        return (x_mixed + y_distributed).reshape(B, T, nC)

    def _L1_xattn_ref(q, k, v):
        import jax, jax.numpy as jnp
        import numpy as np
        EMB_DIM = 64
        HEADS = 8
        B, C, N = q.shape
        H = HEADS
        dh = C // H
        qh = q.transpose(0, 2, 1).reshape(B, N, H, dh)
        kh = k.transpose(0, 2, 1).reshape(B, N, H, dh)
        vh = v.transpose(0, 2, 1).reshape(B, N, H, dh)
        qh = jax.nn.softmax(qh, axis=3)
        kh = jax.nn.softmax(kh, axis=1)
        kvs = jnp.einsum('bnhd,bnhe->bhde', kh, vh)
        out = jnp.einsum('bnhd,bhde->bnhe', qh, kvs)
        return out.transpose(0, 2, 3, 1).reshape(B, C, N)

    def _L1_ffn_ref(hidden_states, gate_w, bias, Wg, Wu, Wd, Sg, Su, Sd):
        import jax, jax.numpy as jnp
        import numpy as np
        H = 512
        I = 256
        E = 16
        TOPK = 4
        SI = 256
        orig_shape = hidden_states.shape
        x = hidden_states.reshape(-1, orig_shape[-1])
        scores = jax.nn.sigmoid(x @ gate_w.T) + bias
        topk_w, topk_idx = jax.lax.top_k(scores, TOPK)
        topk_w = topk_w / (jnp.sum(topk_w, axis=-1, keepdims=True) + 1e-20)
        cw = jnp.sum(jax.nn.one_hot(topk_idx, E, dtype=x.dtype) * topk_w[..., None], axis=1)
        g = jnp.einsum('th,eih->eti', x, Wg)
        u = jnp.einsum('th,eih->eti', x, Wu)
        z = jax.nn.silu(g) * u
        zw = z * cw.T[:, :, None]
        out = jnp.einsum('eti,ehi->th', zw, Wd)
        out = out + jax.nn.silu(x @ Sg.T) * (x @ Su.T) @ Sd.T
        return out.reshape(orig_shape)
    x = x + jnp.tanh(g_xattn[0]) * _L0_xattn_ref(_layernorm(x, axis=-1), ctx_4096, ctx_4096, L0_xattn_Wq, L0_xattn_Wk, L0_xattn_Wv, L0_xattn_Wo, L0_xattn_bo, L0_xattn_g)
    x = x + jnp.tanh(g_ffn[0]) * _L0_ffn_ref(_layernorm(x, axis=-1), L0_ffn_W_res, L0_ffn_W_pre, L0_ffn_W_post, L0_ffn_H_res_base, L0_ffn_H_pre_base, L0_ffn_H_post_base, L0_ffn_gate, L0_ffn_W_branch)
    x = x + jnp.tanh(g_xattn[1]) * _L1_xattn_ref(_layernorm(x, axis=-1), ctx_4096, ctx_4096)
    x = x + jnp.tanh(g_ffn[1]) * _L1_ffn_ref(_layernorm(x, axis=-1), L1_ffn_gate_w, L1_ffn_bias, L1_ffn_Wg, L1_ffn_Wu, L1_ffn_Wd, L1_ffn_Sg, L1_ffn_Su, L1_ffn_Sd)
    return x

_drawn_inputs = setup_inputs


def setup_inputs(seed=0):
    import zlib

    import numpy as np

    out = dict(_drawn_inputs(seed))
    spreads = {'g_ffn': (-1.0, 0.6),
     'L0_xattn_g': (1.0, 0.2),
     'L0_ffn_H_post_base': (0.0, 0.8),
     'L1_ffn_bias': (0.0, 0.66)}
    factors = {'L0_ffn_W_pre': 3.004,
     'L0_ffn_W_post': 2.859,
     'L1_ffn_gate_w': 4.404,
     'L1_ffn_Wg': 3.579,
     'L1_ffn_Wu': 3.511,
     'L1_ffn_Wd': 3.507}
    for name, (base, spread) in spreads.items():
        noise = np.random.default_rng([zlib.crc32(name.encode()), seed]).standard_normal(out[name].shape)
        drawn = base * np.exp(spread * noise) if base else spread * noise
        out[name] = jnp.asarray(drawn.astype(out[name].dtype))
    for name, factor in factors.items():
        out[name] = (out[name] * factor).astype(out[name].dtype)
    return out
```

```python
from contextlib import ExitStack

import concourse.bass as bass
from concourse import mybir


class Count:

    def __init__(self, engine, semaphore):
        self.engine, self.semaphore = engine, semaphore
        self.value, self.index, self.per_turn = 0, 0, 0

    def loop(self, index, per_turn):
        self.index, self.per_turn, self.first = index, per_turn, self.value

    def done(self, turns):
        assert self.value == self.first + self.per_turn, (self.value - self.first, self.per_turn)
        self.value = self.first + turns * self.per_turn
        self.index, self.per_turn = 0, 0

    def mark(self, instruction):
        instruction.then_inc(self.semaphore, 1)
        self.value += 1
        return self.value

    def wait(self, mark=None):
        value = self.value if mark is None else mark
        self.engine.wait_ge(self.semaphore, self.index * self.per_turn + value if self.per_turn else value)

    def link(self, instruction):
        self.mark(instruction)
        self.wait()


def flamingo_program(nc, x, ctx_kv, wq, wk, wv, wo, bo, rms_gain, gates, w24, base24, sig_gate, w_branch,
                     gate_w, bias, wgu, wd, consts, out):
    f32, f32r, i32 = mybir.dt.float32, mybir.dt.float32r, mybir.dt.int32
    ALU, ACT, AX = mybir.AluOpType, mybir.ActivationFunctionType, mybir.AxisListType.X

    ROWS, N = x.shape
    P = 128
    T = ROWS // P
    C = 64
    HD = wq.shape[1]
    HC = HD // P
    NC = N // P
    HEADS = 8
    D = HD // HEADS
    SCALE = D ** -0.5
    DH1 = 8
    G1 = C // DH1
    S = 4
    TAU = 0.1
    ITERS = 50
    BLOCK = 7
    RMS_EPS = 1.1920929e-07
    LN_EPS = 1e-5
    E = gate_w.shape[1]
    IC = 2
    TB = 4
    TOPK = 4

    ctx = ExitStack()
    with ctx:
        def sb(name, shape, dt=f32):
            return ctx.enter_context(nc.sbuf_tensor(name, shape, dt))

        def sem(name):
            return ctx.enter_context(nc.semaphore(name))

        x_all = sb("x_all", [P, T, N])
        kv1_all = sb("kv1_all", [P, T, P])
        mv = sb("mv", [P, T, 2])
        rstd = sb("rstd", [P, T])
        ln_tmp = sb("ln_tmp", [P, 2, P])
        stats = sb("stats", [P, 2, 6])
        moments = sb("moments", [P, 2, 2])
        cst = sb("cst", [P, 2 * P + 2])
        ident, kv_mask, batch_of = cst[:, 0:P], cst[:, P:2 * P], cst[:, 2 * P:2 * P + 2]
        gts = sb("gts", [P, 4])
        tanh_g = sb("tanh_g", [P, 4])
        bo_sb = sb("bo_sb", [P, 1])
        rg_sb = sb("rg_sb", [P, 1])
        gain0 = sb("gain0", [P, 1])
        w24_sb = sb("w24_sb", [P, NC, 24])
        b24_sb = sb("b24_sb", [P, 24])
        sg_sb = sb("sg_sb", [P, 1])
        sgt = sb("sgt", [P, 4])
        wb_sb = sb("wb_sb", [P, P])
        gw_sb = sb("gw_sb", [P, NC, E])
        gwh = sb("gwh", [P, NC, E], f32r)
        gwl = sb("gwl", [P, NC, E], f32r)
        bias_sb = sb("bias_sb", [P, E])
        lg = sb("lg", [P, T, 24])
        cw = sb("cw", [P, E + 1, T])

        psum = [ctx.enter_context(nc.psum_tensor(f"bank{i}", [P, 512], f32)) for i in range(8)]
        (pk, pq, trk, trq, pg, pa, po, pm) = psum

        dma_w = sem("dma_w")
        dma_x = [sem(f"dma_x{i}") for i in range(4)]
        ctx_loaded = [sem(f"ctx_loaded{i}") for i in range(2)]
        dve_own = sem("dve_own")
        o_stored = sem("o_stored")
        s_tanh = sem("s_tanh")
        s_mt = sem("s_mt")
        s_mtc = sem("s_mtc")
        sctx_ready = sem("sctx_ready")
        sy_ready = sem("sy_ready")
        kp_done = sem("kp_done")
        kmax_ready = sem("kmax_ready")
        ek_ready = sem("ek_ready")
        tk_done = sem("tk_done")
        evk = sem("evk")
        qp_done = sem("qp_done")
        qsub_done = sem("qsub_done")
        eq_ready = sem("eq_ready")
        rq_ready = sem("rq_ready")
        p_ready = sem("p_ready")
        tq_done = sem("tq_done")
        evq = sem("evq")
        g_done = sem("g_done")
        gsb_done = sem("gsb_done")
        a_done = sem("a_done")
        at_done = sem("at_done")
        o_done = sem("o_done")
        sq_ready = sem("sq_ready")
        ssq_done = sem("ssq_done")
        ss_copied = sem("ss_copied")
        nm1_ready = sem("nm1_ready")
        e1_ready = sem("e1_ready")
        ct_done = sem("ct_done")
        ct_copied = sem("ct_copied")
        e1t_done = sem("e1t_done")
        e1t_copied = sem("e1t_copied")
        kv_done = sem("kv_done")
        kv_copied = sem("kv_copied")
        phase = sem("phase")
        out_stored = sem("out_stored")
        sp_passed = sem("sp_passed")
        waits_over = sem("waits_over")
        pool_passed = sem("pool_passed")
        pe_passed = sem("pe_passed")

        def rsqrt(own, v, y, a, b):
            own.link(nc.vector.tensor_scalar(y.bitcast(i32), v.bitcast(i32), 1, None, ALU.logical_shift_right))
            own.link(nc.vector.tensor_scalar(y.bitcast(i32), y.bitcast(i32), -1.0, 1597463007.0, ALU.mult, ALU.add))
            for _ in range(4):
                own.link(nc.vector.tensor_tensor(a, y, y, ALU.mult))
                own.link(nc.vector.tensor_tensor(b, a, v, ALU.mult))
                own.link(nc.vector.tensor_scalar(a, b, -0.5, 1.5, ALU.mult, ALU.add))
                own.link(nc.vector.tensor_tensor(y, y, a, ALU.mult))

        def ln_rstd(own):
            own.link(nc.vector.tensor_scalar(ln_tmp[:, 0, 0:T], mv[:, :, 1], LN_EPS, None, ALU.add))
            own.link(nc.vector.tensor_copy(ln_tmp[:, 0, 2 * T:3 * T], ln_tmp[:, 0, 0:T]))
            rsqrt(own, ln_tmp[:, 0, 2 * T:3 * T], rstd[:, :], ln_tmp[:, 1, 0:T], ln_tmp[:, 1, T:2 * T])

        O = ExitStack()
        o_all = O.enter_context(nc.sbuf_tensor("o_all", [P, T, N], f32))
        ss = O.enter_context(nc.sbuf_tensor("ss", [P, T, 2 * NC], f32))
        own = Count(nc.vector, dve_own)
        A = ExitStack()
        with A:
            def sa(name, shape, dt=f32):
                return A.enter_context(nc.sbuf_tensor(name, shape, dt))

            ct = sa("ct", [P, 2, N])
            wq32 = sa("wq32", [P, HD])
            wk32 = sa("wk32", [P, HD])
            wqh, wql = sa("wqh", [P, HD], f32r), sa("wql", [P, HD], f32r)
            wkh, wkl = sa("wkh", [P, HD], f32r), sa("wkl", [P, HD], f32r)
            wv_sb = sa("wv_sb", [P, HC, C])
            wo_sb = sa("wo_sb", [P, HC, C])
            mt = sa("mt", [P, HEADS, C])
            y32 = sa("y32", [P, N])
            sctx = sa("sctx", [P, 2, N], f32r)
            sy = sa("sy", [P, 2, N], f32r)
            ctxT = sa("ctxT", [P, 2, NC, P])
            e1 = sa("e1", [P, N])
            e1T = sa("e1T", [P, NC, P])
            nm1 = sa("nm1", [P, 1])
            s1 = sa("s1", [P, 2])
            nmax = sa("nmax", [P, 8])
            sk = sa("sk", [P, 8])
            rsk = sa("rsk", [P, 4])
            ek = sa("ek", [P, 2, N])
            ekT = sa("ekT", [P, 2, NC, HD])
            mx = sa("mx", [P, 2, HEADS])
            qs = sa("qs", [P, 2, HD])
            eq = sa("eq", [P, 4, HD])
            sumq = sa("sumq", [P, 4, HEADS])
            rq = sa("rq", [P, 4, HEADS])
            pq_sb = sa("pq_sb", [P, 4, HD])
            pT = sa("pT", [P, 2, HC, N])
            g_sb = sa("g_sb", [P, HD])
            aT = sa("aT", [P, HC, C])
            sq = sa("sq", [P, N])

            def at_least(engine, semaphore, value):
                if not isinstance(value, int) or value > 0:
                    engine.wait_ge(semaphore, value)

            def tiles(engine, tile, own=None):
                tile(0, 0, False, True, True)
                tile(1, 1, True, True, True)
                with engine.Fori(1, T // 2 - 1) as u:
                    if own:
                        own.loop(u - 1, 52)
                    tile(2 * u, 0, True, True, True)
                    tile(2 * u + 1, 1, True, True, True)
                if own:
                    own.done(T // 2 - 2)
                tile(T - 2, 0, True, True, True)
                tile(T - 1, 1, True, False, True)
                tile(T, 0, True, False, False)

            with nc.Block() as block:

                @block.sync
                def _(sp):
                    for dst, src in ((cst, consts), (wk32, wk), (wq32, wq), (bo_sb, bo), (rg_sb, rms_gain), (gts, gates),
                                     (b24_sb, base24), (sg_sb, sig_gate), (wb_sb, w_branch), (bias_sb, bias)):
                        sp.dma_start(dst[:, :], src).then_inc(dma_w, 16)
                    for dst, src in ((wv_sb, wv), (wo_sb, wo), (w24_sb, w24), (gw_sb, gate_w)):
                        sp.dma_start(dst[:, :, :], src.rearrange("(c p) n -> p c n", p=P)).then_inc(dma_w, 16)
                    for i in range(2):
                        sp.dma_start(ct[:, i, :], ctx_kv[i * P:(i + 1) * P, :]).then_inc(ctx_loaded[i], 16)
                    for i in range(4):
                        sp.dma_start(x_all[:, 4 * i:4 * i + 4, :],
                                     x[512 * i:512 * i + 512, :].rearrange("(t p) n -> p t n", p=P)).then_inc(dma_x[i], 16)

                    def refill(t, parity):
                        split_of, read, row = sp.snap(2 * t + 2), sp.snap(t + 1), sp.snap((t + 2) * P)
                        for semaphore, value in ((sctx_ready, split_of), (ct_done, read), (e1_ready, read)):
                            sp.wait_ge(semaphore, value)
                            sp.sem_inc(sp_passed)
                        sp.dma_start(ct[:, parity, :], ctx_kv[bass.ds(row, P), :]).then_inc(ctx_loaded[parity], 16)

                    with sp.Fori(0, (T - 2) // 2) as u:
                        refill(2 * u, 0)
                        refill(2 * u + 1, 1)

                NW = 14 * 16

                @block.tensor
                def _(pe):
                    pe.wait_ge(dma_w, NW)
                    for half in range(2):
                        for h in range(HEADS):
                            r = D * (h % 2)
                            last = nc.tensor.matmul((pk, pq)[h % 2][C * half:C * half + C, C * (h // 2):C * (h // 2) + C],
                                                    wv_sb[r:r + D, h // 2, :], wo_sb[r:r + D, h // 2, :],
                                                    start=True, stop=True)
                    last.then_inc(s_mt, 1)
                    pe.wait_ge(s_mtc, 2)

                    def prep(t, parity):
                        pe.wait_ge(ctx_loaded[parity], 16 * (t // 2 + 1) if isinstance(t, int) else 8 * (t - parity) + 16)
                        at_least(pe, kv_copied, t)
                        at_least(pe, ss_copied, t - 2)
                        for i in range(NC):
                            last = nc.tensor.transpose(pm[:, i * P:(i + 1) * P], ct[:, parity, i * P:(i + 1) * P], ident)
                        last.then_inc(ct_done, 1)

                    def prep2(t, parity):
                        pe.wait_ge(ct_copied, t + 1)
                        pe.wait_ge(e1_ready, t + 1)
                        for i in range(NC):
                            last = nc.tensor.transpose(pm[:, i * P:(i + 1) * P], e1[:, i * P:(i + 1) * P], ident)
                        last.then_inc(e1t_done, 1)

                    def prep3(t, parity):
                        pe.wait_ge(e1t_copied, t + 1)
                        for i in range(NC):
                            last = nc.tensor.matmul(pm[:, 0:P], e1T[:, i, :], ctxT[:, parity, i, :],
                                                    start=(i == 0), stop=(i == NC - 1))
                        last.then_inc(kv_done, 1)

                    def tile(t, parity, carry, with_prep, main):
                        for s in range(8):
                            b, c = s // 4, s % 4
                            g, j = 8 * t + s, 2 * t + b
                            old = carry or s > 0
                            if old and (main or s < 1):
                                at_least(pe, ek_ready, g)
                                at_least(pe, evk, g - 1)
                                for i in range(NC):
                                    last = nc.tensor.transpose(trk[:, i * P:(i + 1) * P],
                                                               ek[:, (s - 1) % 2, i * P:(i + 1) * P], ident)
                                last.then_inc(tk_done, 1)
                            if main:
                                pe.wait_ge(sctx_ready, j + 1)
                                at_least(pe, ek_ready, g)
                                nc.tensor.matmul(pk[:, :], wkh[:, c * P:(c + 1) * P], sctx[:, b, :], start=True, stop=False)
                                nc.tensor.matmul(pk[:, :], wkl[:, c * P:(c + 1) * P], sctx[:, b, :],
                                                 start=False, stop=True).then_inc(kp_done, 1)
                                pe.wait_ge(sy_ready, j + 1)
                                at_least(pe, qsub_done, g)
                                nc.tensor.matmul(pq[:, :], sy[:, b, c * P:(c + 1) * P], wqh[:, :], start=True, stop=False)
                                nc.tensor.matmul(pq[:, :], sy[:, b, c * P:(c + 1) * P], wql[:, :],
                                                 start=False, stop=True).then_inc(qp_done, 1)
                            if (carry or s > 2) and (main or s < 3):
                                at_least(pe, p_ready, g - 2)
                                at_least(pe, evq, g - 3)
                                for h in range(HC):
                                    last = nc.tensor.transpose(trq[:, h * P:(h + 1) * P],
                                                               pq_sb[:, (s - 3) % 4, h * P:(h + 1) * P], ident)
                                last.then_inc(tq_done, 1)
                            b1 = 1 - b
                            if (carry or b) and (main or not b):
                                if c == 1:
                                    at_least(pe, evk, 4 * j)
                                    at_least(pe, gsb_done, j - 1)
                                    for i in range(NC):
                                        last = nc.tensor.matmul(pg[C * b1:C * b1 + C, :],
                                                                ctxT[:, parity if b else 1 - parity, i, C * b1:C * b1 + C],
                                                                ekT[:, b1, i, :], start=(i == 0), stop=(i == NC - 1))
                                    last.then_inc(g_done, 1)
                                if c == 2:
                                    at_least(pe, gsb_done, j)
                                    at_least(pe, at_done, j - 1)
                                    for h in range(HC):
                                        last = nc.tensor.matmul(pa[:, h * P:(h + 1) * P],
                                                                g_sb[C * b1:C * b1 + C, h * P:(h + 1) * P],
                                                                mt[C * b1:C * b1 + C, 2 * h:2 * h + 2, :],
                                                                start=True, stop=True)
                                    last.then_inc(a_done, 1)
                                if c == 3:
                                    at_least(pe, at_done, j)
                                    at_least(pe, evq, 4 * j)
                                    if b:
                                        at_least(pe, sq_ready, t)
                                    for h in range(HC):
                                        last = nc.tensor.matmul(po[C * b1:C * b1 + C, :], aT[:, h, :], pT[:, b1, h, :],
                                                                start=(h == 0), stop=(h == HC - 1))
                                    last.then_inc(o_done, 1)
                            if s == 4 and with_prep:
                                prep(t + 1, 1 - parity)
                            if s == 5 and with_prep:
                                prep2(t + 1, 1 - parity)
                            if s == 6 and with_prep:
                                prep3(t + 1, 1 - parity)
                            if s == 7 and carry:
                                at_least(pe, sq_ready, t)
                                at_least(pe, kv_copied, t + 2 if with_prep else T)
                                for i in range(NC):
                                    last = nc.tensor.matmul(pm[:, P + 2 * i:P + 2 * i + 2], sq[:, i * P:(i + 1) * P],
                                                            batch_of, start=True, stop=True)
                                last.then_inc(ssq_done, 1)

                    prep(0, 0)
                    prep2(0, 0)
                    prep3(0, 0)
                    tiles(nc.tensor, tile)

                @block.scalar
                def _(act):
                    act.wait_ge(dma_w, NW)
                    nc.scalar.activation(tanh_g[:, :], gts[:, :], ACT.Tanh).then_inc(s_tanh, 1)
                    act.wait_ge(s_mt, 1)
                    for i in range(2):
                        nc.scalar.activation(mt[:, i:HEADS:2, :], (pk, pq)[i][:, 0:HEADS // 2 * C].rearrange(
                            "p (h c) -> p h c", c=C), ACT.Copy, scale=SCALE).then_inc(s_mtc, 1)

                    def prep(t, parity):
                        act.wait_ge(ct_done, t + 1)
                        if not isinstance(t, int) or t > 0:
                            at_least(act, g_done, 2 * t - 2)
                        nc.scalar.activation(ctxT[:, parity, :, :], pm[:, :].rearrange("p (i c) -> p i c", c=P),
                                             ACT.Copy).then_inc(ct_copied, 1)
                        act.wait_ge(nm1_ready, t + 1)
                        at_least(act, e1t_done, t)
                        nc.scalar.activation(e1[:, :], ct[:, parity, :], ACT.Exp, bias=nm1[:, :],
                                             accum_out=s1[:, 0:1]).then_inc(e1_ready, 1)

                    def prep2(t, parity):
                        act.wait_ge(e1t_done, t + 1)
                        at_least(act, kv_done, t)
                        nc.scalar.activation(e1T[:, :, :], pm[:, :].rearrange("p (i c) -> p i c", c=P),
                                             ACT.Copy).then_inc(e1t_copied, 1)

                    def tile(t, parity, carry, with_prep, main):
                        for s in range(8):
                            b, c = s // 4, s % 4
                            g, j = 8 * t + s, 2 * t + b
                            b1 = 1 - b
                            if main:
                                act.wait_ge(kmax_ready, g + 1)
                                at_least(act, tk_done, g - 1)
                                nc.scalar.activation(ek[:, s % 2, :], pk[:, :], ACT.Exp, bias=nmax[:, s:s + 1],
                                                     accum_out=sk[:, s:s + 1]).then_inc(ek_ready, 1)
                            if (carry or b) and (main or not b) and c == 2:
                                at_least(act, g_done, j)
                                at_least(act, a_done, j - 1)
                                nc.scalar.activation(g_sb[C * b1:C * b1 + C, :], pg[C * b1:C * b1 + C, :],
                                                     ACT.Copy).then_inc(gsb_done, 1)
                            if (carry or s > 0) and (main or s < 1):
                                bb = b if c else b1
                                at_least(act, tk_done, g)
                                at_least(act, g_done, j - 1 if c else j - 2)
                                nc.scalar.activation(ekT[:, bb, :, ((c - 1) % 4) * P:((c - 1) % 4 + 1) * P],
                                                     trk[:, :].rearrange("p (i c) -> p i c", c=P),
                                                     ACT.Copy).then_inc(evk, 1)
                            if main:
                                act.wait_ge(qsub_done, g + 1)
                                at_least(act, p_ready, g - 3)
                                nc.scalar.activation(eq[:, s % 4, :], qs[:, s % 2, :], ACT.Exp).then_inc(eq_ready, 1)
                            if (carry or s > 2) and (main or s < 3):
                                bb = b if c == 3 else b1
                                at_least(act, tq_done, g - 2)
                                at_least(act, o_done, j - 1 if c == 3 else j - 2)
                                i = (c - 3) % 4
                                nc.scalar.activation(pT[:, bb, :, i * P:(i + 1) * P],
                                                     trq[:, :].rearrange("p (h c) -> p h c", c=P),
                                                     ACT.Copy).then_inc(evq, 1)
                            if s == 4 and carry:
                                at_least(act, o_done, 2 * t)
                                nc.scalar.activation(o_all[:, t - 1, :] if isinstance(t, int) else
                                                     o_all[:, bass.ds(t - 1, 1), :], po[:, :], ACT.Identity,
                                                     bias=bo_sb[:, :]).then_inc(o_stored, 1)
                                at_least(act, ssq_done, t - 1)
                                nc.scalar.activation(sq[:, :], po[:, :], ACT.Square, bias=bo_sb[:, :]).then_inc(sq_ready, 1)
                            if s == 4 and with_prep:
                                prep(t + 1, 1 - parity)
                            if s == 5 and with_prep:
                                prep2(t + 1, 1 - parity)

                    prep(0, 0)
                    prep2(0, 0)
                    tiles(nc.scalar, tile)

                @block.gpsimd
                def _(pool):
                    def tile(t, parity, carry, with_prep, main):
                        for s in range(8):
                            if (carry or s > 0) and (main or s < 1):
                                g = 8 * t + s
                                k = (s - 1) % 4
                                at_least(pool, rq_ready, g)
                                at_least(pool, tq_done, g - 4)
                                nc.gpsimd.tensor_tensor(pq_sb[:, k, :].rearrange("p (h d) -> p h d", d=D),
                                                        eq[:, k, :].rearrange("p (h d) -> p h d", d=D),
                                                        rq[:, k, :].unsqueeze(2).broadcast_to([P, HEADS, D]),
                                                        ALU.mult).then_inc(p_ready, 1)

                    tiles(nc.gpsimd, tile)

                @block.vector
                def _(dve):
                    dve.wait_ge(dma_w, NW)
                    for w, hi, lo in ((wk32, wkh, wkl), (wq32, wqh, wql)):
                        own.link(nc.vector.tensor_copy(hi[:, :], w[:, :]))
                        own.mark(nc.vector.tensor_tensor(lo[:, :], w[:, :], hi[:, :].bitcast(f32), ALU.subtract))
                    own.link(nc.vector.tensor_copy(gwh[:, :, :], gw_sb[:, :, :]))
                    own.mark(nc.vector.tensor_tensor(gwl[:, :, :], gw_sb[:, :, :], gwh[:, :, :].bitcast(f32), ALU.subtract))
                    dve.wait_ge(s_tanh, 1)
                    own.link(nc.vector.tensor_scalar(gain0[:, :], rg_sb[:, :], tanh_g[:, 0:1], float(C) ** 0.5,
                                                     ALU.mult, ALU.mult))
                    for t in range(T):
                        dve.wait_ge(dma_x[t // 4], 16)
                        own.link(nc.vector.bn_stats(stats[:, 0, :], x_all[:, t, :]))
                        own.link(nc.vector.bn_aggr(mv[:, t, :], stats[:, 0, :]))
                    ln_rstd(own)

                    def split(source, parts, b, ready):
                        r, q = C * b, C * (1 - b)
                        own.link(nc.vector.tensor_copy(parts[r:r + C, b, :], source[r:r + C, :]))
                        nc.vector.tensor_tensor(parts[q:q + C, b, :], source[r:r + C, :],
                                                parts[r:r + C, b, :].bitcast(f32), ALU.subtract).then_inc(ready, 1)

                    def normed(t):
                        tt = bass.ds(t, 1)
                        if isinstance(t, int):
                            own.link(nc.vector.tensor_scalar(y32[:, :], x_all[:, t, :], mv[:, t, 0:1], rstd[:, t:t + 1],
                                                             ALU.subtract, ALU.mult))
                        else:
                            own.link(nc.vector.tensor_scalar(y32[:, :], x_all[:, tt, :], mv[:, tt, 0:1], rstd[:, tt],
                                                             ALU.subtract, ALU.mult))

                    def prep(t, parity):
                        dve.wait_ge(ctx_loaded[parity], 16 * (t // 2 + 1) if isinstance(t, int) else 8 * (t - parity) + 16)
                        at_least(dve, e1_ready, t)
                        nc.vector.tensor_reduce(nm1[:, :], ct[:, parity, :], AX, ALU.max, negate=True).then_inc(nm1_ready, 1)
                        at_least(dve, sy_ready, 2 * t)
                        normed(t)
                        at_least(dve, kp_done, 8 * t - 4)
                        split(ct[:, parity, :], sctx, 0, sctx_ready)
                        at_least(dve, qp_done, 8 * t - 4)
                        split(y32, sy, 0, sy_ready)

                    def prep_kv(t):
                        dve.wait_ge(kv_done, t + 1)
                        dve.wait_ge(e1_ready, t + 1)
                        own.link(nc.vector.reciprocal(s1[:, 1:2], s1[:, 0:1]))
                        where = kv1_all[:, t, :] if isinstance(t, int) else kv1_all[:, bass.ds(t, 1), :]
                        nc.vector.scalar_tensor_tensor(out=where, in0=pm[:, 0:P], scalar=s1[:, 1:2], in1=kv_mask,
                                                       op0=ALU.mult, op1=ALU.mult).then_inc(kv_copied, 1)

                    def tile(t, parity, carry, with_prep, main):
                        for s in range(8):
                            b, c = s // 4, s % 4
                            g, j = 8 * t + s, 2 * t + b
                            b1 = 1 - b
                            if main:
                                dve.wait_ge(kp_done, g + 1)
                                nc.vector.tensor_reduce(nmax[:, s:s + 1], pk[:, :], AX, ALU.max,
                                                        negate=True).then_inc(kmax_ready, 1)
                                dve.wait_ge(qp_done, g + 1)
                                logits = pq[:, :].rearrange("p (h d) -> p h d", d=D)
                                own.link(nc.vector.tensor_reduce(mx[:, s % 2, :], logits, AX, ALU.max))
                                at_least(dve, eq_ready, g - 1)
                                nc.vector.tensor_tensor(qs[:, s % 2, :].rearrange("p (h d) -> p h d", d=D), logits,
                                                        mx[:, s % 2, :].unsqueeze(2).broadcast_to([P, HEADS, D]),
                                                        ALU.subtract).then_inc(qsub_done, 1)
                            if (carry or s > 0) and (main or s < 1):
                                k = (s - 1) % 4
                                at_least(dve, eq_ready, g)
                                at_least(dve, rq_ready, g - 4)
                                own.link(nc.vector.reduce_sum(sumq[:, k, :], eq[:, k, :].rearrange("p (h d) -> p h d", d=D),
                                                              axis=AX))
                                at_least(dve, p_ready, g - 4)
                                nc.vector.reciprocal(rq[:, k, :], sumq[:, k, :]).then_inc(rq_ready, 1)
                            if (carry or b) and (main or not b) and c == 2:
                                at_least(dve, a_done, j)
                                at_least(dve, ek_ready, 4 * j)
                                own.link(nc.vector.reciprocal(rsk[:, :], sk[:, 4 * b1:4 * b1 + 4]))
                                at_least(dve, o_done, j - 1)
                                for half in range(2):
                                    r = slice(C * half, C * half + C)
                                    last = nc.vector.tensor_tensor(
                                        aT[r, :, :], pa[r, :].rearrange("p (h o) -> p h o", o=P)[:, :, C * half:C * half + C],
                                        rsk[r, :].unsqueeze(2).broadcast_to([C, HC, C]), ALU.mult)
                                    if half == 0:
                                        own.mark(last)
                                last.then_inc(at_done, 1)
                            if s == 0 and main:
                                at_least(dve, kp_done, 8 * t)
                                split(ct[:, parity, :], sctx, 1, sctx_ready)
                                at_least(dve, qp_done, 8 * t)
                                split(y32, sy, 1, sy_ready)
                            if s == 4 and with_prep:
                                prep(t + 1, 1 - parity)
                            if s == 7 and with_prep:
                                prep_kv(t + 1)
                            if s == 7 and carry:
                                at_least(dve, ssq_done, t)
                                src = pm[:, P:P + 2 * NC]
                                if isinstance(t, int):
                                    nc.vector.tensor_copy(ss[:, t - 1, :], src).then_inc(ss_copied, 1)
                                else:
                                    nc.vector.tensor_copy(ss[:, bass.ds(t - 1, 1), :], src).then_inc(ss_copied, 1)

                    prep(0, 0)
                    prep_kv(0)
                    tiles(nc.vector, tile, own)

        def at(tensor, t, *rest):
            alone = isinstance(t, int) and len(tensor.shape) > 2
            return tensor[(slice(None), t if alone else bass.ds(t, 1), *rest)]

        def at_least(engine, semaphore, value):
            if not isinstance(value, int) or value > 0:
                engine.wait_ge(semaphore, value)

        def turns(engine, n, body, own=None, per_turn=0):
            body(0)
            with engine.Fori(1, n) as u:
                if own:
                    own.loop(u - 1, per_turn)
                body(u)
            if own:
                own.done(n - 1)

        def row_stats(own, t, place):
            nc.vector.sem_inc(waits_over)
            own.link(nc.vector.bn_stats(stats[:, place, :], at(x_all, t)))
            nc.vector.sem_inc(waits_over)
            own.link(nc.vector.bn_aggr(moments[:, place, :], stats[:, place, :]))
            own.mark(nc.vector.tensor_scalar(at(mv, t), moments[:, place, :], 1.0, None, ALU.mult))

        r_all = O.enter_context(nc.sbuf_tensor("r_all", [P, T, 2 * NC], f32))
        rt = O.enter_context(nc.sbuf_tensor("rt", [P, 2, 2 * NC, C], f32))
        scaled = O.enter_context(nc.sbuf_tensor("scaled", [P, 2, N], f32))
        norm_ready = sem("norm_ready")
        rt_ready = sem("rt_ready")
        spread = sem("spread")
        x_normed = sem("x_normed")
        with nc.Block() as block:
            @block.scalar
            def _(act):
                act.wait_ge(norm_ready, 1)

                def step(t, parity, reuse):
                    if reuse:
                        act.wait_ge(spread, t - 1)
                    nc.scalar.activation(rt[:, parity, :, :],
                                         r_all[:, t if isinstance(t, int) else bass.ds(t, 1), :].rearrange(
                                             "p a k -> p (a k)" if not isinstance(t, int) else "p k -> p k")
                                         .unsqueeze(2).broadcast_to([P, 2 * NC, C]), ACT.Copy).then_inc(rt_ready, 1)

                step(0, 0, False)
                step(1, 1, False)
                with nc.scalar.Fori(0, (T - 2) // 2) as u:
                    step(2 * u + 2, 0, True)
                    step(2 * u + 3, 1, True)

            @block.tensor
            def _(pe):
                def step(t, parity, reuse):
                    pe.wait_ge(rt_ready, t + 1)
                    if reuse:
                        pe.wait_ge(x_normed, t - 1)
                    for i in range(NC):
                        last = nc.tensor.matmul(psum[parity][:, i * P:(i + 1) * P],
                                                rt[:, parity, 2 * i:2 * i + 2, :].rearrange("p b c -> p (b c)"),
                                                ident, start=True, stop=True)
                    last.then_inc(spread, 1)

                step(0, 0, False)
                step(1, 1, False)
                with nc.tensor.Fori(0, (T - 2) // 2) as u:
                    step(2 * u + 2, 0, True)
                    step(2 * u + 3, 1, True)

            @block.vector
            def _(dve):
                flat, rflat = ss[:, :, :].rearrange("p t k -> p (t k)"), r_all[:, :, :].rearrange("p t k -> p (t k)")
                own.link(nc.vector.tensor_scalar(flat, flat, 1e-24, None, ALU.max))
                rsqrt(own, flat, rflat, ln_tmp[:, 0, :], ln_tmp[:, 1, :])
                nc.vector.tensor_copy(ln_tmp[:, 0, 0:1], rflat[:, 0:1]).then_inc(norm_ready, 1)
                def pair(u):
                    for parity in range(2):
                        t = 2 * u + parity
                        dve.wait_ge(spread, t + 1)
                        nc.vector.tensor_tensor(scaled[:, parity, :], at(o_all, t), psum[parity][:, :],
                                                ALU.mult).then_inc(x_normed, 1)
                        dve.wait_ge(x_normed, t + 1)
                        own.link(nc.vector.scalar_tensor_tensor(out=at(x_all, t), in0=scaled[:, parity, :],
                                                                scalar=gain0[:, :], in1=at(x_all, t),
                                                                op0=ALU.mult, op1=ALU.add))
                        row_stats(own, t, parity)

                turns(nc.vector, T // 2, pair, own, 8)
                own.wait()
                ln_rstd(own)
        O.close()

        GROUP = 4

        def staggered(stages):
            for k in range(GROUP + max(lag for _, lag in stages)):
                for stage, lag in stages:
                    if 0 <= k - lag < GROUP:
                        stage(k - lag)

        H = ExitStack()
        zz = H.enter_context(nc.sbuf_tensor("zz", [P, T, S * S], f32))
        pp = H.enter_context(nc.sbuf_tensor("pp", [P, T, 2, S], f32))

        with ExitStack() as R:
            y4 = R.enter_context(nc.sbuf_tensor("y4", [P, GROUP, N], f32))
            yT = R.enter_context(nc.sbuf_tensor("yT", [P, GROUP, NC, P], f32))
            y_ready, y_turned, yT_ready, lg_done, lg_copied = (
                sem(n) for n in ("y_ready", "y_turned", "yT_ready", "lg_done", "lg_copied"))
            with nc.Block() as block:
                @block.vector
                def _(dve):
                    def group(u):
                        at_least(dve, y_turned, GROUP * u)
                        for i in range(GROUP):
                            t = GROUP * u + i
                            nc.vector.tensor_scalar(y4[:, i, :], at(x_all, t), at(mv, t, slice(0, 1)), at(rstd, t),
                                                    ALU.subtract, ALU.mult).then_inc(y_ready, 1)
                    turns(nc.vector, T // GROUP, group)
                    ms, v = ln_tmp[:, 0, 0:T], ln_tmp[:, 0, T:2 * T]
                    own.link(nc.vector.tensor_tensor(ms, rstd[:, :], rstd[:, :], ALU.mult))
                    own.link(nc.vector.tensor_tensor(ms, ms, mv[:, :, 1], ALU.mult))
                    own.link(nc.vector.tensor_scalar(v, ms, RMS_EPS, None, ALU.add))
                    rsqrt(own, v, ms, ln_tmp[:, 1, 0:T], ln_tmp[:, 1, T:2 * T])
                    at_least(dve, lg_copied, T)
                    own.link(nc.vector.tensor_tensor(lg[:, :, :], lg[:, :, :],
                                                     ms.unsqueeze(2).broadcast_to([P, T, 24]), ALU.mult))
                    own.link(nc.vector.tensor_tensor(lg[:, :, :], lg[:, :, :],
                                                     b24_sb[:, :].unsqueeze(1).broadcast_to([P, T, 24]), ALU.add))

                @block.tensor
                def _(pe):
                    def group(u):
                        def turn(i):
                            at_least(pe, y_ready, GROUP * u + i + 1)
                            if i == 0:
                                at_least(pe, yT_ready, GROUP * u)
                            for c in range(NC):
                                last = nc.tensor.transpose(psum[i][:, c * P:(c + 1) * P], y4[:, i, c * P:(c + 1) * P], ident)
                            last.then_inc(y_turned, 1)

                        def logits(i):
                            at_least(pe, yT_ready, GROUP * u + i + 1)
                            if i == 0:
                                at_least(pe, lg_copied, GROUP * u)
                            for c in range(NC):
                                last = nc.tensor.matmul(psum[4 + i][:, 0:24], yT[:, i, c, :], w24_sb[:, c, :],
                                                        start=(c == 0), stop=(c == NC - 1))
                            last.then_inc(lg_done, 1)

                        staggered(((turn, 0), (logits, 1)))

                    turns(nc.tensor, T // GROUP, group)

                @block.scalar
                def _(act):
                    def group(u):
                        def copy(i):
                            at_least(act, y_turned, GROUP * u + i + 1)
                            if i == 0:
                                at_least(act, lg_done, GROUP * u)
                            nc.scalar.activation(yT[:, i, :, :].rearrange("p c n -> p (c n)"), psum[i][:, :],
                                                 ACT.Copy).then_inc(yT_ready, 1)

                        def logits(i):
                            at_least(act, lg_done, GROUP * u + i + 1)
                            nc.scalar.activation(at(lg, GROUP * u + i), psum[4 + i][:, 0:24],
                                                 ACT.Copy).then_inc(lg_copied, 1)

                        staggered(((copy, 0), (logits, 2)))

                    turns(nc.scalar, T // GROUP, group)


        with ExitStack() as R:
            def rb(name, shape):
                return R.enter_context(nc.sbuf_tensor(name, shape, f32))

            kern, work = rb("kern", [P, T, S * S]), rb("work", [P, T, S * S])
            mxs, sums, ra, cb, logs = (rb(n, [P, T * S]) for n in ("mxs", "sums", "ra", "cb", "logs"))
            csum = rb("csum", [P, T * S])
            to_act, from_act = sem("to_act"), sem("from_act")
            calls = Count(nc.vector, from_act)

            def by_row(z):
                return z[:, :, :].rearrange("p t (i j) -> p (t i) j", j=S)

            def by_column(z):
                return z[:, :, :].rearrange("p t (i j) -> p t j i", j=S)

            def over_j(v):
                return v[:, :].unsqueeze(2).broadcast_to([P, T * S, S])

            def grid(z):
                return z[:, :, :].rearrange("p t (i j) -> p t i j", j=S)

            def over_i(v):
                return v[:, :].rearrange("p (t j) -> p t j", j=S).unsqueeze(2).broadcast_to([P, T, S, S])

            def flat(z):
                return z[:, :, :].rearrange("p t k -> p (t k)")

            pf = pp[:, :, :, :].rearrange("p t a k -> p (t a) k")
            with nc.Block() as block:
                @block.scalar
                def _(act):
                    n = [0]

                    def answer(out_, in_, func, index=None, **kw):
                        n[0] += 1
                        at_least(act, to_act, n[0] if index is None else 3 * index + n[0])
                        nc.scalar.activation(out_, in_, func, **kw).then_inc(from_act, 1)

                    answer(flat(work), flat(work), ACT.Exp)
                    answer(logs[:, :], sums[:, :], ACT.Ln)
                    answer(flat(work), flat(work), ACT.Exp)
                    answer(logs[:, :], sums[:, :], ACT.Ln)
                    answer(flat(kern), flat(zz), ACT.Exp)
                    with nc.scalar.Fori(0, (ITERS - 1) // BLOCK) as k:
                        answer(mxs[:, :], sums[:, :], ACT.Ln, k)
                        answer(logs[:, :], csum[:, :], ACT.Ln, k)
                        answer(flat(kern), flat(zz), ACT.Exp, k)
                    n[0] += 3 * ((ITERS - 1) // BLOCK - 1)
                    answer(pp[:, :, :, :].rearrange("p t a k -> p (t a k)"),
                           pp[:, :, :, :].rearrange("p t a k -> p (t a k)"), ACT.Exp)
                    answer(sgt[:, 0:1], sg_sb[:, :], ACT.Exp, scale=-1.0)

                @block.vector
                def _(dve):
                    V = nc.vector

                    def ask(instruction, wait=True):
                        instruction.then_inc(to_act, 1)
                        calls.value += 1
                        if wait:
                            calls.wait()

                    own.link(V.tensor_scalar(zz[:, :, :], lg[:, :, 0:S * S], 1.0 / TAU, None, ALU.mult))
                    own.link(V.tensor_reduce(mxs[:, :], by_row(zz), AX, ALU.max))
                    own.link(V.tensor_tensor(by_row(zz), by_row(zz), over_j(mxs), ALU.subtract))
                    ask(V.tensor_copy(flat(work), flat(zz)))
                    ask(V.reduce_sum(sums[:, :], by_row(work), axis=AX))
                    own.link(V.tensor_tensor(by_row(zz), by_row(zz), over_j(logs), ALU.subtract))
                    own.link(V.tensor_reduce(mxs[:, :].rearrange("p (t j) -> p t j", j=S), by_column(zz), AX, ALU.max))
                    own.link(V.tensor_tensor(grid(zz), grid(zz), over_i(mxs), ALU.subtract))
                    ask(V.tensor_copy(flat(work), flat(zz)))
                    ask(V.reduce_sum(sums[:, :].rearrange("p (t j) -> p t j", j=S), by_column(work), axis=AX))
                    ask(V.tensor_tensor(grid(zz), grid(zz), over_i(logs), ALU.subtract))
                    with V.Fori(0, (ITERS - 1) // BLOCK) as k:
                        own.loop(k, 6 * BLOCK - 1)
                        calls.loop(k, 3)
                        for n in range(BLOCK):
                            if n:
                                own.link(V.tensor_tensor(grid(work), grid(kern), over_i(cb), ALU.mult))
                            rows_done = V.reduce_sum(sums[:, :], by_row(work if n else kern), axis=AX)
                            own.link(rows_done)
                            own.link(V.reciprocal(ra[:, :], sums[:, :]))
                            own.link(V.tensor_tensor(by_row(work), by_row(kern), over_j(ra), ALU.mult))
                            own.link(V.reduce_sum(csum[:, :].rearrange("p (t j) -> p t j", j=S), by_column(work), axis=AX))
                            if n < BLOCK - 1:
                                own.link(V.reciprocal(cb[:, :], csum[:, :]))
                        ask(V.tensor_copy(cb[:, 0:1], csum[:, 0:1]), wait=False)
                        ask(V.tensor_copy(ra[:, 0:1], sums[:, 0:1]))
                        own.link(V.tensor_tensor(by_row(zz), by_row(zz), over_j(mxs), ALU.subtract))
                        ask(V.tensor_tensor(grid(zz), grid(zz), over_i(logs), ALU.subtract))
                        own.done((ITERS - 1) // BLOCK)
                        calls.done((ITERS - 1) // BLOCK)
                    pm_ = mxs[:, 0:2 * T]
                    own.link(V.tensor_copy(pf, lg[:, :, S * S:24].rearrange("p t (a k) -> p t a k", k=S)))
                    own.link(V.tensor_reduce(pm_, pf, AX, ALU.max))
                    ask(V.tensor_tensor(pf, pf, pm_.unsqueeze(2).broadcast_to([P, 2 * T, S]), ALU.subtract))
                    own.link(V.reduce_sum(pm_, pf, axis=AX))
                    own.link(V.reciprocal(sums[:, 0:2 * T], pm_))
                    own.link(V.tensor_tensor(pf, pf, sums[:, 0:2 * T].unsqueeze(2).broadcast_to([P, 2 * T, S]), ALU.mult))
                    ask(V.tensor_copy(logs[:, 0:1], pm_[:, 0:1]))
                    own.link(V.tensor_scalar(sgt[:, 1:2], sgt[:, 0:1], 1.0, None, ALU.add))
                    own.link(V.reciprocal(sgt[:, 2:3], sgt[:, 1:2]))
                    own.link(V.tensor_tensor(sgt[:, 3:4], sgt[:, 0:1], sgt[:, 2:3], ALU.mult))
                    own.link(V.tensor_scalar(zz[:, :, :], kern[:, :, :], sgt[:, 2:3], None, ALU.mult))
                    own.link(V.tensor_scalar(zz[:, :, 0:S * S:S + 1], zz[:, :, 0:S * S:S + 1], sgt[:, 3:4], None, ALU.add))
                    own.link(V.tensor_scalar(zz[:, :, :], zz[:, :, :], tanh_g[:, 2:3], None, ALU.mult))
                    own.link(V.tensor_scalar(pp[:, :, 1, :], pp[:, :, 1, :], tanh_g[:, 2:3], None, ALU.mult))

        with ExitStack() as R:
            y2 = R.enter_context(nc.sbuf_tensor("y2", [P, 2, N], f32))
            xp = R.enter_context(nc.sbuf_tensor("xp", [P, 2, P], f32))
            xpT = R.enter_context(nc.sbuf_tensor("xpT", [P, 2, P], f32))
            xp_ready, xp_turned, xpT_ready, yb_done = (sem(n) for n in ("xp_ready", "xp_turned", "xpT_ready", "yb_done"))
            with nc.Block() as block:
                @block.tensor
                def _(pe):
                    with nc.tensor.Fori(0, T // 2) as u:
                        for i in range(2):
                            t = 2 * u + i
                            at_least(pe, xp_ready, t + 1)
                            nc.tensor.transpose(psum[i][:, 0:P], xp[:, i, :], ident).then_inc(xp_turned, 1)
                            at_least(pe, xpT_ready, t + 1)
                            nc.tensor.matmul(psum[2 + i][:, 0:P], xpT[:, i, :], wb_sb[:, :],
                                             start=True, stop=True).then_inc(yb_done, 1)

                @block.scalar
                def _(act):
                    with nc.scalar.Fori(0, T // 2) as u:
                        for i in range(2):
                            at_least(act, xp_turned, 2 * u + i + 1)
                            nc.scalar.activation(xpT[:, i, :], psum[i][:, 0:P], ACT.Copy).then_inc(xpT_ready, 1)

                @block.vector
                def _(dve):
                    V = nc.vector
                    with V.Fori(0, T // 2) as u:
                        own.loop(u, 2 * (1 + S - 1 + S * S + S + 3))
                        for i in range(2):
                            t = 2 * u + i

                            def stream(tensor, k):
                                return at(tensor, t, slice(k * P, (k + 1) * P))

                            own.link(V.tensor_scalar(y2[:, i, :], at(x_all, t), at(mv, t, slice(0, 1)), at(rstd, t),
                                                     ALU.subtract, ALU.mult))
                            ys = [y2[:, i, k * P:(k + 1) * P] for k in range(S)]
                            for k in range(S):
                                w = at(pp, t, 0, slice(k, k + 1))
                                if k == 0:
                                    own.link(V.tensor_scalar(xp[:, i, :], ys[0], w, None, ALU.mult))
                                else:
                                    ins = V.scalar_tensor_tensor(out=xp[:, i, :], in0=ys[k], scalar=w, in1=xp[:, i, :],
                                                                 op0=ALU.mult, op1=ALU.add)
                                    if k < S - 1:
                                        own.link(ins)
                                    else:
                                        ins.then_inc(xp_ready, 1)
                            marks = {}
                            for j in range(S):
                                for k in range(S):
                                    if j:
                                        own.wait(marks[k])
                                    marks[k] = own.mark(V.scalar_tensor_tensor(
                                        out=stream(x_all, k), in0=ys[j], scalar=at(zz, t, slice(S * k + j, S * k + j + 1)),
                                        in1=stream(x_all, k), op0=ALU.mult, op1=ALU.add))
                            at_least(dve, yb_done, t + 1)
                            for k in range(S):
                                own.wait(marks[k])
                                own.mark(V.scalar_tensor_tensor(
                                    out=stream(x_all, k), in0=psum[2 + i][:, 0:P], scalar=at(pp, t, 1, slice(k, k + 1)),
                                    in1=stream(x_all, k), op0=ALU.mult, op1=ALU.add))
                            own.wait()
                            row_stats(own, t, i)
                        own.done(T // 2)
                    own.wait()
                    ln_rstd(own)
        H.close()

        with ExitStack() as R:
            def rc(name, shape):
                return R.enter_context(nc.sbuf_tensor(name, shape, f32))

            NG = N // DH1
            y4, q4, e4, p4, qT = (rc(n, [P, GROUP, N]) for n in ("y4c", "q4", "e4", "p4", "qT"))
            mx4, su4, rc4 = (rc(n, [P, GROUP, NG]) for n in ("mx4", "su4", "rc4"))
            kvf = rc("kvf", [P, GROUP, P])
            names = ("c2_y", "c2_yT", "c2_sub", "c2_exp", "c2_rcp", "c2_p", "c2_pT", "c2_qT", "c2_o", "c2_kv", "c2_x")
            y_rdy, y_trn, sub_rdy, exp_rdy, rcp_rdy, p_rdy, p_trn, qT_rdy, o_rdy, kvf_rdy, x_rdy = (sem(n) for n in names)

            def grouped(z):
                return z.rearrange("p (g d) -> p g d", d=DH1)

            def spread_g(v):
                return v.unsqueeze(2).broadcast_to([P, NG, DH1])

            with nc.Block() as block:
                @block.tensor
                def _(pe):
                    def group(u):
                        b = GROUP * u

                        def turn(i):
                            at_least(pe, y_rdy, b + i + 1)
                            at_least(pe, sub_rdy, b + max(i - 1, 0))
                            for c in range(NC):
                                last = nc.tensor.transpose(psum[i % 2][:, c * P:(c + 1) * P],
                                                           y4[:, i, c * P:(c + 1) * P], ident)
                            last.then_inc(y_trn, 1)

                        def back(i):
                            at_least(pe, p_rdy, b + i + 1)
                            at_least(pe, qT_rdy, b + max(i - 1, 0))
                            for c in range(NC):
                                last = nc.tensor.transpose(psum[2 + i % 2][:, c * P:(c + 1) * P],
                                                           p4[:, i, c * P:(c + 1) * P], ident)
                            last.then_inc(p_trn, 1)

                        def product(i):
                            at_least(pe, qT_rdy, b + i + 1)
                            at_least(pe, kvf_rdy, b + i + 1)
                            at_least(pe, x_rdy, b + max(i - 1, 0))
                            nc.tensor.matmul(psum[4 + i % 2][:, :], kvf[:, i, :], qT[:, i, :],
                                             start=True, stop=True).then_inc(o_rdy, 1)

                        staggered(((turn, 0), (back, 2), (product, 3)))

                    turns(nc.tensor, T // GROUP, group)

                @block.scalar
                def _(act):
                    def group(u):
                        b = GROUP * u

                        def exps(i):
                            at_least(act, sub_rdy, b + i + 1)
                            if i == 0:
                                at_least(act, p_rdy, b)
                            nc.scalar.activation(e4[:, i, :], q4[:, i, :], ACT.Exp).then_inc(exp_rdy, 1)

                        def copy(i):
                            at_least(act, p_trn, b + i + 1)
                            if i == 0:
                                at_least(act, o_rdy, b)
                            nc.scalar.activation(qT[:, i, :], psum[2 + i % 2][:, :], ACT.Copy).then_inc(qT_rdy, 1)

                        staggered(((exps, 0), (copy, 2)))

                    turns(nc.scalar, T // GROUP, group)

                @block.gpsimd
                def _(pool):
                    def group(u):
                        b = GROUP * u

                        def probs(i):
                            if i == 0:
                                at_least(pool, o_rdy, b)
                            nc.gpsimd.sem_inc(pool_passed)
                            nc.gpsimd.tensor_copy(kvf[:, i, :], at(kv1_all, b + i)).then_inc(kvf_rdy, 1)
                            at_least(pool, rcp_rdy, b + i + 1)
                            if i == 0:
                                at_least(pool, p_trn, b)
                            nc.gpsimd.tensor_tensor(grouped(p4[:, i, :]), grouped(e4[:, i, :]), spread_g(rc4[:, i, :]),
                                                    ALU.mult).then_inc(p_rdy, 1)

                        staggered(((probs, 0),))

                    turns(nc.gpsimd, T // GROUP, group)

                @block.vector
                def _(dve):
                    V = nc.vector
                    def group(u):
                        b = GROUP * u

                        def norm(i):
                            if i == 0:
                                at_least(dve, y_trn, b)
                            V.tensor_scalar(y4[:, i, :], at(x_all, b + i), at(mv, b + i, slice(0, 1)), at(rstd, b + i),
                                            ALU.subtract, ALU.mult).then_inc(y_rdy, 1)

                        def shift(i):
                            at_least(dve, y_trn, b + i + 1)
                            own.link(V.tensor_reduce(mx4[:, i, :], grouped(psum[i % 2][:, :]), AX, ALU.max))
                            if i == 0:
                                at_least(dve, exp_rdy, b)
                            V.tensor_tensor(grouped(q4[:, i, :]), grouped(psum[i % 2][:, :]), spread_g(mx4[:, i, :]),
                                            ALU.subtract).then_inc(sub_rdy, 1)

                        def sums_(i):
                            at_least(dve, exp_rdy, b + i + 1)
                            own.link(V.reduce_sum(su4[:, i, :], grouped(e4[:, i, :]), axis=AX))
                            if i == 0:
                                at_least(dve, p_rdy, b)
                            V.reciprocal(rc4[:, i, :], su4[:, i, :]).then_inc(rcp_rdy, 1)

                        def update(i):
                            at_least(dve, o_rdy, b + i + 1)
                            V.scalar_tensor_tensor(out=at(x_all, b + i), in0=psum[4 + i % 2][:, :],
                                                   scalar=tanh_g[:, 1:2], in1=at(x_all, b + i),
                                                   op0=ALU.mult, op1=ALU.add).then_inc(x_rdy, 1)
                            at_least(dve, x_rdy, b + i + 1)
                            row_stats(own, b + i, i % 2)

                        staggered(((norm, 0), (shift, 1), (sums_, 2), (update, 4)))

                    turns(nc.vector, T // GROUP, group, own, 5 * GROUP)
                    own.wait()
                    ln_rstd(own)

        xh = sb("xh", [P, NC, ROWS], f32r)
        xl = sb("xl", [P, NC, ROWS], f32r)
        NEVER = 3.0e38
        with ExitStack() as R:
            def rd(name, shape):
                return R.enter_context(nc.sbuf_tensor(name, shape, f32))

            y4 = rd("y4d", [P, GROUP, N])
            s16 = rd("s16", [E, 512])
            sc = rd("sc", [P, T, E])
            padded = rd("padded", [P, T, E + TOPK])
            top = rd("top", [P, T, 8])
            left = rd("left", [P, T, E + TOPK])
            tot = rd("tot", [P, 2, T])
            names = ("c3_y", "c3_yT", "c3_hi", "c3_lo", "c3_gate", "c3_gatec", "c3_score", "c3_scorec", "c3_sub", "c3_exp")
            y_rdy, y_trn, hi_rdy, lo_rdy, gate_rdy, gate_cp, sco_rdy, sco_cp, exp_ask, exp_ans = (sem(n) for n in names)
            with nc.Block() as block:
                @block.vector
                def _(dve):
                    V = nc.vector
                    def group(u):
                        b = GROUP * u

                        def norm(i):
                            if i == 0:
                                at_least(dve, y_trn, b)
                            V.tensor_scalar(y4[:, i, :], at(x_all, b + i), at(mv, b + i, slice(0, 1)), at(rstd, b + i),
                                            ALU.subtract, ALU.mult).then_inc(y_rdy, 1)

                        def low(i):
                            at_least(dve, hi_rdy, b + i + 1)
                            cols = bass.ds((b + i) * P, P)
                            V.tensor_tensor(xl[:, :, cols], psum[i][:, :].rearrange("p (c n) -> p c n", n=P),
                                            xh[:, :, cols].bitcast(f32), ALU.subtract).then_inc(lo_rdy, 1)

                        staggered(((norm, 0), (low, 1)))
                        at_least(dve, sco_rdy, u + 1)
                        V.tensor_copy(sc[:, bass.ds(b, GROUP), :],
                                      psum[5][:, 0:GROUP * E].rearrange("p (t e) -> p t e", e=E)).then_inc(sco_cp, 1)

                    turns(nc.vector, T // GROUP, group)
                    at_least(dve, sco_cp, T // GROUP)
                    flat_sc = sc[:, :, :].rearrange("p t e -> p (t e)")
                    V.tensor_copy(tot[:, 0, 0:1], flat_sc[:, 0:1]).then_inc(exp_ask, 1)
                    at_least(dve, exp_ans, 1)
                    own.link(V.tensor_scalar(flat_sc, flat_sc, 1.0, None, ALU.add))
                    own.link(V.reciprocal(flat_sc, flat_sc))
                    own.link(V.tensor_tensor(sc[:, :, :], sc[:, :, :],
                                             bias_sb[:, :].unsqueeze(1).broadcast_to([P, T, E]), ALU.add))
                    own.mark(V.memset(padded[:, :, E:E + TOPK], NEVER))
                    own.mark(V.memset(cw[:, :, :], 1.0))
                    own.link(V.tensor_copy(padded[:, :, 0:E], sc[:, :, :]))
                    for t in range(T):
                        own.mark(V.max(out=top[:, t, :], in_=padded[:, t, 0:E]))
                    own.wait()
                    own.link(V.memset(top[:, :, TOPK:8], NEVER))
                    for t in range(T):
                        own.mark(V.match_replace(out=left[:, t, :], in_to_replace=top[:, t, :], in_values=padded[:, t, :],
                                                 imm_value=-NEVER))
                    own.wait()
                    own.link(V.tensor_scalar(left[:, :, 0:E], left[:, :, 0:E], -1.0e38, None, ALU.is_lt))
                    own.link(V.tensor_tensor(left[:, :, 0:E], left[:, :, 0:E], sc[:, :, :], ALU.mult))
                    own.link(V.reduce_sum(tot[:, 0, :], left[:, :, 0:E], axis=AX))
                    own.link(V.tensor_scalar(tot[:, 0, :], tot[:, 0, :], 1e-20, None, ALU.add))
                    own.link(V.reciprocal(tot[:, 1, :], tot[:, 0, :]))
                    own.link(V.tensor_tensor(cw[:, 1:E + 1, :], left[:, :, 0:E].rearrange("p t e -> p e t"),
                                             tot[:, 1, :].unsqueeze(1).broadcast_to([P, E, T]), ALU.mult))
                    own.link(V.tensor_scalar(cw[:, :, :], cw[:, :, :], tanh_g[:, 3:4], None, ALU.mult))

                @block.scalar
                def _(act):
                    def group(u):
                        b = GROUP * u
                        for i in range(GROUP):
                            at_least(act, y_trn, b + i + 1)
                            nc.scalar.activation(xh[:, :, bass.ds((b + i) * P, P)],
                                                 psum[i][:, :].rearrange("p (c n) -> p c n", n=P),
                                                 ACT.Copy).then_inc(hi_rdy, 1)
                        at_least(act, gate_rdy, u + 1)
                        nc.scalar.activation(s16[:, :], psum[4][0:E, :], ACT.Copy).then_inc(gate_cp, 1)

                    turns(nc.scalar, T // GROUP, group)
                    at_least(act, exp_ask, 1)
                    flat_sc = sc[:, :, :].rearrange("p t e -> p (t e)")
                    nc.scalar.activation(flat_sc, flat_sc, ACT.Exp, scale=-1.0).then_inc(exp_ans, 1)

                @block.tensor
                def _(pe):
                    def group(u):
                        b = GROUP * u
                        for i in range(GROUP):
                            at_least(pe, y_rdy, b + i + 1)
                            if i == 0:
                                at_least(pe, lo_rdy, b)
                            for c in range(NC):
                                last = nc.tensor.transpose(psum[i][:, c * P:(c + 1) * P], y4[:, i, c * P:(c + 1) * P], ident)
                            last.then_inc(y_trn, 1)
                        at_least(pe, lo_rdy, b + GROUP)
                        at_least(pe, gate_cp, u)
                        for c in range(NC):
                            for k, (w, v) in enumerate(((gwh, xh), (gwl, xh), (gwh, xl), (gwl, xl))):
                                last = nc.tensor.matmul(psum[4][0:E, :], w[:, c, :], v[:, c, bass.ds(u * 512, 512)],
                                                        start=(c == 0 and k == 0), stop=(c == NC - 1 and k == 3))
                        last.then_inc(gate_rdy, 1)
                        at_least(pe, gate_cp, u + 1)
                        at_least(pe, sco_cp, u)
                        nc.tensor.sem_inc(pe_passed)
                        for i in range(GROUP):
                            last = nc.tensor.transpose(psum[5][:, i * E:(i + 1) * E], s16[:, i * P:(i + 1) * P],
                                                       ident[0:E, 0:E])
                        last.then_inc(sco_rdy, 1)

                    turns(nc.tensor, T // GROUP, group)


        with ExitStack() as R:
            GU, DN = 2 * NC * IC * P, IC * N
            w32 = R.enter_context(nc.sbuf_tensor("w32", [P, GU + DN], f32))
            wh = [R.enter_context(nc.sbuf_tensor(f"wh{i}", [P, GU + DN], f32r)) for i in range(2)]
            wl = [R.enter_context(nc.sbuf_tensor(f"wl{i}", [P, GU + DN], f32r)) for i in range(2)]
            sg2 = R.enter_context(nc.sbuf_tensor("sg2", [P, IC, 512], f32))
            z32 = R.enter_context(nc.sbuf_tensor("z32", [P, IC, 512], f32))
            zh = R.enter_context(nc.sbuf_tensor("zh", [P, 2, IC, 512], f32r))
            zl = R.enter_context(nc.sbuf_tensor("zl", [P, 2, IC, 512], f32r))
            names = ("w_loaded", "w_high", "w_split", "gu_done", "silu_done", "z_mult", "z_ready", "down_done",
                     "acc_done")
            w_loaded, w_high, w_split, gu_done, silu_done, z_mult, z_ready, down_done, acc_done = (
                sem(n) for n in names)

            def all_experts(engine, expert, count=None, per_turn=0):
                expert(0, 0, False)
                with engine.Fori(0, E // 2) as u:
                    if count:
                        count.loop(u, 2 * per_turn)
                    expert(2 * u + 1, 1, True)
                    expert(2 * u + 2, 0, True)
                if count:
                    count.done(E // 2)

            with nc.Block() as block:
                @block.sync
                def _(sp):
                    def load(row):
                        sp.dma_start(w32[:, 0:GU], wgu[row, :]).then_inc(w_loaded, 16)
                        sp.dma_start(w32[:, GU:GU + DN], wd[row, :]).then_inc(w_loaded, 16)

                    load(slice(0, P))
                    with sp.Fori(1, E + 1) as n:
                        row = sp.snap(n * P)
                        sp.wait_ge(w_split, sp.snap(n + 0))
                        sp.sem_inc(sp_passed)
                        load(bass.ds(row, P))
                    for tb in range(TB):
                        sp.wait_ge(acc_done, 4 * (TB * E + tb + 1))
                        sp.dma_start(out[512 * tb:512 * tb + 512, :].rearrange("(t p) n -> p t n", p=P),
                                     x_all[:, 4 * tb:4 * tb + 4, :]).then_inc(out_stored, 16)
                    sp.wait_ge(out_stored, 16 * TB)

                @block.gpsimd
                def _(pool):
                    def split(n, parity):
                        pool.wait_ge(w_loaded, 32 * n + 32)
                        at_least(pool, down_done, 4 * TB * (n - 1))
                        nc.gpsimd.sem_inc(pool_passed)
                        nc.gpsimd.tensor_copy(wh[parity][:, :], w32[:, :]).then_inc(w_high, 1)
                        pool.wait_ge(w_high, n + 1)
                        nc.gpsimd.tensor_tensor(wl[parity][:, :], w32[:, :], wh[parity][:, :].bitcast(f32),
                                                ALU.subtract).then_inc(w_split, 1)

                    split(0, 0)
                    split(1, 1)
                    split(2, 0)
                    with nc.gpsimd.Fori(1, E // 2) as u:
                        split(2 * u + 1, 1)
                        split(2 * u + 2, 0)

                @block.tensor
                def _(pe):
                    def gate_up(n, parity, tb, ic):
                        hi, lo = wh[parity], wl[parity]
                        k = TB * n + tb
                        at_least(pe, z_ready, 2 * k - 1 + ic)
                        if tb == 0 and ic == 0:
                            pe.wait_ge(w_split, n + 1)
                        for m in range(2):
                            for c in range(NC):
                                first = ((m * NC) + c) * IC * P + ic * P
                                cols = slice(512 * tb, 512 * tb + 512)
                                for q, (w, v) in enumerate(((hi, xh), (lo, xh), (hi, xl))):
                                    last = nc.tensor.matmul(psum[2 * ic + m][:, :], w[:, first:first + P], v[:, c, cols],
                                                            start=(c == 0 and q == 0), stop=(c == NC - 1 and q == 2))
                        last.then_inc(gu_done, 1)

                    def down(n, parity, tb):
                        hi, lo = wh[parity], wl[parity]
                        k = TB * n + tb
                        pe.wait_ge(z_ready, 2 * k + 2)
                        at_least(pe, acc_done, 4 * k)
                        for tt in range(4):
                            for ic in range(IC):
                                first = GU + ic * N
                                cols = slice(tt * P, tt * P + P)
                                for q, (z, w) in enumerate(((zh, hi), (zh, lo), (zl, hi))):
                                    last = nc.tensor.matmul(psum[4 + tt][:, :], z[:, tb % 2, ic, cols],
                                                            w[:, first:first + N], start=(ic == 0 and q == 0),
                                                            stop=(ic == IC - 1 and q == 2))
                            last.then_inc(down_done, 1)

                    def expert(n, parity, carry):
                        for tb in range(TB):
                            gate_up(n, parity, tb, 0)
                            gate_up(n, parity, tb, 1)
                            if tb:
                                down(n, parity, tb - 1)
                            elif carry:
                                down(n - 1, 1 - parity, TB - 1)

                    all_experts(nc.tensor, expert)
                    down(E, 0, TB - 1)

                @block.scalar
                def _(act):
                    def expert(n, parity, carry):
                        for tb in range(TB):
                            for ic in range(IC):
                                k = TB * n + tb
                                act.wait_ge(gu_done, 2 * k + ic + 1)
                                at_least(act, z_mult, 2 * k + ic - 1)
                                nc.scalar.activation(sg2[:, ic, :], psum[2 * ic][:, :], ACT.Silu).then_inc(silu_done, 1)

                    all_experts(nc.scalar, expert)

                @block.vector
                def _(dve):
                    V = nc.vector

                    def hidden(n, tb, ic):
                        k = TB * n + tb
                        dve.wait_ge(silu_done, 2 * k + ic + 1)
                        V.tensor_tensor(z32[:, ic, :], sg2[:, ic, :], psum[2 * ic + 1][:, :],
                                        ALU.mult).then_inc(z_mult, 1)
                        dve.wait_ge(z_mult, 2 * k + ic + 1)
                        at_least(dve, down_done, 4 * (k - 1))
                        own.link(V.tensor_copy(zh[:, tb % 2, ic, :], z32[:, ic, :]))
                        V.tensor_tensor(zl[:, tb % 2, ic, :], z32[:, ic, :], zh[:, tb % 2, ic, :].bitcast(f32),
                                        ALU.subtract).then_inc(z_ready, 1)

                    def add(n, tb):
                        for tt in range(4):
                            t = 4 * tb + tt
                            dve.wait_ge(down_done, 4 * (TB * n + tb) + tt + 1)
                            V.scalar_tensor_tensor(out=x_all[:, t, :], in0=psum[4 + tt][:, :],
                                                   scalar=at(cw, n, slice(t, t + 1)), in1=x_all[:, t, :],
                                                   op0=ALU.mult, op1=ALU.add).then_inc(acc_done, 1)

                    def expert(n, parity, carry):
                        for tb in range(TB):
                            hidden(n, tb, 0)
                            hidden(n, tb, 1)
                            if tb:
                                add(n, tb - 1)
                            elif carry:
                                add(n - 1, TB - 1)

                    all_experts(nc.vector, expert, own, IC * TB)
                    add(E, TB - 1)


def kernel(x, ctx_4096, g_xattn, g_ffn, L0_xattn_Wq, L0_xattn_Wk, L0_xattn_Wv, L0_xattn_Wo, L0_xattn_bo, L0_xattn_g,
           L0_ffn_W_res, L0_ffn_W_pre, L0_ffn_W_post, L0_ffn_H_res_base, L0_ffn_H_pre_base, L0_ffn_H_post_base,
           L0_ffn_gate, L0_ffn_W_branch, L1_ffn_gate_w, L1_ffn_bias, L1_ffn_Wg, L1_ffn_Wu, L1_ffn_Wd,
           L1_ffn_Sg, L1_ffn_Su, L1_ffn_Sd):
    import numpy as np
    import concourse.bacc as bacc
    from concourse.bass_utils import run_bass_kernel_spmd

    def a(v):
        return np.asarray(v)

    def rows(v, n=128):
        return np.broadcast_to(a(v).reshape(1, -1), (n, a(v).size))

    def twice(v):
        return np.concatenate([a(v), a(v)], axis=0)

    B, C, N = x.shape
    H = L1_ffn_Sg.shape[1]
    I = L1_ffn_Sg.shape[0]
    E = L1_ffn_Wg.shape[0]
    P = 128

    def by_partition(w):
        k, m = w.shape
        return w.reshape(k // P, P, m).transpose(1, 0, 2).reshape(P, -1)

    gates_up = [np.stack([by_partition(a(g).T), by_partition(a(u).T)], axis=1)
                for g, u in [(L1_ffn_Sg, L1_ffn_Su)] + list(zip(a(L1_ffn_Wg), a(L1_ffn_Wu)))]
    downs = [by_partition(a(d).T) for d in [L1_ffn_Sd] + list(a(L1_ffn_Wd))]
    consts = np.zeros((P, 2 * P + 2), np.float32)
    consts[:, :P] = np.eye(P)
    consts[:, P:2 * P] = np.kron(np.eye(P // 8), np.ones((8, 8)))
    consts[:, 2 * P:] = np.kron(np.eye(2), np.ones((P // 2, 1)))
    arrays = {
        "x": a(x).reshape(B * C, N),
        "ctx_kv": a(ctx_4096).reshape(B * C, N),
        "wq": twice(a(L0_xattn_Wq).T),
        "wk": twice(a(L0_xattn_Wk).T),
        "wv": a(L0_xattn_Wv),
        "wo": a(L0_xattn_Wo).T,
        "bo": twice(a(L0_xattn_bo).reshape(C, 1)),
        "rms_gain": twice(a(L0_xattn_g).reshape(C, 1)),
        "gates": rows(np.concatenate([a(g_xattn), a(g_ffn)])),
        "w24": np.concatenate([a(L0_ffn_W_res), a(L0_ffn_W_pre), a(L0_ffn_W_post)], axis=0).T,
        "base24": rows(np.concatenate([a(L0_ffn_H_res_base).reshape(-1), a(L0_ffn_H_pre_base), a(L0_ffn_H_post_base)])),
        "sig_gate": rows(L0_ffn_gate),
        "w_branch": a(L0_ffn_W_branch),
        "gate_w": a(L1_ffn_gate_w).T,
        "bias": rows(L1_ffn_bias),
        "wgu": np.stack(gates_up).reshape((E + 1) * P, -1),
        "wd": np.stack(downs).reshape((E + 1) * P, -1),
        "consts": consts,
    }
    arrays = {f"in_{k}": np.ascontiguousarray(v) for k, v in arrays.items()}
    nc = bacc.Bacc("TRN2", target_bir_lowering=False, num_devices=1)
    args = [nc.dram_tensor(k, v.shape, mybir.dt.from_np(v.dtype), kind="ExternalInput").ap() for k, v in arrays.items()]
    out = nc.dram_tensor("out", (B * C, N), mybir.dt.float32, kind="ExternalOutput").ap()
    flamingo_program(nc, *args, out)
    r = run_bass_kernel_spmd(nc, [arrays], core_ids=[0])
    return r.results[0]["out"].reshape(B, C, N)
```

```python
from contextlib import ExitStack

import concourse.bass as bass
from concourse import mybir


class Count:

    def __init__(self, engine, semaphore):
        self.engine, self.semaphore = engine, semaphore
        self.value, self.index, self.per_turn = 0, 0, 0

    def loop(self, index, per_turn):
        self.index, self.per_turn, self.first = index, per_turn, self.value

    def done(self, turns):
        assert self.value == self.first + self.per_turn, (self.value - self.first, self.per_turn)
        self.value = self.first + turns * self.per_turn
        self.index, self.per_turn = 0, 0

    def mark(self, instruction):
        instruction.then_inc(self.semaphore, 1)
        self.value += 1
        return self.value

    def wait(self, mark=None):
        value = self.value if mark is None else mark
        self.engine.wait_ge(self.semaphore, self.index * self.per_turn + value if self.per_turn else value)

    def link(self, instruction):
        self.mark(instruction)
        self.wait()


def flamingo_program(nc, x, ctx_kv, wq, wk, wv, wo, bo, rms_gain, gates, w24, base24, sig_gate, w_branch,
                     gate_w, bias, wgu, wd, consts, out):
    f32, f32r, i32 = mybir.dt.float32, mybir.dt.float32r, mybir.dt.int32
    ALU, ACT, AX = mybir.AluOpType, mybir.ActivationFunctionType, mybir.AxisListType.X

    ROWS, N = x.shape
    P = 128
    T = ROWS // P
    C = 64
    HD = wq.shape[1]
    HC = HD // P
    NC = N // P
    HEADS = 8
    D = HD // HEADS
    SCALE = D ** -0.5
    DH1 = 8
    G1 = C // DH1
    S = 4
    TAU = 0.1
    ITERS = 50
    BLOCK = 16
    REFRESHES = 2
    LAST = ITERS - 1 - REFRESHES * BLOCK
    RMS_EPS = 1.1920929e-07
    LN_EPS = 1e-5
    E = gate_w.shape[1]
    IC = 2
    TB = 4
    TOPK = 4

    ctx = ExitStack()
    with ctx:
        def sb(name, shape, dt=f32):
            return ctx.enter_context(nc.sbuf_tensor(name, shape, dt))

        def sem(name):
            return ctx.enter_context(nc.semaphore(name))

        x_all = sb("x_all", [P, T, N])
        kv1_all = sb("kv1_all", [P, T, P])
        mv = sb("mv", [P, T, 2])
        rstd = sb("rstd", [P, T])
        ln_tmp = sb("ln_tmp", [P, 2, P])
        stats = sb("stats", [P, 2, 6])
        moments = sb("moments", [P, 2, 2])
        cst = sb("cst", [P, 2 * P + 2])
        ident, kv_mask, batch_of = cst[:, 0:P], cst[:, P:2 * P], cst[:, 2 * P:2 * P + 2]
        gts = sb("gts", [P, 4])
        tanh_g = sb("tanh_g", [P, 4])
        bo_sb = sb("bo_sb", [P, 1])
        rg_sb = sb("rg_sb", [P, 1])
        gain0 = sb("gain0", [P, 1])
        w24_sb = sb("w24_sb", [P, NC, 24])
        b24_sb = sb("b24_sb", [P, 24])
        sg_sb = sb("sg_sb", [P, 1])
        sgt = sb("sgt", [P, 4])
        wb_sb = sb("wb_sb", [P, P])
        gw_sb = sb("gw_sb", [P, NC, E])
        gwh = sb("gwh", [P, NC, E], f32r)
        gwl = sb("gwl", [P, NC, E], f32r)
        bias_sb = sb("bias_sb", [P, E])
        lg = sb("lg", [P, T, 24])
        cw = sb("cw", [P, E + 1, T])

        psum = [ctx.enter_context(nc.psum_tensor(f"bank{i}", [P, 512], f32)) for i in range(8)]
        pk, pq, tr, pg, po, pm = psum[0], psum[1:3], psum[3], psum[4], psum[5:7], psum[7]

        dma_w = sem("dma_w")
        dma_x = [sem(f"dma_x{i}") for i in range(4)]
        ctx_loaded = [sem(f"ctx_loaded{i}") for i in range(2)]
        dve_own = sem("dve_own")
        o_stored = sem("o_stored")
        s_tanh = sem("s_tanh")
        s_mt = sem("s_mt")
        s_mtc = sem("s_mtc")
        sctx_ready = sem("sctx_ready")
        sy_ready = sem("sy_ready")
        kp_done = sem("kp_done")
        kmax_ready = sem("kmax_ready")
        ek_ready = sem("ek_ready")
        tk_done = sem("tk_done")
        evk = sem("evk")
        qp_done = sem("qp_done")
        qsub_done = sem("qsub_done")
        eq_ready = sem("eq_ready")
        rq_ready = sem("rq_ready")
        p_ready = sem("p_ready")
        tq_done = sem("tq_done")
        evq = sem("evq")
        ctx_high = sem("ctx_high")
        y_high = sem("y_high")
        y32_ready = sem("y32_ready")
        g_done = sem("g_done")
        gsb_done = sem("gsb_done")
        a_done = sem("a_done")
        at_done = sem("at_done")
        o_done = sem("o_done")
        ot_ready = sem("ot_ready")
        o_turned = sem("o_turned")
        half_summed = sem("half_summed")
        quarters_ready = sem("quarters_ready")
        sq_ready = sem("sq_ready")
        ssq_done = sem("ssq_done")
        ss_copied = sem("ss_copied")
        nm1_ready = sem("nm1_ready")
        e1_ready = sem("e1_ready")
        ct_done = sem("ct_done")
        ct_copied = sem("ct_copied")
        e1t_done = sem("e1t_done")
        e1t_copied = sem("e1t_copied")
        kv_done = sem("kv_done")
        kv_copied = sem("kv_copied")
        phase = sem("phase")
        out_stored = sem("out_stored")
        sp_passed = sem("sp_passed")
        waits_over = sem("waits_over")
        pool_passed = sem("pool_passed")
        pe_passed = sem("pe_passed")

        def at(tensor, t, *rest):
            alone = isinstance(t, int) and len(tensor.shape) > 2
            return tensor[(slice(None), t if alone else bass.ds(t, 1), *rest)]

        def rsqrt(own, v, y, a, b):
            own.link(nc.vector.tensor_scalar(y.bitcast(i32), v.bitcast(i32), 1, None, ALU.logical_shift_right))
            own.link(nc.vector.tensor_scalar(y.bitcast(i32), y.bitcast(i32), -1.0, 1597463007.0, ALU.mult, ALU.add))
            for _ in range(4):
                own.link(nc.vector.tensor_tensor(a, y, y, ALU.mult))
                own.link(nc.vector.tensor_tensor(b, a, v, ALU.mult))
                own.link(nc.vector.tensor_scalar(a, b, -0.5, 1.5, ALU.mult, ALU.add))
                own.link(nc.vector.tensor_tensor(y, y, a, ALU.mult))

        def ln_rstd(own, t0=0, t1=T):
            v, p, q = ln_tmp[:, 0, t0:t1], ln_tmp[:, 1, t0:t1], ln_tmp[:, 1, T + t0:T + t1]
            own.link(nc.vector.tensor_scalar(v, mv[:, t0:t1, 1], LN_EPS, None, ALU.add))
            rsqrt(own, v, rstd[:, t0:t1], p, q)

        O = ExitStack()
        o_all = O.enter_context(nc.sbuf_tensor("o_all", [P, T, N], f32))
        ss = O.enter_context(nc.sbuf_tensor("ss", [P, T, 2 * NC], f32))
        own = Count(nc.vector, dve_own)
        A = ExitStack()
        with A:
            def sa(name, shape, dt=f32):
                return A.enter_context(nc.sbuf_tensor(name, shape, dt))

            ct = sa("ct", [P, 2, N])
            wq32 = sa("wq32", [P, HD])
            wk32 = sa("wk32", [P, HD])
            wqh, wql = sa("wqh", [P, HD], f32r), sa("wql", [P, HD], f32r)
            wkh, wkl = sa("wkh", [P, HD], f32r), sa("wkl", [P, HD], f32r)
            wv_sb = sa("wv_sb", [P, HC, C])
            wo_sb = sa("wo_sb", [P, HC, C])
            mt = sa("mt", [P, HEADS, C])
            y32 = sa("y32", [P, N])
            sctx = sa("sctx", [P, 2, N], f32r)
            sy = sa("sy", [P, 2, N], f32r)
            ctxT = sa("ctxT", [P, 2, NC, P])
            e1 = sa("e1", [P, N])
            e1T = sa("e1T", [P, NC, P])
            nm1 = sa("nm1", [P, 1])
            s1 = sa("s1", [P, 2])
            nmax = sa("nmax", [P, 8])
            sk = sa("sk", [P, 8])
            rsk = sa("rsk", [P, 4])
            ek = sa("ek", [P, 2, N])
            ekT = sa("ekT", [P, 4, NC, P])
            mx = sa("mx", [P, 2, HEADS])
            qs = sa("qs", [P, 2, HD])
            eq = sa("eq", [P, 4, HD])
            sumq = sa("sumq", [P, 4, HEADS])
            rq = sa("rq", [P, 4, HEADS])
            pq_sb = sa("pq_sb", [P, 4, HD])
            pT = sa("pT", [P, 8, HC, P])
            g_sb = sa("g_sb", [P, HD])
            aT = sa("aT", [P, 2, HC, C])
            sq = sa("sq", [P, N])
            oT = sa("oT", [P, N])
            halves = sa("halves", [P, HEADS, D // 2])
            quarters = sa("quarters", [P, 2, HEADS, D // 4])

            def at_least(engine, semaphore, value):
                if not isinstance(value, int) or value > 0:
                    engine.wait_ge(semaphore, value)

            def tiles(engine, tile, own=None, per_pair=0):
                tile(0, 0)
                tile(1, 1)
                with engine.Fori(1, T // 2 - 1) as u:
                    if own:
                        own.loop(u - 1, per_pair)
                    tile(2 * u, 0)
                    tile(2 * u + 1, 1)
                if own:
                    own.done(T // 2 - 2)
                for t in range(T - 2, T + 2):
                    tile(t, t % 2)

            def real(t, s, behind):
                return not isinstance(t, int) or 0 <= 8 * t + s - behind < 8 * T

            with nc.Block() as block:

                @block.sync
                def _(sp):
                    for dst, src in ((cst, consts), (wk32, wk), (wq32, wq), (bo_sb, bo), (rg_sb, rms_gain), (gts, gates),
                                     (b24_sb, base24), (sg_sb, sig_gate), (wb_sb, w_branch), (bias_sb, bias)):
                        sp.dma_start(dst[:, :], src).then_inc(dma_w, 16)
                    for dst, src in ((wv_sb, wv), (wo_sb, wo), (w24_sb, w24), (gw_sb, gate_w)):
                        sp.dma_start(dst[:, :, :], src.rearrange("(c p) n -> p c n", p=P)).then_inc(dma_w, 16)
                    for i in range(2):
                        sp.dma_start(ct[:, i, :], ctx_kv[i * P:(i + 1) * P, :]).then_inc(ctx_loaded[i], 16)
                    for i in range(4):
                        sp.dma_start(x_all[:, 4 * i:4 * i + 4, :],
                                     x[512 * i:512 * i + 512, :].rearrange("(t p) n -> p t n", p=P)).then_inc(dma_x[i], 16)

                    def refill(t, parity):
                        split_of, read, row = sp.snap(2 * t + 2), sp.snap(t + 1), sp.snap((t + 2) * P)
                        for semaphore, value in ((sctx_ready, split_of), (ct_done, read), (e1_ready, read)):
                            sp.wait_ge(semaphore, value)
                            sp.sem_inc(sp_passed)
                        sp.dma_start(ct[:, parity, :], ctx_kv[bass.ds(row, P), :]).then_inc(ctx_loaded[parity], 16)

                    with sp.Fori(0, (T - 2) // 2) as u:
                        refill(2 * u, 0)
                        refill(2 * u + 1, 1)

                NW = 14 * 16

                @block.tensor
                def _(pe):
                    pe.wait_ge(dma_w, NW)
                    for half in range(2):
                        for h in range(HEADS):
                            r = D * (h % 2)
                            last = nc.tensor.matmul((pk, tr)[h % 2][C * half:C * half + C, C * (h // 2):C * (h // 2) + C],
                                                    wv_sb[r:r + D, h // 2, :], wo_sb[r:r + D, h // 2, :],
                                                    start=True, stop=True)
                    last.then_inc(s_mt, 1)
                    pe.wait_ge(s_mtc, 2)

                    def prep(t, parity):
                        pe.wait_ge(ctx_loaded[parity], 16 * (t // 2 + 1) if isinstance(t, int) else 8 * (t - parity) + 16)
                        at_least(pe, at_done, 2 * t - 1 + (0 if isinstance(t, int) and t == 0 else -1))
                        at_least(pe, kv_copied, t)
                        for i in range(NC):
                            last = nc.tensor.transpose(pm[:, i * P:(i + 1) * P], ct[:, parity, i * P:(i + 1) * P], ident)
                        last.then_inc(ct_done, 1)

                    def prep2(t, parity):
                        pe.wait_ge(ct_copied, t + 1)
                        pe.wait_ge(e1_ready, t + 1)
                        for i in range(NC):
                            last = nc.tensor.transpose(pm[:, i * P:(i + 1) * P], e1[:, i * P:(i + 1) * P], ident)
                        last.then_inc(e1t_done, 1)

                    def prep3(t, parity):
                        pe.wait_ge(e1t_copied, t + 1)
                        for i in range(NC):
                            last = nc.tensor.matmul(pm[:, 0:P], e1T[:, i, :], ctxT[:, parity, i, :],
                                                    start=(i == 0), stop=(i == NC - 1))
                        last.then_inc(kv_done, 1)

                    def tile(t, parity):
                        for s in range(8):
                            b, c = s // 4, s % 4
                            g, j = 8 * t + s, 2 * t + b
                            if real(t, s, 1):
                                at_least(pe, ek_ready, g)
                                at_least(pe, evq, g - 3)
                                for i in range(NC):
                                    last = nc.tensor.transpose(tr[:, i * P:(i + 1) * P],
                                                               ek[:, (s - 1) % 2, i * P:(i + 1) * P], ident)
                                last.then_inc(tk_done, 1)
                            if real(t, s, 0):
                                pe.wait_ge(sy_ready, j + 1)
                                at_least(pe, qsub_done, g - 1)
                                nc.tensor.matmul(pq[s % 2][:, :], sy[:, b, c * P:(c + 1) * P], wqh[:, :],
                                                 start=True, stop=False)
                                nc.tensor.matmul(pq[s % 2][:, :], sy[:, b, c * P:(c + 1) * P], wql[:, :],
                                                 start=False, stop=True).then_inc(qp_done, 1)
                                pe.wait_ge(sctx_ready, j + 1)
                                at_least(pe, ek_ready, g)
                                nc.tensor.matmul(pk[:, :], wkh[:, c * P:(c + 1) * P], sctx[:, b, :],
                                                 start=True, stop=False)
                                nc.tensor.matmul(pk[:, :], wkl[:, c * P:(c + 1) * P], sctx[:, b, :],
                                                 start=False, stop=True).then_inc(kp_done, 1)
                            if real(t, s, 2):
                                bb, h = (s - 2) % 8 // 4, (s - 2) % 4
                                at_least(pe, evk, g - 1)
                                if h == 0:
                                    at_least(pe, gsb_done, j - 1)
                                tp = parity if s > 1 else 1 - parity
                                for i in range(NC):
                                    last = nc.tensor.matmul(pg[C * bb:C * bb + C, h * P:(h + 1) * P],
                                                            ctxT[:, tp, i, C * bb:C * bb + C],
                                                            ekT[:, (s - 2) % 4, i, :],
                                                            start=(i == 0), stop=(i == NC - 1))
                                last.then_inc(g_done, 1)
                            if real(t, s, 3):
                                at_least(pe, p_ready, g - 2)
                                at_least(pe, evk, g if not isinstance(t, int) else min(g, 8 * T))
                                at_least(pe, evq, g - 3)
                                for h in range(HC):
                                    last = nc.tensor.transpose(tr[:, h * P:(h + 1) * P],
                                                               pq_sb[:, (s - 3) % 4, h * P:(h + 1) * P], ident)
                                last.then_inc(tq_done, 1)
                            if real(t, s, 8):
                                at_least(pe, at_done, j - 1)
                                at_least(pe, evq, g - 7)
                                if s == 0:
                                    at_least(pe, ss_copied, t - 2)
                                for h in range(HC):
                                    last = nc.tensor.matmul(po[1 - parity][:, c * P + C * b:c * P + C * b + C],
                                                            pT[:, s, h, :], aT[:, b, h, :],
                                                            start=(h == 0), stop=(h == HC - 1))
                                last.then_inc(o_done, 1)
                            if c == 2 and real(t, s, 6):
                                r = slice(C * (1 - b), C * (1 - b) + C)
                                at_least(pe, gsb_done, j)
                                at_least(pe, at_done, j - 1)
                                at_least(pe, kv_copied, t + 1 + b if not isinstance(t, int) else min(t + 1 + b, T))
                                for h in range(HC):
                                    last = nc.tensor.matmul(pm[:, h * P:(h + 1) * P], g_sb[r, h * P:(h + 1) * P],
                                                            mt[r, 2 * h:2 * h + 2, :], start=True, stop=True)
                                last.then_inc(a_done, 1)
                            if s in (3, 4, 5) and real(t, 0, -8):
                                (prep, prep2, prep3)[s - 3](t + 1, 1 - parity)
                            if s == 1 and real(t, 0, 16):
                                at_least(pe, ot_ready, t - 1)
                                for i in range(NC):
                                    last = nc.tensor.transpose(po[parity][:, i * P:(i + 1) * P],
                                                               oT[:, i * P:(i + 1) * P], ident)
                                last.then_inc(o_turned, 1)
                            if s == 3 and real(t, 0, 16):
                                at_least(pe, sq_ready, t - 1)
                                for i in range(NC):
                                    last = nc.tensor.matmul(po[parity][:, 2 * i:2 * i + 2], sq[:, i * P:(i + 1) * P],
                                                            batch_of, start=True, stop=True)
                                last.then_inc(ssq_done, 1)

                    prep(0, 0)
                    prep2(0, 0)
                    prep3(0, 0)
                    tiles(nc.tensor, tile)

                @block.scalar
                def _(act):
                    act.wait_ge(dma_w, NW)
                    nc.scalar.activation(tanh_g[:, :], gts[:, :], ACT.Tanh).then_inc(s_tanh, 1)
                    act.wait_ge(s_mt, 1)
                    for i in range(2):
                        nc.scalar.activation(mt[:, i:HEADS:2, :], (pk, tr)[i][:, 0:HEADS // 2 * C].rearrange(
                            "p (h c) -> p h c", c=C), ACT.Copy, scale=SCALE).then_inc(s_mtc, 1)

                    def prep(t, parity):
                        act.wait_ge(ct_done, t + 1)
                        if not isinstance(t, int) or t > 0:
                            at_least(act, g_done, 8 * t - 8)
                        nc.scalar.activation(ctxT[:, parity, :, :], pm[:, :].rearrange("p (i c) -> p i c", c=P),
                                             ACT.Copy).then_inc(ct_copied, 1)
                        act.wait_ge(nm1_ready, t + 1)
                        at_least(act, e1t_done, t)
                        nc.scalar.activation(e1[:, :], ct[:, parity, :], ACT.Exp, bias=nm1[:, :],
                                             accum_out=s1[:, 0:1]).then_inc(e1_ready, 1)

                    def prep2(t, parity):
                        act.wait_ge(e1t_done, t + 1)
                        at_least(act, kv_done, t)
                        nc.scalar.activation(e1T[:, :, :], pm[:, :].rearrange("p (i c) -> p i c", c=P),
                                             ACT.Copy).then_inc(e1t_copied, 1)

                    def high(source, parts, b, ready):
                        r = slice(C * b, C * b + C)
                        nc.scalar.activation(parts[r, b, :], source[r, :], ACT.Copy).then_inc(ready, 1)

                    def high_parts(t, parity, b):
                        at_least(act, kp_done, 8 * t + 4 * b - 4)
                        high(ct[:, parity, :], sctx, b, ctx_high)
                        act.wait_ge(y32_ready, t + 1)
                        at_least(act, qp_done, 8 * t + 4 * b - 4)
                        high(y32, sy, b, y_high)

                    def tile(t, parity):
                        for s in range(8):
                            b, c = s // 4, s % 4
                            g, j = 8 * t + s, 2 * t + b
                            if real(t, s, 1):
                                at_least(act, tk_done, g)
                                at_least(act, g_done, g - 4)
                                nc.scalar.activation(ekT[:, (s - 1) % 4, :, :], tr[:, :].rearrange(
                                    "p (i c) -> p i c", c=P), ACT.Copy).then_inc(evk, 1)
                            if c == 2 and real(t, s, 6):
                                r = slice(C * (1 - b), C * (1 - b) + C)
                                at_least(act, g_done, 4 * j)
                                at_least(act, a_done, j - 1)
                                nc.scalar.activation(g_sb[r, :], pg[r, :], ACT.Copy).then_inc(gsb_done, 1)
                            if real(t, s, 0):
                                act.wait_ge(kmax_ready, g + 1)
                                at_least(act, tk_done, g - 1)
                                nc.scalar.activation(ek[:, s % 2, :], pk[:, :], ACT.Exp, bias=nmax[:, s:s + 1],
                                                     accum_out=sk[:, s:s + 1]).then_inc(ek_ready, 1)
                            if real(t, s, 3):
                                at_least(act, tq_done, g - 2)
                                at_least(act, o_done, g - 10)
                                nc.scalar.activation(pT[:, (s - 3) % 8, :, :], tr[:, :].rearrange(
                                    "p (h c) -> p h c", c=P), ACT.Copy).then_inc(evq, 1)
                            if real(t, s, 0):
                                act.wait_ge(qsub_done, g + 1)
                                at_least(act, p_ready, g - 3)
                                nc.scalar.activation(eq[:, s % 4, :], qs[:, s % 2, :], ACT.Exp).then_inc(eq_ready, 1)
                            if real(t, 0, 16):
                                if s == 0:
                                    at_least(act, o_done, 8 * t - 8)
                                    nc.scalar.activation(oT[:, :], po[parity][:, :], ACT.Copy).then_inc(ot_ready, 1)
                                if s == 2:
                                    at_least(act, o_turned, t - 1)
                                    nc.scalar.activation(at(o_all, t - 2), po[parity][:, :], ACT.Identity,
                                                         bias=bo_sb[:, :]).then_inc(o_stored, 1)
                                    at_least(act, ssq_done, t - 2)
                                    nc.scalar.activation(sq[:, :], po[parity][:, :], ACT.Square,
                                                         bias=bo_sb[:, :]).then_inc(sq_ready, 1)
                            if s == 0 and real(t, 0, 0):
                                high_parts(t, parity, 1)
                            if s == 3 and real(t, 0, -8):
                                prep(t + 1, 1 - parity)
                            if s == 4 and real(t, 0, -8):
                                high_parts(t + 1, 1 - parity, 0)
                                prep2(t + 1, 1 - parity)

                    prep(0, 0)
                    high_parts(0, 0, 0)
                    prep2(0, 0)
                    tiles(nc.scalar, tile)

                @block.gpsimd
                def _(pool):
                    def tile(t, parity):
                        for s in range(8):
                            g = 8 * t + s
                            if real(t, s, 1):
                                e = eq[:, (s - 1) % 4, :].rearrange("p (h d) -> p h d", d=D)
                                at_least(pool, eq_ready, g)
                                at_least(pool, quarters_ready, g - 1)
                                nc.gpsimd.tensor_tensor(halves[:, :, :], e[:, :, 0:D // 2], e[:, :, D // 2:D],
                                                        ALU.add).then_inc(half_summed, 1)
                                at_least(pool, half_summed, g)
                                at_least(pool, rq_ready, g - 2)
                                nc.gpsimd.tensor_tensor(quarters[:, (s - 1) % 2, :, :], halves[:, :, 0:D // 4],
                                                        halves[:, :, D // 4:D // 2], ALU.add).then_inc(quarters_ready, 1)
                            if real(t, s, 2):
                                k = (s - 2) % 4
                                at_least(pool, rq_ready, g - 1)
                                at_least(pool, tq_done, g - 5)
                                nc.gpsimd.tensor_tensor(pq_sb[:, k, :].rearrange("p (h d) -> p h d", d=D),
                                                        eq[:, k, :].rearrange("p (h d) -> p h d", d=D),
                                                        rq[:, k, :].unsqueeze(2).broadcast_to([P, HEADS, D]),
                                                        ALU.mult).then_inc(p_ready, 1)

                    tiles(nc.gpsimd, tile)

                @block.vector
                def _(dve):
                    dve.wait_ge(dma_w, NW)
                    for w, hi, lo in ((wk32, wkh, wkl), (wq32, wqh, wql)):
                        own.link(nc.vector.tensor_copy(hi[:, :], w[:, :]))
                        own.mark(nc.vector.tensor_tensor(lo[:, :], w[:, :], hi[:, :].bitcast(f32), ALU.subtract))
                    own.link(nc.vector.tensor_copy(gwh[:, :, :], gw_sb[:, :, :]))
                    own.mark(nc.vector.tensor_tensor(gwl[:, :, :], gw_sb[:, :, :], gwh[:, :, :].bitcast(f32), ALU.subtract))
                    dve.wait_ge(s_tanh, 1)
                    own.link(nc.vector.tensor_scalar(gain0[:, :], rg_sb[:, :], tanh_g[:, 0:1], float(C) ** 0.5,
                                                     ALU.mult, ALU.mult))
                    def tile_stats(t):
                        dve.wait_ge(dma_x[t // 4], 16)
                        own.link(nc.vector.bn_stats(stats[:, 0, :], x_all[:, t, :]))
                        own.link(nc.vector.bn_aggr(mv[:, t, :], stats[:, 0, :]))

                    for t in range(4):
                        tile_stats(t)
                    ln_rstd(own, 0, 4)

                    def low(source, parts, b, ready):
                        r, q = slice(C * b, C * b + C), slice(C * (1 - b), C * (1 - b) + C)
                        nc.vector.tensor_tensor(parts[q, b, :], source[r, :], parts[r, b, :].bitcast(f32),
                                                ALU.subtract).then_inc(ready, 1)

                    def low_ctx(t, parity, b):
                        dve.wait_ge(ctx_high, 2 * t + b + 1)
                        low(ct[:, parity, :], sctx, b, sctx_ready)

                    def low_y(t, b):
                        dve.wait_ge(y_high, 2 * t + b + 1)
                        low(y32, sy, b, sy_ready)

                    def prep(t, parity):
                        dve.wait_ge(ctx_loaded[parity], 16 * (t // 2 + 1) if isinstance(t, int) else 8 * (t - parity) + 16)
                        at_least(dve, e1_ready, t)
                        nc.vector.tensor_reduce(nm1[:, :], ct[:, parity, :], AX, ALU.max, negate=True).then_inc(nm1_ready, 1)
                        at_least(dve, sy_ready, 2 * t)
                        nc.vector.tensor_scalar(y32[:, :], at(x_all, t), at(mv, t, slice(0, 1)), at(rstd, t),
                                                ALU.subtract, ALU.mult).then_inc(y32_ready, 1)

                    def prep_kv(t):
                        dve.wait_ge(kv_done, t + 1)
                        dve.wait_ge(e1_ready, t + 1)
                        own.link(nc.vector.reciprocal(s1[:, 1:2], s1[:, 0:1]))
                        nc.vector.scalar_tensor_tensor(out=at(kv1_all, t), in0=pm[:, 0:P], scalar=s1[:, 1:2], in1=kv_mask,
                                                       op0=ALU.mult, op1=ALU.mult).then_inc(kv_copied, 1)

                    def tile(t, parity):
                        for s in range(8):
                            b, c = s // 4, s % 4
                            g, j = 8 * t + s, 2 * t + b
                            k = (s - 1) % 4
                            if real(t, s, 0):
                                dve.wait_ge(kp_done, g + 1)
                                nc.vector.tensor_reduce(nmax[:, s:s + 1], pk[:, :], AX, ALU.max,
                                                        negate=True).then_inc(kmax_ready, 1)
                                dve.wait_ge(qp_done, g + 1)
                                logits = pq[s % 2][:, :].rearrange("p (h d) -> p h d", d=D)
                                maxima = own.mark(nc.vector.tensor_reduce(mx[:, s % 2, :], logits, AX, ALU.max))
                            if c == 3 and real(t, s, 7):
                                at_least(dve, a_done, j)
                                at_least(dve, ek_ready, 4 * j)
                                own.link(nc.vector.reciprocal(rsk[:, :], sk[:, 4 * (1 - b):4 * (1 - b) + 4]))
                                at_least(dve, o_done, 4 * j - 8)
                                for half in range(2):
                                    r = slice(C * half, C * half + C)
                                    last = nc.vector.tensor_tensor(
                                        aT[r, 1 - b, :, :],
                                        pm[r, :].rearrange("p (h o) -> p h o", o=P)[:, :, C * half:C * half + C],
                                        rsk[r, :].unsqueeze(2).broadcast_to([C, HC, C]), ALU.mult)
                                    if half == 0:
                                        own.mark(last)
                                last.then_inc(at_done, 1)
                            if real(t, s, 0):
                                own.wait(maxima)
                                at_least(dve, eq_ready, g - 1)
                                nc.vector.tensor_tensor(qs[:, s % 2, :].rearrange("p (h d) -> p h d", d=D), logits,
                                                        mx[:, s % 2, :].unsqueeze(2).broadcast_to([P, HEADS, D]),
                                                        ALU.subtract).then_inc(qsub_done, 1)
                            if real(t, s, 1):
                                at_least(dve, quarters_ready, g)
                                own.link(nc.vector.reduce_sum(sumq[:, k, :], quarters[:, (s - 1) % 2, :, :], axis=AX))
                                at_least(dve, p_ready, g - 4)
                                nc.vector.reciprocal(rq[:, k, :], sumq[:, k, :]).then_inc(rq_ready, 1)
                            if real(t, 0, 0):
                                if s == 1:
                                    low_ctx(t, parity, 1)
                                if s == 2:
                                    low_y(t, 1)
                            if real(t, 0, -8):
                                if s == 3:
                                    prep(t + 1, 1 - parity)
                                if s == 5:
                                    low_ctx(t + 1, 1 - parity, 0)
                                    prep_kv(t + 1)
                                if s == 6:
                                    low_y(t + 1, 0)
                            if s == 4 and real(t, 0, 16):
                                at_least(dve, ssq_done, t - 1)
                                nc.vector.tensor_copy(at(ss, t - 2), po[parity][:, 0:2 * NC]).then_inc(ss_copied, 1)
                            if isinstance(t, int) and t == 0 and s < 6:
                                tile_stats(4 + 2 * s)
                                tile_stats(5 + 2 * s)
                            if isinstance(t, int) and t == 0 and s == 6:
                                ln_rstd(own, 4, T)

                    prep(0, 0)
                    low_ctx(0, 0, 0)
                    low_y(0, 0)
                    prep_kv(0)
                    tiles(nc.vector, tile, own, 42)

        def at_least(engine, semaphore, value):
            if not isinstance(value, int) or value > 0:
                engine.wait_ge(semaphore, value)

        def turns(engine, n, body, own=None, per_turn=0):
            body(0)
            with engine.Fori(1, n) as u:
                if own:
                    own.loop(u - 1, per_turn)
                body(u)
            if own:
                own.done(n - 1)

        def row_stats(own, t, place):
            nc.vector.sem_inc(waits_over)
            own.link(nc.vector.bn_stats(stats[:, place, :], at(x_all, t)))
            nc.vector.sem_inc(waits_over)
            own.link(nc.vector.bn_aggr(moments[:, place, :], stats[:, place, :]))
            own.mark(nc.vector.tensor_scalar(at(mv, t), moments[:, place, :], 1.0, None, ALU.mult))

        r_all = O.enter_context(nc.sbuf_tensor("r_all", [P, T, 2 * NC], f32))
        rt = O.enter_context(nc.sbuf_tensor("rt", [P, 2, 2 * NC, C], f32))
        scaled = O.enter_context(nc.sbuf_tensor("scaled", [P, 2, N], f32))
        norm_ready = sem("norm_ready")
        rt_ready = sem("rt_ready")
        spread = sem("spread")
        x_normed = sem("x_normed")
        with nc.Block() as block:
            @block.scalar
            def _(act):
                act.wait_ge(norm_ready, 1)

                def step(t, parity, reuse):
                    if reuse:
                        act.wait_ge(spread, t - 1)
                    nc.scalar.activation(rt[:, parity, :, :],
                                         r_all[:, t if isinstance(t, int) else bass.ds(t, 1), :].rearrange(
                                             "p a k -> p (a k)" if not isinstance(t, int) else "p k -> p k")
                                         .unsqueeze(2).broadcast_to([P, 2 * NC, C]), ACT.Copy).then_inc(rt_ready, 1)

                step(0, 0, False)
                step(1, 1, False)
                with nc.scalar.Fori(0, (T - 2) // 2) as u:
                    step(2 * u + 2, 0, True)
                    step(2 * u + 3, 1, True)

            @block.tensor
            def _(pe):
                def step(t, parity, reuse):
                    pe.wait_ge(rt_ready, t + 1)
                    if reuse:
                        pe.wait_ge(x_normed, t - 1)
                    for i in range(NC):
                        last = nc.tensor.matmul(psum[parity][:, i * P:(i + 1) * P],
                                                rt[:, parity, 2 * i:2 * i + 2, :].rearrange("p b c -> p (b c)"),
                                                ident, start=True, stop=True)
                    last.then_inc(spread, 1)

                step(0, 0, False)
                step(1, 1, False)
                with nc.tensor.Fori(0, (T - 2) // 2) as u:
                    step(2 * u + 2, 0, True)
                    step(2 * u + 3, 1, True)

            @block.vector
            def _(dve):
                flat, rflat = ss[:, :, :].rearrange("p t k -> p (t k)"), r_all[:, :, :].rearrange("p t k -> p (t k)")
                own.link(nc.vector.tensor_scalar(flat, flat, 1e-24, None, ALU.max))
                rsqrt(own, flat, rflat, ln_tmp[:, 0, :], ln_tmp[:, 1, :])
                nc.vector.tensor_copy(ln_tmp[:, 0, 0:1], rflat[:, 0:1]).then_inc(norm_ready, 1)
                def pair(u):
                    for parity in range(2):
                        t = 2 * u + parity
                        dve.wait_ge(spread, t + 1)
                        nc.vector.tensor_tensor(scaled[:, parity, :], at(o_all, t), psum[parity][:, :],
                                                ALU.mult).then_inc(x_normed, 1)
                        dve.wait_ge(x_normed, t + 1)
                        own.link(nc.vector.scalar_tensor_tensor(out=at(x_all, t), in0=scaled[:, parity, :],
                                                                scalar=gain0[:, :], in1=at(x_all, t),
                                                                op0=ALU.mult, op1=ALU.add))
                        row_stats(own, t, parity)

                turns(nc.vector, T // 2, pair, own, 8)
                own.wait()
                ln_rstd(own)
        O.close()

        GROUP = 4

        def staggered(stages):
            for k in range(GROUP + max(lag for _, lag in stages)):
                for stage, lag in stages:
                    if 0 <= k - lag < GROUP:
                        stage(k - lag)

        H = ExitStack()
        zz = H.enter_context(nc.sbuf_tensor("zz", [P, T, S * S], f32))
        pp = H.enter_context(nc.sbuf_tensor("pp", [P, T, 2, S], f32))

        with ExitStack() as R:
            y4 = R.enter_context(nc.sbuf_tensor("y4", [P, GROUP, N], f32))
            yT = R.enter_context(nc.sbuf_tensor("yT", [P, GROUP, NC, P], f32))
            y_ready, y_turned, yT_ready, lg_done, lg_copied = (
                sem(n) for n in ("y_ready", "y_turned", "yT_ready", "lg_done", "lg_copied"))
            with nc.Block() as block:
                @block.vector
                def _(dve):
                    def group(u):
                        at_least(dve, y_turned, GROUP * u)
                        for i in range(GROUP):
                            t = GROUP * u + i
                            nc.vector.tensor_scalar(y4[:, i, :], at(x_all, t), at(mv, t, slice(0, 1)), at(rstd, t),
                                                    ALU.subtract, ALU.mult).then_inc(y_ready, 1)
                    turns(nc.vector, T // GROUP, group)
                    ms, v = ln_tmp[:, 0, 0:T], ln_tmp[:, 0, T:2 * T]
                    own.link(nc.vector.tensor_tensor(ms, rstd[:, :], rstd[:, :], ALU.mult))
                    own.link(nc.vector.tensor_tensor(ms, ms, mv[:, :, 1], ALU.mult))
                    own.link(nc.vector.tensor_scalar(v, ms, RMS_EPS, None, ALU.add))
                    rsqrt(own, v, ms, ln_tmp[:, 1, 0:T], ln_tmp[:, 1, T:2 * T])
                    at_least(dve, lg_copied, T)
                    own.link(nc.vector.tensor_tensor(lg[:, :, :], lg[:, :, :],
                                                     ms.unsqueeze(2).broadcast_to([P, T, 24]), ALU.mult))
                    own.link(nc.vector.tensor_tensor(lg[:, :, :], lg[:, :, :],
                                                     b24_sb[:, :].unsqueeze(1).broadcast_to([P, T, 24]), ALU.add))

                @block.tensor
                def _(pe):
                    def group(u):
                        def turn(i):
                            at_least(pe, y_ready, GROUP * u + i + 1)
                            if i == 0:
                                at_least(pe, yT_ready, GROUP * u)
                            for c in range(NC):
                                last = nc.tensor.transpose(psum[i][:, c * P:(c + 1) * P], y4[:, i, c * P:(c + 1) * P], ident)
                            last.then_inc(y_turned, 1)

                        def logits(i):
                            at_least(pe, yT_ready, GROUP * u + i + 1)
                            if i == 0:
                                at_least(pe, lg_copied, GROUP * u)
                            for c in range(NC):
                                last = nc.tensor.matmul(psum[4 + i][:, 0:24], yT[:, i, c, :], w24_sb[:, c, :],
                                                        start=(c == 0), stop=(c == NC - 1))
                            last.then_inc(lg_done, 1)

                        staggered(((turn, 0), (logits, 1)))

                    turns(nc.tensor, T // GROUP, group)

                @block.scalar
                def _(act):
                    def group(u):
                        def copy(i):
                            at_least(act, y_turned, GROUP * u + i + 1)
                            if i == 0:
                                at_least(act, lg_done, GROUP * u)
                            nc.scalar.activation(yT[:, i, :, :].rearrange("p c n -> p (c n)"), psum[i][:, :],
                                                 ACT.Copy).then_inc(yT_ready, 1)

                        def logits(i):
                            at_least(act, lg_done, GROUP * u + i + 1)
                            nc.scalar.activation(at(lg, GROUP * u + i), psum[4 + i][:, 0:24],
                                                 ACT.Copy).then_inc(lg_copied, 1)

                        staggered(((copy, 0), (logits, 2)))

                    turns(nc.scalar, T // GROUP, group)


        with ExitStack() as R:
            def rb(name, shape):
                return R.enter_context(nc.sbuf_tensor(name, shape, f32))

            kern, work = rb("kern", [P, T, S * S]), rb("work", [P, T, S * S])
            mxs, sums, ra, cb, logs = (rb(n, [P, T * S]) for n in ("mxs", "sums", "ra", "cb", "logs"))
            csum = rb("csum", [P, T * S])
            to_act, from_act = sem("to_act"), sem("from_act")
            calls = Count(nc.vector, from_act)

            def by_row(z):
                return z[:, :, :].rearrange("p t (i j) -> p (t i) j", j=S)

            def by_column(z):
                return z[:, :, :].rearrange("p t (i j) -> p t j i", j=S)

            def over_j(v):
                return v[:, :].unsqueeze(2).broadcast_to([P, T * S, S])

            def grid(z):
                return z[:, :, :].rearrange("p t (i j) -> p t i j", j=S)

            def over_i(v):
                return v[:, :].rearrange("p (t j) -> p t j", j=S).unsqueeze(2).broadcast_to([P, T, S, S])

            def flat(z):
                return z[:, :, :].rearrange("p t k -> p (t k)")

            pf = pp[:, :, :, :].rearrange("p t a k -> p (t a) k")
            with nc.Block() as block:
                @block.scalar
                def _(act):
                    n = [0]

                    def answer(out_, in_, func, index=None, **kw):
                        n[0] += 1
                        at_least(act, to_act, n[0] if index is None else 3 * index + n[0])
                        nc.scalar.activation(out_, in_, func, **kw).then_inc(from_act, 1)

                    answer(flat(work), flat(work), ACT.Exp)
                    answer(logs[:, :], sums[:, :], ACT.Ln)
                    answer(flat(work), flat(work), ACT.Exp)
                    answer(logs[:, :], sums[:, :], ACT.Ln)
                    answer(flat(kern), flat(zz), ACT.Exp)
                    with nc.scalar.Fori(0, REFRESHES) as k:
                        answer(mxs[:, :], sums[:, :], ACT.Ln, k)
                        answer(logs[:, :], csum[:, :], ACT.Ln, k)
                        answer(flat(kern), flat(zz), ACT.Exp, k)
                    n[0] += 3 * (REFRESHES - 1)
                    answer(pp[:, :, :, :].rearrange("p t a k -> p (t a k)"),
                           pp[:, :, :, :].rearrange("p t a k -> p (t a k)"), ACT.Exp)
                    answer(sgt[:, 0:1], sg_sb[:, :], ACT.Exp, scale=-1.0)

                @block.vector
                def _(dve):
                    V = nc.vector

                    def ask(instruction, wait=True):
                        instruction.then_inc(to_act, 1)
                        calls.value += 1
                        if wait:
                            calls.wait()

                    own.link(V.tensor_scalar(zz[:, :, :], lg[:, :, 0:S * S], 1.0 / TAU, None, ALU.mult))
                    own.link(V.tensor_reduce(mxs[:, :], by_row(zz), AX, ALU.max))
                    own.link(V.tensor_tensor(by_row(zz), by_row(zz), over_j(mxs), ALU.subtract))
                    ask(V.tensor_copy(flat(work), flat(zz)))
                    ask(V.reduce_sum(sums[:, :], by_row(work), axis=AX))
                    own.link(V.tensor_tensor(by_row(zz), by_row(zz), over_j(logs), ALU.subtract))
                    own.link(V.tensor_reduce(mxs[:, :].rearrange("p (t j) -> p t j", j=S), by_column(zz), AX, ALU.max))
                    own.link(V.tensor_tensor(grid(zz), grid(zz), over_i(mxs), ALU.subtract))
                    ask(V.tensor_copy(flat(work), flat(zz)))
                    ask(V.reduce_sum(sums[:, :].rearrange("p (t j) -> p t j", j=S), by_column(work), axis=AX))
                    ask(V.tensor_tensor(grid(zz), grid(zz), over_i(logs), ALU.subtract))
                    def scale_columns(out_):
                        own.link(V.tensor_tensor(grid(out_), grid(work if out_ is kern else kern), over_i(cb), ALU.mult))

                    def steps(count):
                        for n in range(count):
                            if n:
                                own.link(V.reciprocal(cb[:, :], csum[:, :]))
                                scale_columns(work)
                            own.link(V.reduce_sum(sums[:, :], by_row(work if n else kern), axis=AX))
                            own.link(V.reciprocal(ra[:, :], sums[:, :]))
                            own.link(V.tensor_tensor(by_row(work), by_row(kern), over_j(ra), ALU.mult))
                            own.link(V.reduce_sum(csum[:, :].rearrange("p (t j) -> p t j", j=S), by_column(work), axis=AX))

                    with V.Fori(0, REFRESHES) as k:
                        own.loop(k, 6 * BLOCK - 1)
                        calls.loop(k, 3)
                        steps(BLOCK)
                        ask(V.tensor_copy(cb[:, 0:1], csum[:, 0:1]), wait=False)
                        ask(V.tensor_copy(ra[:, 0:1], sums[:, 0:1]))
                        own.link(V.tensor_tensor(by_row(zz), by_row(zz), over_j(mxs), ALU.subtract))
                        ask(V.tensor_tensor(grid(zz), grid(zz), over_i(logs), ALU.subtract))
                        own.done(REFRESHES)
                        calls.done(REFRESHES)
                    steps(LAST)
                    own.link(V.reciprocal(cb[:, :], csum[:, :]))
                    scale_columns(kern)
                    pm_ = mxs[:, 0:2 * T]
                    own.link(V.tensor_copy(pf, lg[:, :, S * S:24].rearrange("p t (a k) -> p t a k", k=S)))
                    own.link(V.tensor_reduce(pm_, pf, AX, ALU.max))
                    ask(V.tensor_tensor(pf, pf, pm_.unsqueeze(2).broadcast_to([P, 2 * T, S]), ALU.subtract))
                    own.link(V.reduce_sum(pm_, pf, axis=AX))
                    own.link(V.reciprocal(sums[:, 0:2 * T], pm_))
                    own.link(V.tensor_tensor(pf, pf, sums[:, 0:2 * T].unsqueeze(2).broadcast_to([P, 2 * T, S]), ALU.mult))
                    ask(V.tensor_copy(logs[:, 0:1], pm_[:, 0:1]))
                    own.link(V.tensor_scalar(sgt[:, 1:2], sgt[:, 0:1], 1.0, None, ALU.add))
                    own.link(V.reciprocal(sgt[:, 2:3], sgt[:, 1:2]))
                    own.link(V.tensor_tensor(sgt[:, 3:4], sgt[:, 0:1], sgt[:, 2:3], ALU.mult))
                    own.link(V.tensor_scalar(zz[:, :, :], kern[:, :, :], sgt[:, 2:3], None, ALU.mult))
                    own.link(V.tensor_scalar(zz[:, :, 0:S * S:S + 1], zz[:, :, 0:S * S:S + 1], sgt[:, 3:4], None, ALU.add))
                    own.link(V.tensor_scalar(zz[:, :, :], zz[:, :, :], tanh_g[:, 2:3], None, ALU.mult))
                    own.link(V.tensor_scalar(pp[:, :, 1, :], pp[:, :, 1, :], tanh_g[:, 2:3], None, ALU.mult))

        with ExitStack() as R:
            y2 = R.enter_context(nc.sbuf_tensor("y2", [P, 2, N], f32))
            pre = R.enter_context(nc.sbuf_tensor("pre", [P, 2, S, P], f32))
            mixer = R.enter_context(nc.sbuf_tensor("mixer", [P, 2, S * S, P], f32))
            xpT = R.enter_context(nc.sbuf_tensor("xpT", [P, 2, P], f32))
            names = ("c1_y", "pre_ready", "mixer_pool", "mixer_act", "xp_done", "xpT_ready", "mix_done", "yb_done", "mixed")
            y_rdy, pre_ready, mixer_pool, mixer_act, xp_done, xpT_ready, mix_done, yb_done, mixed = (sem(n) for n in names)
            SHARE = 8

            with nc.Block() as block:
                @block.tensor
                def _(pe):
                    def pair(u):
                        for i in range(2):
                            t = 2 * u + i
                            at_least(pe, y_rdy, t + 1)
                            at_least(pe, pre_ready, t + 1)
                            for j in range(S):
                                last = nc.tensor.matmul(psum[i][:, 0:P], y2[:, i, j * P:(j + 1) * P], pre[:, i, j, :],
                                                        start=(j == 0), stop=(j == S - 1))
                            last.then_inc(xp_done, 1)
                            at_least(pe, mixer_pool, t + 1)
                            at_least(pe, mixer_act, t + 1)
                            at_least(pe, mixed, t - 1)
                            for k in range(S):
                                for j in range(S):
                                    last = nc.tensor.matmul(psum[4 + i][:, k * P:(k + 1) * P], mixer[:, i, S * k + j, :],
                                                            y2[:, i, j * P:(j + 1) * P], start=(j == 0), stop=(j == S - 1))
                            last.then_inc(mix_done, 1)
                            at_least(pe, xpT_ready, t + 1)
                            nc.tensor.matmul(psum[2 + i][:, 0:P], xpT[:, i, :], wb_sb[:, :],
                                             start=True, stop=True).then_inc(yb_done, 1)

                    turns(nc.tensor, T // 2, pair)

                @block.gpsimd
                def _(pool):
                    def diagonals(out_, weights, count):
                        return nc.gpsimd.tensor_tensor(
                            out_, ident.unsqueeze(1).broadcast_to([P, count, P]),
                            weights.unsqueeze(2).broadcast_to([P, count, P]), ALU.mult)

                    def pair(u):
                        for i in range(2):
                            t = 2 * u + i
                            at_least(pool, mix_done, t - 1)
                            nc.gpsimd.sem_inc(pool_passed)
                            if isinstance(t, int):
                                first, rest = pp[:, t, 0, :], zz[:, t, 0:SHARE]
                            else:
                                first = pp[:, bass.ds(t, 1), 0, :].rearrange("p a k -> p (a k)")
                                rest = zz[:, bass.ds(t, 1), 0:SHARE].rearrange("p a k -> p (a k)")
                            diagonals(pre[:, i, :, :], first, S).then_inc(pre_ready, 1)
                            diagonals(mixer[:, i, 0:SHARE, :], rest, SHARE).then_inc(mixer_pool, 1)

                    turns(nc.gpsimd, T // 2, pair)

                @block.scalar
                def _(act):
                    def pair(u):
                        for i in range(2):
                            t = 2 * u + i
                            at_least(act, mix_done, t - 1)
                            for k in range(SHARE, S * S):
                                last = nc.scalar.activation(mixer[:, i, k, :], ident, ACT.Copy,
                                                            scale=at(zz, t, slice(k, k + 1)))
                            last.then_inc(mixer_act, 1)
                            at_least(act, xp_done, t + 1)
                            nc.scalar.activation(xpT[:, i, :], psum[i][:, 0:P], ACT.Copy).then_inc(xpT_ready, 1)

                    turns(nc.scalar, T // 2, pair)

                @block.vector
                def _(dve):
                    V = nc.vector

                    def norm(t, i):
                        V.tensor_scalar(y2[:, i, :], at(x_all, t), at(mv, t, slice(0, 1)), at(rstd, t),
                                        ALU.subtract, ALU.mult).then_inc(y_rdy, 1)

                    def update(t, i):
                        dve.wait_ge(mix_done, t + 1)
                        own.link(V.tensor_tensor(at(x_all, t), at(x_all, t), psum[4 + i][:, :], ALU.add))
                        dve.wait_ge(yb_done, t + 1)
                        for k in range(S):
                            stream = at(x_all, t, slice(k * P, (k + 1) * P))
                            last = V.scalar_tensor_tensor(out=stream, in0=psum[2 + i][:, 0:P],
                                                          scalar=at(pp, t, 1, slice(k, k + 1)), in1=stream,
                                                          op0=ALU.mult, op1=ALU.add)
                            if k < S - 1:
                                own.mark(last)
                            else:
                                last.then_inc(mixed, 1)
                        own.wait()
                        dve.wait_ge(mixed, t + 1)
                        row_stats(own, t, i)

                    norm(0, 0)
                    norm(1, 1)
                    with V.Fori(0, T // 2 - 1) as u:
                        own.loop(u, 2 * (1 + S - 1 + 3))
                        for i in range(2):
                            update(2 * u + i, i)
                            norm(2 * u + 2 + i, i)
                        own.done(T // 2 - 1)
                    update(T - 2, 0)
                    update(T - 1, 1)
                    own.wait()
                    ln_rstd(own)
        H.close()

        with ExitStack() as R:
            def rc(name, shape):
                return R.enter_context(nc.sbuf_tensor(name, shape, f32))

            NG = N // DH1
            y4, q4, e4, p4, qT = (rc(n, [P, GROUP, N]) for n in ("y4c", "q4", "e4", "p4", "qT"))
            mx4, su4, rc4 = (rc(n, [P, GROUP, NG]) for n in ("mx4", "su4", "rc4"))
            kvf = rc("kvf", [P, GROUP, P])
            names = ("c2_y", "c2_yT", "c2_sub", "c2_exp", "c2_rcp", "c2_p", "c2_pT", "c2_qT", "c2_o", "c2_kv", "c2_x")
            y_rdy, y_trn, sub_rdy, exp_rdy, rcp_rdy, p_rdy, p_trn, qT_rdy, o_rdy, kvf_rdy, x_rdy = (sem(n) for n in names)

            def grouped(z):
                return z.rearrange("p (g d) -> p g d", d=DH1)

            def spread_g(v):
                return v.unsqueeze(2).broadcast_to([P, NG, DH1])

            with nc.Block() as block:
                @block.tensor
                def _(pe):
                    def group(u):
                        b = GROUP * u

                        def turn(i):
                            at_least(pe, y_rdy, b + i + 1)
                            at_least(pe, sub_rdy, b + max(i - 1, 0))
                            for c in range(NC):
                                last = nc.tensor.transpose(psum[i % 2][:, c * P:(c + 1) * P],
                                                           y4[:, i, c * P:(c + 1) * P], ident)
                            last.then_inc(y_trn, 1)

                        def back(i):
                            at_least(pe, p_rdy, b + i + 1)
                            at_least(pe, qT_rdy, b + max(i - 1, 0))
                            for c in range(NC):
                                last = nc.tensor.transpose(psum[2 + i % 2][:, c * P:(c + 1) * P],
                                                           p4[:, i, c * P:(c + 1) * P], ident)
                            last.then_inc(p_trn, 1)

                        def product(i):
                            at_least(pe, qT_rdy, b + i + 1)
                            at_least(pe, kvf_rdy, b + i + 1)
                            at_least(pe, x_rdy, b + max(i - 1, 0))
                            nc.tensor.matmul(psum[4 + i % 2][:, :], kvf[:, i, :], qT[:, i, :],
                                             start=True, stop=True).then_inc(o_rdy, 1)

                        staggered(((turn, 0), (back, 2), (product, 3)))

                    turns(nc.tensor, T // GROUP, group)

                @block.scalar
                def _(act):
                    def group(u):
                        b = GROUP * u

                        def exps(i):
                            at_least(act, sub_rdy, b + i + 1)
                            if i == 0:
                                at_least(act, p_rdy, b)
                            nc.scalar.activation(e4[:, i, :], q4[:, i, :], ACT.Exp).then_inc(exp_rdy, 1)

                        def copy(i):
                            at_least(act, p_trn, b + i + 1)
                            if i == 0:
                                at_least(act, o_rdy, b)
                            nc.scalar.activation(qT[:, i, :], psum[2 + i % 2][:, :], ACT.Copy).then_inc(qT_rdy, 1)

                        staggered(((exps, 0), (copy, 2)))

                    turns(nc.scalar, T // GROUP, group)

                @block.gpsimd
                def _(pool):
                    def group(u):
                        b = GROUP * u

                        def probs(i):
                            if i == 0:
                                at_least(pool, o_rdy, b)
                            nc.gpsimd.sem_inc(pool_passed)
                            nc.gpsimd.tensor_copy(kvf[:, i, :], at(kv1_all, b + i)).then_inc(kvf_rdy, 1)
                            at_least(pool, rcp_rdy, b + i + 1)
                            if i == 0:
                                at_least(pool, p_trn, b)
                            nc.gpsimd.tensor_tensor(grouped(p4[:, i, :]), grouped(e4[:, i, :]), spread_g(rc4[:, i, :]),
                                                    ALU.mult).then_inc(p_rdy, 1)

                        staggered(((probs, 0),))

                    turns(nc.gpsimd, T // GROUP, group)

                @block.vector
                def _(dve):
                    V = nc.vector
                    def group(u):
                        b = GROUP * u

                        def norm(i):
                            if i == 0:
                                at_least(dve, y_trn, b)
                            V.tensor_scalar(y4[:, i, :], at(x_all, b + i), at(mv, b + i, slice(0, 1)), at(rstd, b + i),
                                            ALU.subtract, ALU.mult).then_inc(y_rdy, 1)

                        def shift(i):
                            at_least(dve, y_trn, b + i + 1)
                            own.link(V.tensor_reduce(mx4[:, i, :], grouped(psum[i % 2][:, :]), AX, ALU.max))
                            if i == 0:
                                at_least(dve, exp_rdy, b)
                            V.tensor_tensor(grouped(q4[:, i, :]), grouped(psum[i % 2][:, :]), spread_g(mx4[:, i, :]),
                                            ALU.subtract).then_inc(sub_rdy, 1)

                        def sums_(i):
                            at_least(dve, exp_rdy, b + i + 1)
                            own.link(V.reduce_sum(su4[:, i, :], grouped(e4[:, i, :]), axis=AX))
                            if i == 0:
                                at_least(dve, p_rdy, b)
                            V.reciprocal(rc4[:, i, :], su4[:, i, :]).then_inc(rcp_rdy, 1)

                        def update(i):
                            at_least(dve, o_rdy, b + i + 1)
                            V.scalar_tensor_tensor(out=at(x_all, b + i), in0=psum[4 + i % 2][:, :],
                                                   scalar=tanh_g[:, 1:2], in1=at(x_all, b + i),
                                                   op0=ALU.mult, op1=ALU.add).then_inc(x_rdy, 1)
                            at_least(dve, x_rdy, b + i + 1)
                            row_stats(own, b + i, i % 2)

                        staggered(((norm, 0), (shift, 1), (sums_, 2), (update, 4)))

                    turns(nc.vector, T // GROUP, group, own, 5 * GROUP)
                    own.wait()
                    ln_rstd(own)

        xh = sb("xh", [P, NC, ROWS], f32r)
        xl = sb("xl", [P, NC, ROWS], f32r)
        NEVER = 3.0e38
        GU, DN = 2 * NC * IC * P, IC * N
        w32 = sb("w32", [P, GU + DN])
        wh, wl = [sb("wh0", [P, GU + DN], f32r)], [sb("wl0", [P, GU + DN], f32r)]
        w_loaded, w_high, w_split = sem("w_loaded"), sem("w_high"), sem("w_split")

        def load_weights(sp, row):
            sp.dma_start(w32[:, 0:GU], wgu[row, :]).then_inc(w_loaded, 16)
            sp.dma_start(w32[:, GU:GU + DN], wd[row, :]).then_inc(w_loaded, 16)

        def split_weights(pool, n, parity):
            nc.gpsimd.tensor_copy(wh[parity][:, :], w32[:, :]).then_inc(w_high, 1)
            pool.wait_ge(w_high, n + 1)
            nc.gpsimd.tensor_tensor(wl[parity][:, :], w32[:, :], wh[parity][:, :].bitcast(f32),
                                    ALU.subtract).then_inc(w_split, 1)

        with ExitStack() as R:
            def rd(name, shape):
                return R.enter_context(nc.sbuf_tensor(name, shape, f32))

            y4 = rd("y4d", [P, GROUP, N])
            s16 = rd("s16", [E, 512])
            sc = rd("sc", [P, T, E])
            padded = rd("padded", [P, T, E + TOPK])
            top = rd("top", [P, T, 8])
            left = rd("left", [P, T, E + TOPK])
            tot = rd("tot", [P, 2, T])
            names = ("c3_y", "c3_yT", "c3_hi", "c3_lo", "c3_gate", "c3_gatec", "c3_score", "c3_scorec", "c3_sub", "c3_exp")
            y_rdy, y_trn, hi_rdy, lo_rdy, gate_rdy, gate_cp, sco_rdy, sco_cp, exp_ask, exp_ans = (sem(n) for n in names)
            with nc.Block() as block:
                @block.sync
                def _(sp):
                    load_weights(sp, slice(0, P))
                    sp.wait_ge(w_split, 1)
                    load_weights(sp, slice(P, 2 * P))

                @block.gpsimd
                def _(pool):
                    pool.wait_ge(w_loaded, 32)
                    nc.gpsimd.sem_inc(pool_passed)
                    split_weights(pool, 0, 0)

                @block.vector
                def _(dve):
                    V = nc.vector
                    def group(u):
                        b = GROUP * u

                        def norm(i):
                            if i == 0:
                                at_least(dve, y_trn, b)
                            V.tensor_scalar(y4[:, i, :], at(x_all, b + i), at(mv, b + i, slice(0, 1)), at(rstd, b + i),
                                            ALU.subtract, ALU.mult).then_inc(y_rdy, 1)

                        def low(i):
                            at_least(dve, hi_rdy, b + i + 1)
                            cols = bass.ds((b + i) * P, P)
                            V.tensor_tensor(xl[:, :, cols], psum[i][:, :].rearrange("p (c n) -> p c n", n=P),
                                            xh[:, :, cols].bitcast(f32), ALU.subtract).then_inc(lo_rdy, 1)

                        staggered(((norm, 0), (low, 1)))
                        at_least(dve, sco_rdy, u + 1)
                        V.tensor_copy(sc[:, bass.ds(b, GROUP), :],
                                      psum[5][:, 0:GROUP * E].rearrange("p (t e) -> p t e", e=E)).then_inc(sco_cp, 1)

                    turns(nc.vector, T // GROUP, group)
                    at_least(dve, sco_cp, T // GROUP)
                    flat_sc = sc[:, :, :].rearrange("p t e -> p (t e)")
                    V.tensor_copy(tot[:, 0, 0:1], flat_sc[:, 0:1]).then_inc(exp_ask, 1)
                    at_least(dve, exp_ans, 1)
                    own.link(V.tensor_scalar(flat_sc, flat_sc, 1.0, None, ALU.add))
                    own.link(V.reciprocal(flat_sc, flat_sc))
                    own.link(V.tensor_tensor(sc[:, :, :], sc[:, :, :],
                                             bias_sb[:, :].unsqueeze(1).broadcast_to([P, T, E]), ALU.add))
                    own.mark(V.memset(padded[:, :, E:E + TOPK], NEVER))
                    own.mark(V.memset(cw[:, :, :], 1.0))
                    own.link(V.tensor_copy(padded[:, :, 0:E], sc[:, :, :]))
                    for t in range(T):
                        own.mark(V.max(out=top[:, t, :], in_=padded[:, t, 0:E]))
                    own.wait()
                    own.link(V.memset(top[:, :, TOPK:8], NEVER))
                    for t in range(T):
                        own.mark(V.match_replace(out=left[:, t, :], in_to_replace=top[:, t, :], in_values=padded[:, t, :],
                                                 imm_value=-NEVER))
                    own.wait()
                    own.link(V.tensor_scalar(left[:, :, 0:E], left[:, :, 0:E], -1.0e38, None, ALU.is_lt))
                    own.link(V.tensor_tensor(left[:, :, 0:E], left[:, :, 0:E], sc[:, :, :], ALU.mult))
                    own.link(V.reduce_sum(tot[:, 0, :], left[:, :, 0:E], axis=AX))
                    own.link(V.tensor_scalar(tot[:, 0, :], tot[:, 0, :], 1e-20, None, ALU.add))
                    own.link(V.reciprocal(tot[:, 1, :], tot[:, 0, :]))
                    own.link(V.tensor_tensor(cw[:, 1:E + 1, :], left[:, :, 0:E].rearrange("p t e -> p e t"),
                                             tot[:, 1, :].unsqueeze(1).broadcast_to([P, E, T]), ALU.mult))
                    own.link(V.tensor_scalar(cw[:, :, :], cw[:, :, :], tanh_g[:, 3:4], None, ALU.mult))

                @block.scalar
                def _(act):
                    def group(u):
                        b = GROUP * u
                        for i in range(GROUP):
                            at_least(act, y_trn, b + i + 1)
                            nc.scalar.activation(xh[:, :, bass.ds((b + i) * P, P)],
                                                 psum[i][:, :].rearrange("p (c n) -> p c n", n=P),
                                                 ACT.Copy).then_inc(hi_rdy, 1)
                        at_least(act, gate_rdy, u + 1)
                        nc.scalar.activation(s16[:, :], psum[4][0:E, :], ACT.Copy).then_inc(gate_cp, 1)

                    turns(nc.scalar, T // GROUP, group)
                    at_least(act, exp_ask, 1)
                    flat_sc = sc[:, :, :].rearrange("p t e -> p (t e)")
                    nc.scalar.activation(flat_sc, flat_sc, ACT.Exp, scale=-1.0).then_inc(exp_ans, 1)

                @block.tensor
                def _(pe):
                    def group(u):
                        b = GROUP * u
                        for i in range(GROUP):
                            at_least(pe, y_rdy, b + i + 1)
                            if i == 0:
                                at_least(pe, lo_rdy, b)
                            for c in range(NC):
                                last = nc.tensor.transpose(psum[i][:, c * P:(c + 1) * P], y4[:, i, c * P:(c + 1) * P], ident)
                            last.then_inc(y_trn, 1)
                        at_least(pe, lo_rdy, b + GROUP)
                        at_least(pe, gate_cp, u)
                        for c in range(NC):
                            for k, (w, v) in enumerate(((gwh, xh), (gwl, xh), (gwh, xl), (gwl, xl))):
                                last = nc.tensor.matmul(psum[4][0:E, :], w[:, c, :], v[:, c, bass.ds(u * 512, 512)],
                                                        start=(c == 0 and k == 0), stop=(c == NC - 1 and k == 3))
                        last.then_inc(gate_rdy, 1)
                        at_least(pe, gate_cp, u + 1)
                        at_least(pe, sco_cp, u)
                        nc.tensor.sem_inc(pe_passed)
                        for i in range(GROUP):
                            last = nc.tensor.transpose(psum[5][:, i * E:(i + 1) * E], s16[:, i * P:(i + 1) * P],
                                                       ident[0:E, 0:E])
                        last.then_inc(sco_rdy, 1)

                    turns(nc.tensor, T // GROUP, group)


        with ExitStack() as R:
            wh.append(R.enter_context(nc.sbuf_tensor("wh1", [P, GU + DN], f32r)))
            wl.append(R.enter_context(nc.sbuf_tensor("wl1", [P, GU + DN], f32r)))
            sg2 = R.enter_context(nc.sbuf_tensor("sg2", [P, IC, 512], f32))
            z32 = R.enter_context(nc.sbuf_tensor("z32", [P, IC, 512], f32))
            zh = R.enter_context(nc.sbuf_tensor("zh", [P, 2, IC, 512], f32r))
            zl = R.enter_context(nc.sbuf_tensor("zl", [P, 2, IC, 512], f32r))
            names = ("gu_done", "silu_done", "z_mult", "z_ready", "down_done", "acc_done")
            gu_done, silu_done, z_mult, z_ready, down_done, acc_done = (sem(n) for n in names)

            def all_experts(engine, expert, count=None, per_turn=0):
                expert(0, 0, False)
                with engine.Fori(0, E // 2) as u:
                    if count:
                        count.loop(u, 2 * per_turn)
                    expert(2 * u + 1, 1, True)
                    expert(2 * u + 2, 0, True)
                if count:
                    count.done(E // 2)

            with nc.Block() as block:
                @block.sync
                def _(sp):
                    with sp.Fori(2, E + 1) as n:
                        row = sp.snap(n * P)
                        sp.wait_ge(w_split, sp.snap(n + 0))
                        sp.sem_inc(sp_passed)
                        load_weights(sp, bass.ds(row, P))
                    for tb in range(TB):
                        sp.wait_ge(acc_done, 4 * (TB * E + tb + 1))
                        sp.dma_start(out[512 * tb:512 * tb + 512, :].rearrange("(t p) n -> p t n", p=P),
                                     x_all[:, 4 * tb:4 * tb + 4, :]).then_inc(out_stored, 16)
                    sp.wait_ge(out_stored, 16 * TB)

                @block.gpsimd
                def _(pool):
                    def split(n, parity):
                        pool.wait_ge(w_loaded, 32 * n + 32)
                        at_least(pool, down_done, 4 * TB * (n - 1))
                        nc.gpsimd.sem_inc(pool_passed)
                        split_weights(pool, n, parity)

                    split(1, 1)
                    split(2, 0)
                    with nc.gpsimd.Fori(1, E // 2) as u:
                        split(2 * u + 1, 1)
                        split(2 * u + 2, 0)

                @block.tensor
                def _(pe):
                    def gate_up(n, parity, tb, ic):
                        hi, lo = wh[parity], wl[parity]
                        k = TB * n + tb
                        at_least(pe, z_ready, 2 * k - 1 + ic)
                        if tb == 0 and ic == 0:
                            pe.wait_ge(w_split, n + 1)
                        for m in range(2):
                            for c in range(NC):
                                first = ((m * NC) + c) * IC * P + ic * P
                                cols = slice(512 * tb, 512 * tb + 512)
                                for q, (w, v) in enumerate(((hi, xh), (lo, xh), (hi, xl))):
                                    last = nc.tensor.matmul(psum[2 * ic + m][:, :], w[:, first:first + P], v[:, c, cols],
                                                            start=(c == 0 and q == 0), stop=(c == NC - 1 and q == 2))
                        last.then_inc(gu_done, 1)

                    def down(n, parity, tb):
                        hi, lo = wh[parity], wl[parity]
                        k = TB * n + tb
                        pe.wait_ge(z_ready, 2 * k + 2)
                        at_least(pe, acc_done, 4 * k)
                        for tt in range(4):
                            for ic in range(IC):
                                first = GU + ic * N
                                cols = slice(tt * P, tt * P + P)
                                for q, (z, w) in enumerate(((zh, hi), (zh, lo), (zl, hi))):
                                    last = nc.tensor.matmul(psum[4 + tt][:, :], z[:, tb % 2, ic, cols],
                                                            w[:, first:first + N], start=(ic == 0 and q == 0),
                                                            stop=(ic == IC - 1 and q == 2))
                            last.then_inc(down_done, 1)

                    def expert(n, parity, carry):
                        for tb in range(TB):
                            gate_up(n, parity, tb, 0)
                            gate_up(n, parity, tb, 1)
                            if tb:
                                down(n, parity, tb - 1)
                            elif carry:
                                down(n - 1, 1 - parity, TB - 1)

                    all_experts(nc.tensor, expert)
                    down(E, 0, TB - 1)

                @block.scalar
                def _(act):
                    def expert(n, parity, carry):
                        for tb in range(TB):
                            for ic in range(IC):
                                k = TB * n + tb
                                act.wait_ge(gu_done, 2 * k + ic + 1)
                                at_least(act, z_mult, 2 * k + ic - 1)
                                nc.scalar.activation(sg2[:, ic, :], psum[2 * ic][:, :], ACT.Silu).then_inc(silu_done, 1)

                    all_experts(nc.scalar, expert)

                @block.vector
                def _(dve):
                    V = nc.vector

                    def hidden(n, tb, ic):
                        k = TB * n + tb
                        dve.wait_ge(silu_done, 2 * k + ic + 1)
                        V.tensor_tensor(z32[:, ic, :], sg2[:, ic, :], psum[2 * ic + 1][:, :],
                                        ALU.mult).then_inc(z_mult, 1)
                        dve.wait_ge(z_mult, 2 * k + ic + 1)
                        at_least(dve, down_done, 4 * (k - 1))
                        own.link(V.tensor_copy(zh[:, tb % 2, ic, :], z32[:, ic, :]))
                        V.tensor_tensor(zl[:, tb % 2, ic, :], z32[:, ic, :], zh[:, tb % 2, ic, :].bitcast(f32),
                                        ALU.subtract).then_inc(z_ready, 1)

                    def add(n, tb):
                        for tt in range(4):
                            t = 4 * tb + tt
                            dve.wait_ge(down_done, 4 * (TB * n + tb) + tt + 1)
                            V.scalar_tensor_tensor(out=x_all[:, t, :], in0=psum[4 + tt][:, :],
                                                   scalar=at(cw, n, slice(t, t + 1)), in1=x_all[:, t, :],
                                                   op0=ALU.mult, op1=ALU.add).then_inc(acc_done, 1)

                    def expert(n, parity, carry):
                        for tb in range(TB):
                            hidden(n, tb, 0)
                            hidden(n, tb, 1)
                            if tb:
                                add(n, tb - 1)
                            elif carry:
                                add(n - 1, TB - 1)

                    all_experts(nc.vector, expert, own, IC * TB)
                    add(E, TB - 1)


def kernel(x, ctx_4096, g_xattn, g_ffn, L0_xattn_Wq, L0_xattn_Wk, L0_xattn_Wv, L0_xattn_Wo, L0_xattn_bo, L0_xattn_g,
           L0_ffn_W_res, L0_ffn_W_pre, L0_ffn_W_post, L0_ffn_H_res_base, L0_ffn_H_pre_base, L0_ffn_H_post_base,
           L0_ffn_gate, L0_ffn_W_branch, L1_ffn_gate_w, L1_ffn_bias, L1_ffn_Wg, L1_ffn_Wu, L1_ffn_Wd,
           L1_ffn_Sg, L1_ffn_Su, L1_ffn_Sd):
    import numpy as np
    import concourse.bacc as bacc
    from concourse.bass_utils import run_bass_kernel_spmd

    def a(v):
        return np.asarray(v)

    def rows(v, n=128):
        return np.broadcast_to(a(v).reshape(1, -1), (n, a(v).size))

    def twice(v):
        return np.concatenate([a(v), a(v)], axis=0)

    B, C, N = x.shape
    H = L1_ffn_Sg.shape[1]
    I = L1_ffn_Sg.shape[0]
    E = L1_ffn_Wg.shape[0]
    P = 128

    def by_partition(w):
        k, m = w.shape
        return w.reshape(k // P, P, m).transpose(1, 0, 2).reshape(P, -1)

    gates_up = [np.stack([by_partition(a(g).T), by_partition(a(u).T)], axis=1)
                for g, u in [(L1_ffn_Sg, L1_ffn_Su)] + list(zip(a(L1_ffn_Wg), a(L1_ffn_Wu)))]
    downs = [by_partition(a(d).T) for d in [L1_ffn_Sd] + list(a(L1_ffn_Wd))]
    consts = np.zeros((P, 2 * P + 2), np.float32)
    consts[:, :P] = np.eye(P)
    consts[:, P:2 * P] = np.kron(np.eye(P // 8), np.ones((8, 8)))
    consts[:, 2 * P:] = np.kron(np.eye(2), np.ones((P // 2, 1)))
    arrays = {
        "x": a(x).reshape(B * C, N),
        "ctx_kv": a(ctx_4096).reshape(B * C, N),
        "wq": twice(a(L0_xattn_Wq).T),
        "wk": twice(a(L0_xattn_Wk).T),
        "wv": a(L0_xattn_Wv),
        "wo": a(L0_xattn_Wo).T,
        "bo": twice(a(L0_xattn_bo).reshape(C, 1)),
        "rms_gain": twice(a(L0_xattn_g).reshape(C, 1)),
        "gates": rows(np.concatenate([a(g_xattn), a(g_ffn)])),
        "w24": np.concatenate([a(L0_ffn_W_res), a(L0_ffn_W_pre), a(L0_ffn_W_post)], axis=0).T,
        "base24": rows(np.concatenate([a(L0_ffn_H_res_base).reshape(-1), a(L0_ffn_H_pre_base), a(L0_ffn_H_post_base)])),
        "sig_gate": rows(L0_ffn_gate),
        "w_branch": a(L0_ffn_W_branch),
        "gate_w": a(L1_ffn_gate_w).T,
        "bias": rows(L1_ffn_bias),
        "wgu": np.stack(gates_up).reshape((E + 1) * P, -1),
        "wd": np.stack(downs).reshape((E + 1) * P, -1),
        "consts": consts,
    }
    arrays = {f"in_{k}": np.ascontiguousarray(v) for k, v in arrays.items()}
    nc = bacc.Bacc("TRN2", target_bir_lowering=False, num_devices=1)
    args = [nc.dram_tensor(k, v.shape, mybir.dt.from_np(v.dtype), kind="ExternalInput").ap() for k, v in arrays.items()]
    out = nc.dram_tensor("out", (B * C, N), mybir.dt.float32, kind="ExternalOutput").ap()
    flamingo_program(nc, *args, out)
    r = run_bass_kernel_spmd(nc, [arrays], core_ids=[0])
    return r.results[0]["out"].reshape(B, C, N)
```

```python
from contextlib import ExitStack

import concourse.bass as bass
from concourse import mybir


class Count:

    def __init__(self, engine, semaphore):
        self.engine, self.semaphore = engine, semaphore
        self.value, self.index, self.per_turn = 0, 0, 0

    def loop(self, index, per_turn):
        self.index, self.per_turn, self.first = index, per_turn, self.value

    def done(self, turns):
        assert self.value == self.first + self.per_turn, (self.value - self.first, self.per_turn)
        self.value = self.first + turns * self.per_turn
        self.index, self.per_turn = 0, 0

    def mark(self, instruction):
        instruction.then_inc(self.semaphore, 1)
        self.value += 1
        return self.value

    def wait(self, mark=None):
        value = self.value if mark is None else mark
        self.engine.wait_ge(self.semaphore, self.index * self.per_turn + value if self.per_turn else value)

    def link(self, instruction):
        self.mark(instruction)
        self.wait()


def flamingo_program(nc, x, ctx_kv, wq, wk, wv, wo, bo, rms_gain, gates, w24, base24, sig_gate, w_branch,
                     gate_w, bias, wgu, wd, consts, out):
    f32, f32r, i32 = mybir.dt.float32, mybir.dt.float32r, mybir.dt.int32
    ALU, ACT, AX = mybir.AluOpType, mybir.ActivationFunctionType, mybir.AxisListType.X

    ROWS, N = x.shape
    P = 128
    T = ROWS // P
    C = 64
    HD = wq.shape[1]
    HC = HD // P
    NC = N // P
    HEADS = 8
    D = HD // HEADS
    SCALE = D ** -0.5
    DH1 = 8
    S = 4
    TAU = 0.1
    ITERS = 50
    BLOCK = 16
    REFRESHES = 2
    LAST = ITERS - 1 - REFRESHES * BLOCK
    RMS_EPS = 1.1920929e-07
    LN_EPS = 1e-5
    E = gate_w.shape[1]
    IC = 2
    TB = 4
    TOPK = 4

    ctx = ExitStack()
    with ctx:
        def sb(name, shape, dt=f32):
            return ctx.enter_context(nc.sbuf_tensor(name, shape, dt))

        def sem(name):
            return ctx.enter_context(nc.semaphore(name))

        x_all = sb("x_all", [P, T, N])
        kv1_all = sb("kv1_all", [P, T, P])
        mv = sb("mv", [P, T, 2])
        rstd = sb("rstd", [P, T])
        ln_tmp = sb("ln_tmp", [P, 2, P])
        stats = sb("stats", [P, 2, 6])
        moments = sb("moments", [P, 2, 2])
        cst = sb("cst", [P, 2 * P + 2])
        ident, kv_mask, batch_of = cst[:, 0:P], cst[:, P:2 * P], cst[:, 2 * P:2 * P + 2]
        gts = sb("gts", [P, 4])
        tanh_g = sb("tanh_g", [P, 4])
        bo_sb = sb("bo_sb", [P, 1])
        rg_sb = sb("rg_sb", [P, 1])
        gain0 = sb("gain0", [P, 1])
        w24_sb = sb("w24_sb", [P, NC, 24])
        b24_sb = sb("b24_sb", [P, 24])
        sg_sb = sb("sg_sb", [P, 1])
        sgt = sb("sgt", [P, 4])
        wb_sb = sb("wb_sb", [P, P])
        gw_sb = sb("gw_sb", [P, NC, E])
        gwh = sb("gwh", [P, NC, E], f32r)
        gwl = sb("gwl", [P, NC, E], f32r)
        bias_sb = sb("bias_sb", [P, E])
        lg = sb("lg", [P, T, 24])
        cw = sb("cw", [P, E + 1, T])

        psum = [ctx.enter_context(nc.psum_tensor(f"bank{i}", [P, 512], f32)) for i in range(8)]
        pk, pq, tr, pg, po, pm = psum[0], psum[1:3], psum[3], psum[4], psum[5:7], psum[7]

        dma_w = sem("dma_w")
        dma_late = sem("dma_late")
        dma_wk = sem("dma_wk")
        dma_x = [sem(f"dma_x{i}") for i in range(4)]
        X_TILES = (0, 2, 6, 11, T)
        ctx_loaded = [sem(f"ctx_loaded{i}") for i in range(2)]
        dve_own = sem("dve_own")
        o_stored = sem("o_stored")
        tanh_ready = sem("tanh_ready")
        mt_done = sem("mt_done")
        mt_copied = sem("mt_copied")
        sctx_ready = sem("sctx_ready")
        sy_ready = sem("sy_ready")
        kp_done = sem("kp_done")
        kmax_ready = sem("kmax_ready")
        ek_ready = sem("ek_ready")
        ek_turned = sem("ek_turned")
        ekT_ready = sem("ekT_ready")
        qp_done = sem("qp_done")
        qsub_done = sem("qsub_done")
        eq_ready = sem("eq_ready")
        rq_ready = sem("rq_ready")
        p_ready = sem("p_ready")
        p_turned = sem("p_turned")
        pT_ready = sem("pT_ready")
        ctx_high = sem("ctx_high")
        y_high = sem("y_high")
        y32_ready = sem("y32_ready")
        g_done = sem("g_done")
        gsb_done = sem("gsb_done")
        aT_done = sem("aT_done")
        aT_ready = sem("aT_ready")
        o_done = sem("o_done")
        ot_ready = sem("ot_ready")
        o_turned = sem("o_turned")
        half_summed = sem("half_summed")
        quarters_ready = sem("quarters_ready")
        sq_ready = sem("sq_ready")
        ssq_done = sem("ssq_done")
        ss_copied = sem("ss_copied")
        nm1_ready = sem("nm1_ready")
        e1_ready = sem("e1_ready")
        ct_done = sem("ct_done")
        ct_copied = sem("ct_copied")
        e1t_done = sem("e1t_done")
        e1t_copied = sem("e1t_copied")
        kv_done = sem("kv_done")
        kv_copied = sem("kv_copied")
        out_stored = sem("out_stored")
        sp_passed = sem("sp_passed")
        waits_over = sem("waits_over")
        pool_passed = sem("pool_passed")
        pe_passed = sem("pe_passed")

        def at(tensor, t, *rest):
            alone = isinstance(t, int) and len(tensor.shape) > 2
            return tensor[(slice(None), t if alone else bass.ds(t, 1), *rest)]

        def at_least(engine, semaphore, value):
            if not isinstance(value, int) or value > 0:
                engine.wait_ge(semaphore, value)

        def rsqrt(own, v, y, a, b):
            own.link(nc.vector.tensor_scalar(y.bitcast(i32), v.bitcast(i32), 1, None, ALU.logical_shift_right))
            own.link(nc.vector.tensor_scalar(y.bitcast(i32), y.bitcast(i32), -1.0, 1597463007.0, ALU.mult, ALU.add))
            for _ in range(3):
                own.link(nc.vector.tensor_tensor(a, y, y, ALU.mult))
                own.link(nc.vector.scalar_tensor_tensor(out=b, in0=a, scalar=-0.5, in1=v, op0=ALU.mult, op1=ALU.mult))
                own.link(nc.vector.scalar_tensor_tensor(out=y, in0=b, scalar=1.5, in1=y, op0=ALU.add, op1=ALU.mult))

        def ln_rstd(own, t0=0, t1=T):
            v, p, q = ln_tmp[:, 0, t0:t1], ln_tmp[:, 1, t0:t1], ln_tmp[:, 1, T + t0:T + t1]
            own.link(nc.vector.tensor_scalar(v, mv[:, t0:t1, 1], LN_EPS, None, ALU.add))
            rsqrt(own, v, rstd[:, t0:t1], p, q)

        O = ExitStack()
        o_all = O.enter_context(nc.sbuf_tensor("o_all", [P, T, N], f32))
        ss = O.enter_context(nc.sbuf_tensor("ss", [P, T, 2 * NC], f32))
        own = Count(nc.vector, dve_own)
        A = ExitStack()
        with A:
            def sa(name, shape, dt=f32):
                return A.enter_context(nc.sbuf_tensor(name, shape, dt))

            ct = sa("ct", [P, 2, N])
            wq32 = sa("wq32", [P, HD])
            wk32 = sa("wk32", [P, HD])
            wqh, wql = sa("wqh", [P, HD], f32r), sa("wql", [P, HD], f32r)
            wkh, wkl = sa("wkh", [P, HD], f32r), sa("wkl", [P, HD], f32r)
            wv_sb = sa("wv_sb", [P, HC, C])
            wo_sb = sa("wo_sb", [P, HC, C])
            mt = sa("mt", [P, HEADS, C])
            y32 = sa("y32", [P, N])
            sctx = sa("sctx", [P, 2, N], f32r)
            sy = sa("sy", [P, 2, N], f32r)
            ctxT = sa("ctxT", [P, 2, NC, P])
            e1 = sa("e1", [P, N])
            e1T = sa("e1T", [P, NC, P])
            nm1 = sa("nm1", [P, 1])
            s1 = sa("s1", [P, 2])
            nmax = sa("nmax", [P, 8])
            sk = sa("sk", [P, 8])
            rsk = sa("rsk", [P, 4])
            ek = sa("ek", [P, 2, N])
            ekT = sa("ekT", [P, 4, NC, P])
            mx = sa("mx", [P, 2, HEADS])
            qs = sa("qs", [P, 2, HD])
            eq = sa("eq", [P, 4, HD])
            sumq = sa("sumq", [P, 4, HEADS])
            rq = sa("rq", [P, 4, HEADS])
            pq_sb = sa("pq_sb", [P, 4, HD])
            pT = sa("pT", [P, 8, HC, P])
            g_sb = sa("g_sb", [P, HD])
            aT = sa("aT", [P, 2, HC, C])
            sq = sa("sq", [P, N])
            oT = sa("oT", [P, N])
            halves = sa("halves", [P, HEADS, D // 2])
            quarters = sa("quarters", [P, 2, HEADS, D // 4])

            def tiles(engine, tile, own=None, per_pair=0):
                tile(0, 0)
                tile(1, 1)
                with engine.Fori(1, T // 2 - 1) as u:
                    if own:
                        own.loop(u - 1, per_pair)
                    tile(2 * u, 0)
                    tile(2 * u + 1, 1)
                if own:
                    own.done(T // 2 - 2)
                for t in range(T - 2, T + 2):
                    tile(t, t % 2)

            def real(t, s, behind):
                return not isinstance(t, int) or 0 <= 8 * t + s - behind < 8 * T

            with nc.Block() as block:

                @block.sync
                def _(sp):
                    def chunked(w):
                        return w.rearrange("(c p) n -> p c n", p=P)

                    sp.dma_start(ct[:, 0, :], ctx_kv[0:P, :]).then_inc(ctx_loaded[0], 16)
                    load_x = [x[P * a:P * b, :].rearrange("(t p) n -> p t n", p=P) for a, b in zip(X_TILES, X_TILES[1:])]
                    sp.dma_start(x_all[:, 0:X_TILES[1], :], load_x[0]).then_inc(dma_x[0], 16)
                    for dst, src in ((wk32, wk), (wq32, wq)):
                        sp.dma_start(dst[:, :], src).then_inc(dma_wk, 16)
                    for dst, src in ((cst, consts), (wv_sb, wv), (wo_sb, wo)):
                        sp.dma_start(dst[(slice(None),) * len(dst.shape)], src if dst is cst else chunked(src)).then_inc(dma_w, 16)
                    for dst, src in ((gts, gates), (bo_sb, bo), (rg_sb, rms_gain)):
                        sp.dma_start(dst[:, :], src).then_inc(dma_w, 16)
                    sp.dma_start(ct[:, 1, :], ctx_kv[P:2 * P, :]).then_inc(ctx_loaded[1], 16)
                    for i in range(1, 4):
                        sp.dma_start(x_all[:, X_TILES[i]:X_TILES[i + 1], :], load_x[i]).then_inc(dma_x[i], 16)
                    for dst, src in ((b24_sb, base24), (sg_sb, sig_gate), (wb_sb, w_branch), (bias_sb, bias)):
                        sp.dma_start(dst[:, :], src).then_inc(dma_late, 16)
                    for dst, src in ((w24_sb, w24), (gw_sb, gate_w)):
                        sp.dma_start(dst[:, :, :], chunked(src)).then_inc(dma_late, 16)

                    def refill(t, parity):
                        split_of, read, row = sp.snap(2 * t + 2), sp.snap(t + 1), sp.snap((t + 2) * P)
                        for semaphore, value in ((sctx_ready, split_of), (ct_done, read), (e1_ready, read)):
                            sp.wait_ge(semaphore, value)
                            sp.sem_inc(sp_passed)
                        sp.dma_start(ct[:, parity, :], ctx_kv[bass.ds(row, P), :]).then_inc(ctx_loaded[parity], 16)

                    with sp.Fori(0, (T - 2) // 2) as u:
                        refill(2 * u, 0)
                        refill(2 * u + 1, 1)

                NW = 6 * 16

                @block.tensor
                def _(pe):
                    pe.wait_ge(dma_w, NW)
                    def prep(t, parity):
                        pe.wait_ge(ctx_loaded[parity], 16 * (t // 2 + 1) if isinstance(t, int) else 8 * (t - parity) + 16)
                        at_least(pe, aT_ready, 2 * t - 1 + (0 if isinstance(t, int) and t == 0 else -1))
                        at_least(pe, kv_copied, t)
                        for i in range(NC):
                            last = nc.tensor.transpose(pm[:, i * P:(i + 1) * P], ct[:, parity, i * P:(i + 1) * P], ident)
                        last.then_inc(ct_done, 1)

                    def prep2(t, parity):
                        pe.wait_ge(ct_copied, t + 1)
                        pe.wait_ge(e1_ready, t + 1)
                        for i in range(NC):
                            last = nc.tensor.transpose(pm[:, i * P:(i + 1) * P], e1[:, i * P:(i + 1) * P], ident)
                        last.then_inc(e1t_done, 1)

                    def prep3(t, parity):
                        pe.wait_ge(e1t_copied, t + 1)
                        for i in range(NC):
                            last = nc.tensor.matmul(pm[:, 0:P], e1T[:, i, :], ctxT[:, parity, i, :],
                                                    start=(i == 0), stop=(i == NC - 1))
                        last.then_inc(kv_done, 1)

                    def tile(t, parity):
                        for s in range(8):
                            b, c = s // 4, s % 4
                            g, j = 8 * t + s, 2 * t + b
                            if real(t, s, 0):
                                pe.wait_ge(sy_ready, j + 1)
                                at_least(pe, qsub_done, g - 1)
                                nc.tensor.matmul(pq[s % 2][:, :], sy[:, b, c * P:(c + 1) * P], wqh[:, :],
                                                 start=True, stop=False)
                                nc.tensor.matmul(pq[s % 2][:, :], sy[:, b, c * P:(c + 1) * P], wql[:, :],
                                                 start=False, stop=True).then_inc(qp_done, 1)
                            if real(t, s, 1):
                                at_least(pe, ek_ready, g)
                                at_least(pe, pT_ready, g - 3)
                                for i in range(NC):
                                    last = nc.tensor.transpose(tr[:, i * P:(i + 1) * P],
                                                               ek[:, (s - 1) % 2, i * P:(i + 1) * P], ident)
                                last.then_inc(ek_turned, 1)
                            if real(t, s, 0):
                                pe.wait_ge(sctx_ready, j + 1)
                                at_least(pe, ek_ready, g)
                                nc.tensor.matmul(pk[:, :], wkh[:, c * P:(c + 1) * P], sctx[:, b, :],
                                                 start=True, stop=False)
                                nc.tensor.matmul(pk[:, :], wkl[:, c * P:(c + 1) * P], sctx[:, b, :],
                                                 start=False, stop=True).then_inc(kp_done, 1)
                            if real(t, s, 8):
                                at_least(pe, aT_ready, j - 1)
                                at_least(pe, pT_ready, g - 7)
                                if s == 0:
                                    at_least(pe, ss_copied, t - 2)
                                for h in range(HC):
                                    last = nc.tensor.matmul(po[1 - parity][:, c * P + C * b:c * P + C * b + C],
                                                            pT[:, s, h, :], aT[:, b, h, :],
                                                            start=(h == 0), stop=(h == HC - 1))
                                last.then_inc(o_done, 1)
                            if real(t, s, 3):
                                at_least(pe, p_ready, g - 2)
                                at_least(pe, ekT_ready, g if not isinstance(t, int) else min(g, 8 * T))
                                at_least(pe, pT_ready, g - 3)
                                for h in range(HC):
                                    last = nc.tensor.transpose(tr[:, h * P:(h + 1) * P],
                                                               pq_sb[:, (s - 3) % 4, h * P:(h + 1) * P], ident)
                                last.then_inc(p_turned, 1)
                            if real(t, s, 2):
                                bb, h = (s - 2) % 8 // 4, (s - 2) % 4
                                at_least(pe, ekT_ready, g - 1)
                                if h == 0:
                                    at_least(pe, gsb_done, j - 1)
                                tp = parity if s > 1 else 1 - parity
                                for i in range(NC):
                                    last = nc.tensor.matmul(pg[C * bb:C * bb + C, h * P:(h + 1) * P],
                                                            ctxT[:, tp, i, C * bb:C * bb + C],
                                                            ekT[:, (s - 2) % 4, i, :],
                                                            start=(i == 0), stop=(i == NC - 1))
                                last.then_inc(g_done, 1)
                            if c == 2 and real(t, s, 6):
                                r = slice(C * (1 - b), C * (1 - b) + C)
                                at_least(pe, gsb_done, j)
                                at_least(pe, aT_ready, j - 1)
                                at_least(pe, kv_copied, t + 1 + b if not isinstance(t, int) else min(t + 1 + b, T))
                                for h in range(HC):
                                    last = nc.tensor.matmul(pm[:, h * P:(h + 1) * P], g_sb[r, h * P:(h + 1) * P],
                                                            mt[r, 2 * h:2 * h + 2, :], start=True, stop=True)
                                last.then_inc(aT_done, 1)
                            if s in (3, 4, 5) and real(t, 0, -8):
                                (prep, prep2, prep3)[s - 3](t + 1, 1 - parity)
                            if s == 1 and real(t, 0, 16):
                                at_least(pe, ot_ready, t - 1)
                                for i in range(NC):
                                    last = nc.tensor.transpose(po[parity][:, i * P:(i + 1) * P],
                                                               oT[:, i * P:(i + 1) * P], ident)
                                last.then_inc(o_turned, 1)
                            if s == 6 and real(t, 0, 16):
                                at_least(pe, sq_ready, t - 1)
                                at_least(pe, o_stored, t - 1)
                                for i in range(NC):
                                    last = nc.tensor.matmul(po[parity][:, 2 * i:2 * i + 2], sq[:, i * P:(i + 1) * P],
                                                            batch_of, start=True, stop=True)
                                last.then_inc(ssq_done, 1)

                    prep(0, 0)
                    for half in range(2):
                        for h in range(HEADS):
                            r = D * (h % 2)
                            last = nc.tensor.matmul((pk, tr)[h % 2][C * half:C * half + C, C * (h // 2):C * (h // 2) + C],
                                                    wv_sb[r:r + D, h // 2, :], wo_sb[r:r + D, h // 2, :],
                                                    start=True, stop=True)
                    last.then_inc(mt_done, 1)
                    prep2(0, 0)
                    prep3(0, 0)
                    pe.wait_ge(mt_copied, 2)
                    tiles(nc.tensor, tile)

                @block.scalar
                def _(act):
                    act.wait_ge(dma_w, NW)
                    nc.scalar.activation(tanh_g[:, :], gts[:, :], ACT.Tanh).then_inc(tanh_ready, 1)

                    def prep(t, parity):
                        act.wait_ge(ct_done, t + 1)
                        if not isinstance(t, int) or t > 0:
                            at_least(act, g_done, 8 * t - 8)
                        nc.scalar.activation(ctxT[:, parity, :, :], pm[:, :].rearrange("p (i c) -> p i c", c=P),
                                             ACT.Copy).then_inc(ct_copied, 1)
                        act.wait_ge(nm1_ready, t + 1)
                        at_least(act, e1t_done, t)
                        nc.scalar.activation(e1[:, :], ct[:, parity, :], ACT.Exp, bias=nm1[:, :],
                                             accum_out=s1[:, 0:1]).then_inc(e1_ready, 1)

                    def prep2(t, parity):
                        act.wait_ge(e1t_done, t + 1)
                        at_least(act, kv_done, t)
                        nc.scalar.activation(e1T[:, :, :], pm[:, :].rearrange("p (i c) -> p i c", c=P),
                                             ACT.Copy).then_inc(e1t_copied, 1)

                    def high(source, parts, b, ready):
                        r = slice(C * b, C * b + C)
                        nc.scalar.activation(parts[r, b, :], source[r, :], ACT.Copy).then_inc(ready, 1)

                    def high_ctx(t, parity, b):
                        at_least(act, kp_done, 8 * t + 4 * b - 4)
                        high(ct[:, parity, :], sctx, b, ctx_high)

                    def high_y(t, b):
                        act.wait_ge(y32_ready, t + 1)
                        at_least(act, qp_done, 8 * t + 4 * b - 4)
                        high(y32, sy, b, y_high)

                    def tile(t, parity):
                        for s in range(8):
                            b, c = s // 4, s % 4
                            g, j = 8 * t + s, 2 * t + b
                            if real(t, s, 1):
                                at_least(act, ek_turned, g)
                                at_least(act, g_done, g - 4)
                                nc.scalar.activation(ekT[:, (s - 1) % 4, :, :], tr[:, :].rearrange(
                                    "p (i c) -> p i c", c=P), ACT.Copy).then_inc(ekT_ready, 1)
                            if c == 2 and real(t, s, 6):
                                r = slice(C * (1 - b), C * (1 - b) + C)
                                at_least(act, g_done, 4 * j)
                                at_least(act, aT_done, j - 1)
                                nc.scalar.activation(g_sb[r, :], pg[r, :], ACT.Copy).then_inc(gsb_done, 1)
                            if real(t, s, 0):
                                act.wait_ge(kmax_ready, g + 1)
                                at_least(act, ek_turned, g - 1)
                                nc.scalar.activation(ek[:, s % 2, :], pk[:, :], ACT.Exp, bias=nmax[:, s:s + 1],
                                                     accum_out=sk[:, s:s + 1]).then_inc(ek_ready, 1)
                            if real(t, s, 3):
                                at_least(act, p_turned, g - 2)
                                at_least(act, o_done, g - 10)
                                nc.scalar.activation(pT[:, (s - 3) % 8, :, :], tr[:, :].rearrange(
                                    "p (h c) -> p h c", c=P), ACT.Copy).then_inc(pT_ready, 1)
                            if real(t, s, 0):
                                act.wait_ge(qsub_done, g + 1)
                                at_least(act, p_ready, g - 3)
                                nc.scalar.activation(eq[:, s % 4, :], qs[:, s % 2, :], ACT.Exp).then_inc(eq_ready, 1)
                            if real(t, 0, 16):
                                if s == 0:
                                    at_least(act, o_done, 8 * t - 8)
                                    nc.scalar.activation(oT[:, :], po[parity][:, :], ACT.Copy).then_inc(ot_ready, 1)
                                if s == 5:
                                    nc.scalar.activation(at(o_all, t - 2), po[parity][:, :], ACT.Identity,
                                                         bias=bo_sb[:, :]).then_inc(o_stored, 1)
                                if s == 2:
                                    at_least(act, o_turned, t - 1)
                                    at_least(act, ssq_done, t - 2)
                                    nc.scalar.activation(sq[:, :], po[parity][:, :], ACT.Square,
                                                         bias=bo_sb[:, :]).then_inc(sq_ready, 1)
                            if s == 0 and real(t, 0, 0):
                                high_ctx(t, parity, 1)
                            if s == 1 and real(t, 0, 0):
                                high_y(t, 1)
                            if s == 3 and real(t, 0, -8):
                                prep(t + 1, 1 - parity)
                            if s == 4 and real(t, 0, -8):
                                high_ctx(t + 1, 1 - parity, 0)
                                prep2(t + 1, 1 - parity)
                            if s == 5 and real(t, 0, -8):
                                high_y(t + 1, 0)

                    prep(0, 0)
                    act.wait_ge(mt_done, 1)
                    for i in range(2):
                        nc.scalar.activation(mt[:, i:HEADS:2, :], (pk, tr)[i][:, 0:HEADS // 2 * C].rearrange(
                            "p (h c) -> p h c", c=C), ACT.Copy, scale=SCALE).then_inc(mt_copied, 1)
                    high_ctx(0, 0, 0)
                    high_y(0, 0)
                    prep2(0, 0)
                    tiles(nc.scalar, tile)

                @block.gpsimd
                def _(pool):
                    def tile(t, parity):
                        for s in range(8):
                            g = 8 * t + s
                            if real(t, s, 1):
                                e = eq[:, (s - 1) % 4, :].rearrange("p (h d) -> p h d", d=D)
                                at_least(pool, eq_ready, g)
                                at_least(pool, quarters_ready, g - 1)
                                nc.gpsimd.tensor_tensor(halves[:, :, :], e[:, :, 0:D // 2], e[:, :, D // 2:D],
                                                        ALU.add).then_inc(half_summed, 1)
                                at_least(pool, half_summed, g)
                                at_least(pool, rq_ready, g - 2)
                                nc.gpsimd.tensor_tensor(quarters[:, (s - 1) % 2, :, :], halves[:, :, 0:D // 4],
                                                        halves[:, :, D // 4:D // 2], ALU.add).then_inc(quarters_ready, 1)
                            if real(t, s, 2):
                                k = (s - 2) % 4
                                at_least(pool, rq_ready, g - 1)
                                at_least(pool, p_turned, g - 5)
                                nc.gpsimd.tensor_tensor(pq_sb[:, k, :].rearrange("p (h d) -> p h d", d=D),
                                                        eq[:, k, :].rearrange("p (h d) -> p h d", d=D),
                                                        rq[:, k, :].unsqueeze(2).broadcast_to([P, HEADS, D]),
                                                        ALU.mult).then_inc(p_ready, 1)

                    tiles(nc.gpsimd, tile)

                @block.vector
                def _(dve):
                    def tile_stats(*tiles):
                        for half in range(0, len(tiles), 2):
                            two = [(i, t) for i, t in enumerate(tiles[half:half + 2])]
                            for i, t in two:
                                dve.wait_ge(dma_x[sum(t >= b for b in X_TILES[1:4])], 16)
                                own.mark(nc.vector.bn_stats(stats[:, i, :], x_all[:, t, :]))
                            own.wait()
                            for i, t in two:
                                own.mark(nc.vector.bn_aggr(mv[:, t, :], stats[:, i, :]))
                        own.wait()

                    tile_stats(0, 1)
                    ln_rstd(own, 0, 2)

                    def low(source, parts, b, ready):
                        r, q = slice(C * b, C * b + C), slice(C * (1 - b), C * (1 - b) + C)
                        nc.vector.tensor_tensor(parts[q, b, :], source[r, :], parts[r, b, :].bitcast(f32),
                                                ALU.subtract).then_inc(ready, 1)

                    def low_ctx(t, parity, b):
                        dve.wait_ge(ctx_high, 2 * t + b + 1)
                        low(ct[:, parity, :], sctx, b, sctx_ready)

                    def low_y(t, b):
                        dve.wait_ge(y_high, 2 * t + b + 1)
                        low(y32, sy, b, sy_ready)

                    def prep(t, parity):
                        dve.wait_ge(ctx_loaded[parity], 16 * (t // 2 + 1) if isinstance(t, int) else 8 * (t - parity) + 16)
                        at_least(dve, e1_ready, t)
                        nc.vector.tensor_reduce(nm1[:, :], ct[:, parity, :], AX, ALU.max, negate=True).then_inc(nm1_ready, 1)
                        at_least(dve, sy_ready, 2 * t)
                        nc.vector.tensor_scalar(y32[:, :], at(x_all, t), at(mv, t, slice(0, 1)), at(rstd, t),
                                                ALU.subtract, ALU.mult).then_inc(y32_ready, 1)

                    def prep_kv(t):
                        dve.wait_ge(kv_done, t + 1)
                        dve.wait_ge(e1_ready, t + 1)
                        own.link(nc.vector.reciprocal(s1[:, 1:2], s1[:, 0:1]))
                        nc.vector.scalar_tensor_tensor(out=at(kv1_all, t), in0=pm[:, 0:P], scalar=s1[:, 1:2], in1=kv_mask,
                                                       op0=ALU.mult, op1=ALU.mult).then_inc(kv_copied, 1)

                    def tile(t, parity):
                        for s in range(8):
                            b, c = s // 4, s % 4
                            g, j = 8 * t + s, 2 * t + b
                            k = (s - 1) % 4
                            if real(t, s, 0):
                                dve.wait_ge(kp_done, g + 1)
                                nc.vector.tensor_reduce(nmax[:, s:s + 1], pk[:, :], AX, ALU.max,
                                                        negate=True).then_inc(kmax_ready, 1)
                                dve.wait_ge(qp_done, g + 1)
                                logits = pq[s % 2][:, :].rearrange("p (h d) -> p h d", d=D)
                                maxima = own.mark(nc.vector.tensor_reduce(mx[:, s % 2, :], logits, AX, ALU.max))
                            if c == 3 and real(t, s, 7):
                                at_least(dve, aT_done, j)
                                at_least(dve, ek_ready, 4 * j)
                                own.link(nc.vector.reciprocal(rsk[:, :], sk[:, 4 * (1 - b):4 * (1 - b) + 4]))
                                at_least(dve, o_done, 4 * j - 8)
                                for half in range(2):
                                    r = slice(C * half, C * half + C)
                                    last = nc.vector.tensor_tensor(
                                        aT[r, 1 - b, :, :],
                                        pm[r, :].rearrange("p (h o) -> p h o", o=P)[:, :, C * half:C * half + C],
                                        rsk[r, :].unsqueeze(2).broadcast_to([C, HC, C]), ALU.mult)
                                    if half == 0:
                                        own.mark(last)
                                last.then_inc(aT_ready, 1)
                            if real(t, s, 0):
                                own.wait(maxima)
                                at_least(dve, eq_ready, g - 1)
                                nc.vector.tensor_tensor(qs[:, s % 2, :].rearrange("p (h d) -> p h d", d=D), logits,
                                                        mx[:, s % 2, :].unsqueeze(2).broadcast_to([P, HEADS, D]),
                                                        ALU.subtract).then_inc(qsub_done, 1)
                            if real(t, s, 1):
                                at_least(dve, quarters_ready, g)
                                own.link(nc.vector.reduce_sum(sumq[:, k, :], quarters[:, (s - 1) % 2, :, :], axis=AX))
                                at_least(dve, p_ready, g - 4)
                                nc.vector.reciprocal(rq[:, k, :], sumq[:, k, :]).then_inc(rq_ready, 1)
                            if real(t, 0, 0):
                                if s == 1:
                                    low_ctx(t, parity, 1)
                                if s == 2:
                                    low_y(t, 1)
                            if real(t, 0, -8):
                                if s == 3:
                                    prep(t + 1, 1 - parity)
                                if s == 5:
                                    low_ctx(t + 1, 1 - parity, 0)
                                    prep_kv(t + 1)
                                if s == 6:
                                    low_y(t + 1, 0)
                            if s == 7 and real(t, 0, 16):
                                at_least(dve, ssq_done, t - 1)
                                nc.vector.tensor_copy(at(ss, t - 2), po[parity][:, 0:2 * NC]).then_inc(ss_copied, 1)
                            if isinstance(t, int) and t == 0:
                                if s < 7:
                                    tile_stats(2 + 2 * s, 3 + 2 * s)
                                else:
                                    ln_rstd(own, 2, T)
                            if isinstance(t, int) and t == 1 and s == 7:
                                dve.wait_ge(dma_late, 6 * 16)
                                own.link(nc.vector.tensor_copy(gwh[:, :, :], gw_sb[:, :, :]))
                                own.mark(nc.vector.tensor_tensor(gwl[:, :, :], gw_sb[:, :, :],
                                                                 gwh[:, :, :].bitcast(f32), ALU.subtract))
                                dve.wait_ge(tanh_ready, 1)
                                own.link(nc.vector.tensor_scalar(gain0[:, :], rg_sb[:, :], tanh_g[:, 0:1], float(C) ** 0.5,
                                                                 ALU.mult, ALU.mult))

                    prep(0, 0)
                    dve.wait_ge(dma_wk, 32)
                    for w, hi, lo in ((wk32, wkh, wkl), (wq32, wqh, wql)):
                        own.link(nc.vector.tensor_copy(hi[:, :], w[:, :]))
                        own.mark(nc.vector.tensor_tensor(lo[:, :], w[:, :], hi[:, :].bitcast(f32), ALU.subtract))
                    low_ctx(0, 0, 0)
                    low_y(0, 0)
                    prep_kv(0)
                    tiles(nc.vector, tile, own, 42)

        def turns(engine, n, body, own=None, per_turn=0):
            body(0)
            with engine.Fori(1, n) as u:
                if own:
                    own.loop(u - 1, per_turn)
                body(u)
            if own:
                own.done(n - 1)

        def row_stats(own, t, place):
            nc.vector.sem_inc(waits_over)
            own.link(nc.vector.bn_stats(stats[:, place, :], at(x_all, t)))
            nc.vector.sem_inc(waits_over)
            own.link(nc.vector.bn_aggr(moments[:, place, :], stats[:, place, :]))
            own.mark(nc.vector.tensor_scalar(at(mv, t), moments[:, place, :], 1.0, None, ALU.mult))

        def staged(engine, stages, depth, own=None, per_pair=0):
            peeled = depth + 2 + depth % 2

            def slot(t, parity):
                for stage, lag in stages:
                    if not isinstance(t, int) or 0 <= t - lag < T:
                        stage(t - lag, (parity - lag) % 2)

            for t in range(peeled):
                slot(t, t % 2)
            with engine.Fori(peeled // 2, T // 2) as u:
                if own:
                    own.loop(u - peeled // 2, per_pair)
                slot(2 * u, 0)
                slot(2 * u + 1, 1)
            if own:
                own.done(T // 2 - peeled // 2)
            for t in range(T, T + depth):
                slot(t, t % 2)

        class RowStats:

            def __init__(self, name, updated):
                self.updated = updated
                self.summed, self.aggregated = sem(name + "_summed"), sem(name + "_aggregated")

            def first(self, k, place):
                at_least(nc.vector, self.updated, k + 1)
                nc.vector.sem_inc(waits_over)
                nc.vector.bn_stats(stats[:, place, :], at(x_all, k)).then_inc(self.summed, 1)

            def second(self, k, place):
                at_least(nc.vector, self.summed, k + 1)
                nc.vector.sem_inc(waits_over)
                nc.vector.bn_aggr(moments[:, place, :], stats[:, place, :]).then_inc(self.aggregated, 1)

            def third(self, k, place):
                at_least(nc.vector, self.aggregated, k + 1)
                own.mark(nc.vector.tensor_scalar(at(mv, k), moments[:, place, :], 1.0, None, ALU.mult))

        r_all = O.enter_context(nc.sbuf_tensor("r_all", [P, T, 2 * NC], f32))
        rt = O.enter_context(nc.sbuf_tensor("rt", [P, 2, 2 * NC, C], f32))
        scaled = O.enter_context(nc.sbuf_tensor("scaled", [P, 2, N], f32))
        norm_ready = sem("norm_ready")
        rt_ready = sem("rt_ready")
        spread = sem("spread")
        x_normed = sem("x_normed")
        updated = sem("updated")
        with nc.Block() as block:
            @block.scalar
            def _(act):
                act.wait_ge(norm_ready, 1)

                def factors(k, place):
                    at_least(act, spread, k - 1)
                    source = at(r_all, k) if isinstance(k, int) else at(r_all, k).rearrange("p a k -> p (a k)")
                    nc.scalar.activation(rt[:, place, :, :], source.unsqueeze(2).broadcast_to([P, 2 * NC, C]),
                                         ACT.Copy).then_inc(rt_ready, 1)

                staged(nc.scalar, ((factors, 0),), 3)

            @block.tensor
            def _(pe):
                def spreading(k, place):
                    at_least(pe, rt_ready, k + 1)
                    at_least(pe, x_normed, k - 1)
                    for i in range(NC):
                        last = nc.tensor.matmul(psum[place][:, i * P:(i + 1) * P],
                                                rt[:, place, 2 * i:2 * i + 2, :].rearrange("p b c -> p (b c)"),
                                                ident, start=True, stop=True)
                    last.then_inc(spread, 1)

                staged(nc.tensor, ((spreading, 0),), 3)

            @block.vector
            def _(dve):
                flat, rflat = ss[:, :, :].rearrange("p t k -> p (t k)"), r_all[:, :, :].rearrange("p t k -> p (t k)")
                own.link(nc.vector.tensor_scalar(flat, flat, 1e-24, None, ALU.max))
                rsqrt(own, flat, rflat, ln_tmp[:, 0, :], ln_tmp[:, 1, :])
                nc.vector.tensor_copy(ln_tmp[:, 0, 0:1], rflat[:, 0:1]).then_inc(norm_ready, 1)

                def scale(k, place):
                    at_least(dve, spread, k + 1)
                    nc.vector.tensor_tensor(scaled[:, place, :], at(o_all, k), psum[place][:, :],
                                            ALU.mult).then_inc(x_normed, 1)

                def update(k, place):
                    at_least(dve, x_normed, k + 1)
                    nc.vector.scalar_tensor_tensor(out=at(x_all, k), in0=scaled[:, place, :],
                                                   scalar=gain0[:, :], in1=at(x_all, k),
                                                   op0=ALU.mult, op1=ALU.add).then_inc(updated, 1)

                rows = RowStats("a2", updated)
                staged(nc.vector, ((scale, 1), (rows.third, 3), (rows.first, 2), (update, 1), (rows.second, 2)),
                       3, own, 2)
                own.wait()
                ln_rstd(own)
        O.close()

        H = ExitStack()
        zz = H.enter_context(nc.sbuf_tensor("zz", [P, T, S * S], f32))
        pp = H.enter_context(nc.sbuf_tensor("pp", [P, T, 2, S], f32))

        with ExitStack() as R:
            y2 = R.enter_context(nc.sbuf_tensor("y2a", [P, 2, N], f32))
            yT = R.enter_context(nc.sbuf_tensor("yT", [P, 2, NC, P], f32))
            y_ready, y_turned, yT_ready, lg_done, lg_copied = (
                sem(n) for n in ("y_ready", "y_turned", "yT_ready", "lg_done", "lg_copied"))
            with nc.Block() as block:
                @block.vector
                def _(dve):
                    def norm(k, place):
                        at_least(dve, y_turned, k - 1)
                        nc.vector.tensor_scalar(y2[:, place, :], at(x_all, k), at(mv, k, slice(0, 1)), at(rstd, k),
                                                ALU.subtract, ALU.mult).then_inc(y_ready, 1)

                    staged(nc.vector, ((norm, 0),), 1)
                    ms, v = ln_tmp[:, 0, 0:T], ln_tmp[:, 0, T:2 * T]
                    own.link(nc.vector.tensor_tensor(ms, rstd[:, :], rstd[:, :], ALU.mult))
                    own.link(nc.vector.tensor_tensor(ms, ms, mv[:, :, 1], ALU.mult))
                    own.link(nc.vector.tensor_scalar(v, ms, RMS_EPS, None, ALU.add))
                    rsqrt(own, v, ms, ln_tmp[:, 1, 0:T], ln_tmp[:, 1, T:2 * T])
                    at_least(dve, lg_copied, T)
                    own.link(nc.vector.tensor_tensor(lg[:, :, :], lg[:, :, :],
                                                     ms.unsqueeze(2).broadcast_to([P, T, 24]), ALU.mult))
                    own.link(nc.vector.tensor_tensor(lg[:, :, :], lg[:, :, :],
                                                     b24_sb[:, :].unsqueeze(1).broadcast_to([P, T, 24]), ALU.add))

                @block.tensor
                def _(pe):
                    def turn(k, place):
                        at_least(pe, y_ready, k + 1)
                        at_least(pe, yT_ready, k - 1)
                        for c in range(NC):
                            last = nc.tensor.transpose(psum[place][:, c * P:(c + 1) * P],
                                                       y2[:, place, c * P:(c + 1) * P], ident)
                        last.then_inc(y_turned, 1)

                    def logits(k, place):
                        at_least(pe, yT_ready, k + 1)
                        at_least(pe, lg_copied, k - 1)
                        for c in range(NC):
                            last = nc.tensor.matmul(psum[4 + place][:, 0:24], yT[:, place, c, :], w24_sb[:, c, :],
                                                    start=(c == 0), stop=(c == NC - 1))
                        last.then_inc(lg_done, 1)

                    staged(nc.tensor, ((turn, 0), (logits, 1)), 1)

                @block.scalar
                def _(act):
                    def copy(k, place):
                        at_least(act, y_turned, k + 1)
                        at_least(act, lg_done, k - 1)
                        nc.scalar.activation(yT[:, place, :, :].rearrange("p c n -> p (c n)"), psum[place][:, :],
                                             ACT.Copy).then_inc(yT_ready, 1)

                    def store(k, place):
                        at_least(act, lg_done, k + 1)
                        nc.scalar.activation(at(lg, k), psum[4 + place][:, 0:24], ACT.Copy).then_inc(lg_copied, 1)

                    staged(nc.scalar, ((copy, 0), (store, 1)), 1)


        with ExitStack() as R:
            def rb(name, shape):
                return R.enter_context(nc.sbuf_tensor(name, shape, f32))

            kern, work = rb("kern", [P, T, S * S]), rb("work", [P, T, S * S])
            mxs, sums, ra, cb, logs = (rb(n, [P, T * S]) for n in ("mxs", "sums", "ra", "cb", "logs"))
            csum = rb("csum", [P, T * S])
            to_act, from_act = sem("to_act"), sem("from_act")
            calls = Count(nc.vector, from_act)

            def by_row(z):
                return z[:, :, :].rearrange("p t (i j) -> p (t i) j", j=S)

            def by_column(z):
                return z[:, :, :].rearrange("p t (i j) -> p t j i", j=S)

            def over_j(v):
                return v[:, :].unsqueeze(2).broadcast_to([P, T * S, S])

            def grid(z):
                return z[:, :, :].rearrange("p t (i j) -> p t i j", j=S)

            def over_i(v):
                return v[:, :].rearrange("p (t j) -> p t j", j=S).unsqueeze(2).broadcast_to([P, T, S, S])

            def flat(z):
                return z[:, :, :].rearrange("p t k -> p (t k)")

            pf = pp[:, :, :, :].rearrange("p t a k -> p (t a) k")
            with nc.Block() as block:
                @block.scalar
                def _(act):
                    n = [0]

                    def answer(out_, in_, func, index=None, **kw):
                        n[0] += 1
                        at_least(act, to_act, n[0] if index is None else 3 * index + n[0])
                        nc.scalar.activation(out_, in_, func, **kw).then_inc(from_act, 1)

                    answer(flat(work), flat(work), ACT.Exp)
                    answer(logs[:, :], sums[:, :], ACT.Ln)
                    answer(flat(work), flat(work), ACT.Exp)
                    answer(logs[:, :], sums[:, :], ACT.Ln)
                    answer(flat(kern), flat(zz), ACT.Exp)
                    with nc.scalar.Fori(0, REFRESHES) as k:
                        answer(mxs[:, :], sums[:, :], ACT.Ln, k)
                        answer(logs[:, :], csum[:, :], ACT.Ln, k)
                        answer(flat(kern), flat(zz), ACT.Exp, k)
                    n[0] += 3 * (REFRESHES - 1)
                    answer(pp[:, :, :, :].rearrange("p t a k -> p (t a k)"),
                           pp[:, :, :, :].rearrange("p t a k -> p (t a k)"), ACT.Exp)
                    answer(sgt[:, 0:1], sg_sb[:, :], ACT.Exp, scale=-1.0)

                @block.vector
                def _(dve):
                    V = nc.vector

                    def ask(instruction, wait=True):
                        instruction.then_inc(to_act, 1)
                        calls.value += 1
                        if wait:
                            calls.wait()

                    own.link(V.tensor_scalar(zz[:, :, :], lg[:, :, 0:S * S], 1.0 / TAU, None, ALU.mult))
                    own.link(V.tensor_reduce(mxs[:, :], by_row(zz), AX, ALU.max))
                    own.link(V.tensor_tensor(by_row(zz), by_row(zz), over_j(mxs), ALU.subtract))
                    ask(V.tensor_copy(flat(work), flat(zz)))
                    ask(V.reduce_sum(sums[:, :], by_row(work), axis=AX))
                    own.link(V.tensor_tensor(by_row(zz), by_row(zz), over_j(logs), ALU.subtract))
                    own.link(V.tensor_reduce(mxs[:, :].rearrange("p (t j) -> p t j", j=S), by_column(zz), AX, ALU.max))
                    own.link(V.tensor_tensor(grid(zz), grid(zz), over_i(mxs), ALU.subtract))
                    ask(V.tensor_copy(flat(work), flat(zz)))
                    ask(V.reduce_sum(sums[:, :].rearrange("p (t j) -> p t j", j=S), by_column(work), axis=AX))
                    ask(V.tensor_tensor(grid(zz), grid(zz), over_i(logs), ALU.subtract))
                    def scale_columns(out_):
                        own.link(V.tensor_tensor(grid(out_), grid(work if out_ is kern else kern), over_i(cb), ALU.mult))

                    def steps(count):
                        for n in range(count):
                            if n:
                                own.link(V.reciprocal(cb[:, :], csum[:, :]))
                                scale_columns(work)
                            own.link(V.reduce_sum(sums[:, :], by_row(work if n else kern), axis=AX))
                            own.link(V.reciprocal(ra[:, :], sums[:, :]))
                            own.link(V.tensor_tensor(by_row(work), by_row(kern), over_j(ra), ALU.mult))
                            own.link(V.reduce_sum(csum[:, :].rearrange("p (t j) -> p t j", j=S), by_column(work), axis=AX))

                    with V.Fori(0, REFRESHES) as k:
                        own.loop(k, 6 * BLOCK - 1)
                        calls.loop(k, 3)
                        steps(BLOCK)
                        ask(V.tensor_copy(cb[:, 0:1], csum[:, 0:1]), wait=False)
                        ask(V.tensor_copy(ra[:, 0:1], sums[:, 0:1]))
                        own.link(V.tensor_tensor(by_row(zz), by_row(zz), over_j(mxs), ALU.subtract))
                        ask(V.tensor_tensor(grid(zz), grid(zz), over_i(logs), ALU.subtract))
                        own.done(REFRESHES)
                        calls.done(REFRESHES)
                    steps(LAST)
                    own.link(V.reciprocal(cb[:, :], csum[:, :]))
                    scale_columns(kern)
                    pm_ = mxs[:, 0:2 * T]
                    own.link(V.tensor_copy(pf, lg[:, :, S * S:24].rearrange("p t (a k) -> p t a k", k=S)))
                    own.link(V.tensor_reduce(pm_, pf, AX, ALU.max))
                    ask(V.tensor_tensor(pf, pf, pm_.unsqueeze(2).broadcast_to([P, 2 * T, S]), ALU.subtract))
                    own.link(V.reduce_sum(pm_, pf, axis=AX))
                    own.link(V.reciprocal(sums[:, 0:2 * T], pm_))
                    own.link(V.tensor_tensor(pf, pf, sums[:, 0:2 * T].unsqueeze(2).broadcast_to([P, 2 * T, S]), ALU.mult))
                    ask(V.tensor_copy(logs[:, 0:1], pm_[:, 0:1]))
                    own.link(V.tensor_scalar(sgt[:, 1:2], sgt[:, 0:1], 1.0, None, ALU.add))
                    own.link(V.reciprocal(sgt[:, 2:3], sgt[:, 1:2]))
                    own.link(V.tensor_tensor(sgt[:, 3:4], sgt[:, 0:1], sgt[:, 2:3], ALU.mult))
                    own.link(V.tensor_scalar(zz[:, :, :], kern[:, :, :], sgt[:, 2:3], None, ALU.mult))
                    own.link(V.tensor_scalar(zz[:, :, 0:S * S:S + 1], zz[:, :, 0:S * S:S + 1], sgt[:, 3:4], None, ALU.add))
                    own.link(V.tensor_scalar(zz[:, :, :], zz[:, :, :], tanh_g[:, 2:3], None, ALU.mult))
                    own.link(V.tensor_scalar(pp[:, :, 1, :], pp[:, :, 1, :], tanh_g[:, 2:3], None, ALU.mult))

        with ExitStack() as R:
            y2 = R.enter_context(nc.sbuf_tensor("y2", [P, 2, N], f32))
            pre = R.enter_context(nc.sbuf_tensor("pre", [P, 2, S, P], f32))
            mixer = R.enter_context(nc.sbuf_tensor("mixer", [P, 2, S * S, P], f32))
            xpT = R.enter_context(nc.sbuf_tensor("xpT", [P, 2, P], f32))
            names = ("c1_y", "pre_ready", "mixer_pool", "mixer_act", "xp_done", "xpT_ready", "mix_done", "yb_done", "mixed")
            y_rdy, pre_ready, mixer_pool, mixer_act, xp_done, xpT_ready, mix_done, yb_done, mixed = (sem(n) for n in names)
            SHARE = 8

            with nc.Block() as block:
                @block.tensor
                def _(pe):
                    def pair(u):
                        for i in range(2):
                            t = 2 * u + i
                            at_least(pe, y_rdy, t + 1)
                            at_least(pe, pre_ready, t + 1)
                            for j in range(S):
                                last = nc.tensor.matmul(psum[i][:, 0:P], y2[:, i, j * P:(j + 1) * P], pre[:, i, j, :],
                                                        start=(j == 0), stop=(j == S - 1))
                            last.then_inc(xp_done, 1)
                            at_least(pe, mixer_pool, t + 1)
                            at_least(pe, mixer_act, t + 1)
                            at_least(pe, mixed, t - 1)
                            for k in range(S):
                                for j in range(S):
                                    last = nc.tensor.matmul(psum[4 + i][:, k * P:(k + 1) * P], mixer[:, i, S * k + j, :],
                                                            y2[:, i, j * P:(j + 1) * P], start=(j == 0), stop=(j == S - 1))
                            last.then_inc(mix_done, 1)
                            at_least(pe, xpT_ready, t + 1)
                            nc.tensor.matmul(psum[2 + i][:, 0:P], xpT[:, i, :], wb_sb[:, :],
                                             start=True, stop=True).then_inc(yb_done, 1)

                    turns(nc.tensor, T // 2, pair)

                @block.gpsimd
                def _(pool):
                    def diagonals(out_, weights, count):
                        return nc.gpsimd.tensor_tensor(
                            out_, ident.unsqueeze(1).broadcast_to([P, count, P]),
                            weights.unsqueeze(2).broadcast_to([P, count, P]), ALU.mult)

                    def pair(u):
                        for i in range(2):
                            t = 2 * u + i
                            at_least(pool, mix_done, t - 1)
                            nc.gpsimd.sem_inc(pool_passed)
                            if isinstance(t, int):
                                first, rest = pp[:, t, 0, :], zz[:, t, 0:SHARE]
                            else:
                                first = pp[:, bass.ds(t, 1), 0, :].rearrange("p a k -> p (a k)")
                                rest = zz[:, bass.ds(t, 1), 0:SHARE].rearrange("p a k -> p (a k)")
                            diagonals(pre[:, i, :, :], first, S).then_inc(pre_ready, 1)
                            diagonals(mixer[:, i, 0:SHARE, :], rest, SHARE).then_inc(mixer_pool, 1)

                    turns(nc.gpsimd, T // 2, pair)

                @block.scalar
                def _(act):
                    def pair(u):
                        for i in range(2):
                            t = 2 * u + i
                            at_least(act, mix_done, t - 1)
                            for k in range(SHARE, S * S):
                                last = nc.scalar.activation(mixer[:, i, k, :], ident, ACT.Copy,
                                                            scale=at(zz, t, slice(k, k + 1)))
                            last.then_inc(mixer_act, 1)
                            at_least(act, xp_done, t + 1)
                            nc.scalar.activation(xpT[:, i, :], psum[i][:, 0:P], ACT.Copy).then_inc(xpT_ready, 1)

                    turns(nc.scalar, T // 2, pair)

                @block.vector
                def _(dve):
                    V = nc.vector

                    def norm(t, i):
                        V.tensor_scalar(y2[:, i, :], at(x_all, t), at(mv, t, slice(0, 1)), at(rstd, t),
                                        ALU.subtract, ALU.mult).then_inc(y_rdy, 1)

                    def update(t, i):
                        dve.wait_ge(mix_done, t + 1)
                        own.link(V.tensor_tensor(at(x_all, t), at(x_all, t), psum[4 + i][:, :], ALU.add))
                        dve.wait_ge(yb_done, t + 1)
                        for k in range(S):
                            stream = at(x_all, t, slice(k * P, (k + 1) * P))
                            last = V.scalar_tensor_tensor(out=stream, in0=psum[2 + i][:, 0:P],
                                                          scalar=at(pp, t, 1, slice(k, k + 1)), in1=stream,
                                                          op0=ALU.mult, op1=ALU.add)
                            if k < S - 1:
                                own.mark(last)
                            else:
                                last.then_inc(mixed, 1)
                        own.wait()
                        dve.wait_ge(mixed, t + 1)
                        row_stats(own, t, i)

                    norm(0, 0)
                    norm(1, 1)
                    with V.Fori(0, T // 2 - 1) as u:
                        own.loop(u, 2 * (1 + S - 1 + 3))
                        for i in range(2):
                            update(2 * u + i, i)
                            norm(2 * u + 2 + i, i)
                        own.done(T // 2 - 1)
                    update(T - 2, 0)
                    update(T - 1, 1)
                    own.wait()
                    ln_rstd(own)
        H.close()

        with ExitStack() as R:
            def rc(name, shape):
                return R.enter_context(nc.sbuf_tensor(name, shape, f32))

            NG = N // DH1
            y2c, q2, e2, p2, qT = (rc(n, [P, 2, N]) for n in ("y2c", "q2", "e2", "p2", "qT"))
            mx2, su2, rc2 = (rc(n, [P, 2, NG]) for n in ("mx2", "su2", "rc2"))
            kvf = rc("kvf", [P, 2, P])
            names = ("c2_y", "c2_yT", "c2_sub", "c2_exp", "c2_rcp", "c2_p", "c2_pT", "c2_qT", "c2_o", "c2_kv", "c2_x")
            y_rdy, y_trn, sub_rdy, exp_rdy, rcp_rdy, p_rdy, p_trn, qT_rdy, o_rdy, kvf_rdy, x_rdy = (sem(n) for n in names)
            DEPTH = 4

            def grouped(z):
                return z.rearrange("p (g d) -> p g d", d=DH1)

            def spread_g(v):
                return v.unsqueeze(2).broadcast_to([P, NG, DH1])

            with nc.Block() as block:
                @block.tensor
                def _(pe):
                    def turn(k, place):
                        at_least(pe, y_rdy, k + 1)
                        at_least(pe, sub_rdy, k - 1)
                        for c in range(NC):
                            last = nc.tensor.transpose(psum[place][:, c * P:(c + 1) * P],
                                                       y2c[:, place, c * P:(c + 1) * P], ident)
                        last.then_inc(y_trn, 1)

                    def back(k, place):
                        at_least(pe, p_rdy, k + 1)
                        at_least(pe, qT_rdy, k - 1)
                        for c in range(NC):
                            last = nc.tensor.transpose(psum[2 + place][:, c * P:(c + 1) * P],
                                                       p2[:, place, c * P:(c + 1) * P], ident)
                        last.then_inc(p_trn, 1)

                    def product(k, place):
                        at_least(pe, qT_rdy, k + 1)
                        at_least(pe, kvf_rdy, k + 1)
                        at_least(pe, x_rdy, k - 1)
                        nc.tensor.matmul(psum[4 + place][:, :], kvf[:, place, :], qT[:, place, :],
                                         start=True, stop=True).then_inc(o_rdy, 1)

                    staged(nc.tensor, ((back, 3), (turn, 0), (product, 3)), DEPTH)

                @block.scalar
                def _(act):
                    def exps(k, place):
                        at_least(act, sub_rdy, k + 1)
                        at_least(act, p_rdy, k - 1)
                        nc.scalar.activation(e2[:, place, :], q2[:, place, :], ACT.Exp).then_inc(exp_rdy, 1)

                    def copy(k, place):
                        at_least(act, p_trn, k + 1)
                        at_least(act, o_rdy, k - 1)
                        nc.scalar.activation(qT[:, place, :], psum[2 + place][:, :], ACT.Copy).then_inc(qT_rdy, 1)

                    staged(nc.scalar, ((copy, 3), (exps, 1)), DEPTH)

                @block.gpsimd
                def _(pool):
                    def keys_values(k, place):
                        at_least(pool, o_rdy, k - 1)
                        nc.gpsimd.sem_inc(pool_passed)
                        nc.gpsimd.tensor_copy(kvf[:, place, :], at(kv1_all, k)).then_inc(kvf_rdy, 1)

                    def probs(k, place):
                        at_least(pool, rcp_rdy, k + 1)
                        at_least(pool, p_trn, k - 1)
                        nc.gpsimd.tensor_tensor(grouped(p2[:, place, :]), grouped(e2[:, place, :]),
                                                spread_g(rc2[:, place, :]), ALU.mult).then_inc(p_rdy, 1)

                    staged(nc.gpsimd, ((probs, 2), (keys_values, 2)), DEPTH)

                @block.vector
                def _(dve):
                    V = nc.vector
                    maxima, totals = [], []
                    rows = RowStats("c2", x_rdy)

                    def norm(k, place):
                        at_least(dve, y_trn, k - 1)
                        V.tensor_scalar(y2c[:, place, :], at(x_all, k), at(mv, k, slice(0, 1)), at(rstd, k),
                                        ALU.subtract, ALU.mult).then_inc(y_rdy, 1)

                    def update(k, place):
                        at_least(dve, o_rdy, k + 1)
                        V.scalar_tensor_tensor(out=at(x_all, k), in0=psum[4 + place][:, :],
                                               scalar=tanh_g[:, 1:2], in1=at(x_all, k),
                                               op0=ALU.mult, op1=ALU.add).then_inc(x_rdy, 1)

                    def row_maxima(k, place):
                        at_least(dve, y_trn, k + 1)
                        maxima.append(own.mark(V.tensor_reduce(mx2[:, place, :], grouped(psum[place][:, :]), AX, ALU.max)))

                    def shift(k, place):
                        own.wait(maxima.pop())
                        at_least(dve, exp_rdy, k - 1)
                        V.tensor_tensor(grouped(q2[:, place, :]), grouped(psum[place][:, :]), spread_g(mx2[:, place, :]),
                                        ALU.subtract).then_inc(sub_rdy, 1)

                    def sums_(k, place):
                        at_least(dve, exp_rdy, k + 1)
                        totals.append(own.mark(V.reduce_sum(su2[:, place, :], grouped(e2[:, place, :]), axis=AX)))

                    def inverse(k, place):
                        own.wait(totals.pop())
                        at_least(dve, p_rdy, k - 1)
                        V.reciprocal(rc2[:, place, :], su2[:, place, :]).then_inc(rcp_rdy, 1)

                    staged(nc.vector, ((norm, 0), (update, 4), (row_maxima, 1), (rows.first, 4), (shift, 1),
                                       (rows.second, 4), (sums_, 2), (rows.third, 4), (inverse, 2)),
                           DEPTH, own, 2 * 3)
                    own.wait()
                    ln_rstd(own)

        xh = sb("xh", [P, NC, ROWS], f32r)
        xl = sb("xl", [P, NC, ROWS], f32r)
        NEVER = 3.0e38
        sc = sb("sc", [P, T, E])
        padded = sb("padded", [P, T, E + TOPK])
        top = sb("top", [P, T, 8])
        left = sb("left", [P, T, E + TOPK])
        tot = sb("tot", [P, 2, T])
        names = ("c3_y", "c3_yT", "c3_hi", "c3_lo", "c3_gate", "c3_gatec", "c3_score", "c3_scorec", "c3_sub", "c3_exp")
        y_rdy, y_trn, hi_rdy, lo_rdy, gate_rdy, gate_cp, sco_rdy, sco_cp, exp_ask, exp_ans = (sem(n) for n in names)
        PAIRS = T // 2

        def pairs(engine, pair):
            pair(0)
            pair(1)
            with engine.Fori(2, PAIRS - 1) as u:
                pair(u)
            for u in range(PAIRS - 1, PAIRS + 2):
                pair(u)

        def exists(u):
            return not isinstance(u, int) or 0 <= u < PAIRS

        GU, DN = 2 * NC * IC * P, IC * N
        w32 = sb("w32", [P, GU + DN])
        wh, wl = [sb("wh0", [P, GU + DN], f32r)], [sb("wl0", [P, GU + DN], f32r)]
        w_loaded, w_high, w_split = sem("w_loaded"), sem("w_high"), sem("w_split")

        def load_weights(sp, row):
            sp.dma_start(w32[:, 0:GU], wgu[row, :]).then_inc(w_loaded, 16)
            sp.dma_start(w32[:, GU:GU + DN], wd[row, :]).then_inc(w_loaded, 16)

        def split_weights(pool, n, parity):
            nc.gpsimd.tensor_copy(wh[parity][:, :], w32[:, :]).then_inc(w_high, 1)
            pool.wait_ge(w_high, n + 1)
            nc.gpsimd.tensor_tensor(wl[parity][:, :], w32[:, :], wh[parity][:, :].bitcast(f32),
                                    ALU.subtract).then_inc(w_split, 1)

        with ExitStack() as R:
            def rd(name, shape):
                return R.enter_context(nc.sbuf_tensor(name, shape, f32))

            y2 = rd("y2d", [P, 2, N])
            s16 = rd("s16", [E, 2 * P])
            with nc.Block() as block:
                @block.sync
                def _(sp):
                    load_weights(sp, slice(0, P))
                    sp.wait_ge(w_split, 1)
                    load_weights(sp, slice(P, 2 * P))

                @block.gpsimd
                def _(pool):
                    pool.wait_ge(w_loaded, 32)
                    nc.gpsimd.sem_inc(pool_passed)
                    split_weights(pool, 0, 0)

                @block.vector
                def _(dve):
                    V = nc.vector

                    def norm(k, place):
                        V.tensor_scalar(y2[:, place, :], at(x_all, k), at(mv, k, slice(0, 1)), at(rstd, k),
                                        ALU.subtract, ALU.mult).then_inc(y_rdy, 1)

                    def low(k, place):
                        at_least(dve, hi_rdy, k + 1)
                        cols = bass.ds(k * P, P)
                        V.tensor_tensor(xl[:, :, cols], psum[place][:, :].rearrange("p (c n) -> p c n", n=P),
                                        xh[:, :, cols].bitcast(f32), ALU.subtract).then_inc(lo_rdy, 1)

                    def pair(u):
                        for place in range(2):
                            if exists(u + 1):
                                at_least(dve, y_trn, 2 * u + place + 1)
                                norm(2 * u + 2 + place, place)
                            if exists(u):
                                low(2 * u + place, place)
                        if exists(u - 2):
                            at_least(dve, sco_rdy, u - 1)
                            V.tensor_copy(sc[:, bass.ds(2 * u - 4, 2), :],
                                          psum[5][:, 0:2 * E].rearrange("p (t e) -> p t e", e=E)).then_inc(sco_cp, 1)

                    norm(0, 0)
                    norm(1, 1)
                    pairs(nc.vector, pair)

                @block.scalar
                def _(act):
                    def pair(u):
                        if exists(u):
                            for place in range(2):
                                k = 2 * u + place
                                at_least(act, y_trn, k + 1)
                                nc.scalar.activation(xh[:, :, bass.ds(k * P, P)],
                                                     psum[place][:, :].rearrange("p (c n) -> p c n", n=P),
                                                     ACT.Copy).then_inc(hi_rdy, 1)
                        if exists(u - 1):
                            at_least(act, gate_rdy, u)
                            at_least(act, sco_rdy, u - 1)
                            nc.scalar.activation(s16[:, :], psum[4][0:E, 0:2 * P], ACT.Copy).then_inc(gate_cp, 1)

                    pairs(nc.scalar, pair)

                @block.tensor
                def _(pe):
                    def pair(u):
                        if exists(u):
                            for place in range(2):
                                k = 2 * u + place
                                at_least(pe, y_rdy, k + 1)
                                at_least(pe, lo_rdy, k - 1)
                                for c in range(NC):
                                    last = nc.tensor.transpose(psum[place][:, c * P:(c + 1) * P],
                                                               y2[:, place, c * P:(c + 1) * P], ident)
                                last.then_inc(y_trn, 1)
                        if exists(u - 2):
                            at_least(pe, gate_cp, u - 1)
                            at_least(pe, sco_cp, u - 2)
                            nc.tensor.sem_inc(pe_passed)
                            for i in range(2):
                                last = nc.tensor.transpose(psum[5][:, i * E:(i + 1) * E], s16[:, i * P:(i + 1) * P],
                                                           ident[0:E, 0:E])
                            last.then_inc(sco_rdy, 1)
                        if exists(u - 1):
                            at_least(pe, lo_rdy, 2 * u)
                            at_least(pe, gate_cp, u - 1)
                            cols = bass.ds(2 * P * u - 2 * P, 2 * P)
                            for c in range(NC):
                                for q, (w, v) in enumerate(((gwh, xh), (gwl, xh), (gwh, xl), (gwl, xl))):
                                    last = nc.tensor.matmul(psum[4][0:E, 0:2 * P], w[:, c, :], v[:, c, cols],
                                                            start=(c == 0 and q == 0), stop=(c == NC - 1 and q == 3))
                            last.then_inc(gate_rdy, 1)

                    pairs(nc.tensor, pair)


        with ExitStack() as R:
            wh.append(R.enter_context(nc.sbuf_tensor("wh1", [P, GU + DN], f32r)))
            wl.append(R.enter_context(nc.sbuf_tensor("wl1", [P, GU + DN], f32r)))
            sg2 = R.enter_context(nc.sbuf_tensor("sg2", [P, IC, 512], f32))
            z32 = R.enter_context(nc.sbuf_tensor("z32", [P, IC, 512], f32))
            zh = R.enter_context(nc.sbuf_tensor("zh", [P, 2, IC, 512], f32r))
            zl = R.enter_context(nc.sbuf_tensor("zl", [P, 2, IC, 512], f32r))
            names = ("gu_done", "silu_done", "z_mult", "z_ready", "down_done", "acc_done")
            gu_done, silu_done, z_mult, z_ready, down_done, acc_done = (sem(n) for n in names)

            def all_experts(engine, expert, count=None, per_turn=0):
                expert(0, 0, False)
                with engine.Fori(0, E // 2) as u:
                    if count:
                        count.loop(u, 2 * per_turn)
                    expert(2 * u + 1, 1, True)
                    expert(2 * u + 2, 0, True)
                if count:
                    count.done(E // 2)

            with nc.Block() as block:
                @block.sync
                def _(sp):
                    with sp.Fori(2, E + 1) as n:
                        row = sp.snap(n * P)
                        sp.wait_ge(w_split, sp.snap(n + 0))
                        sp.sem_inc(sp_passed)
                        load_weights(sp, bass.ds(row, P))
                    for tb in range(TB):
                        sp.wait_ge(acc_done, 4 * (TB * E + tb + 1))
                        sp.dma_start(out[512 * tb:512 * tb + 512, :].rearrange("(t p) n -> p t n", p=P),
                                     x_all[:, 4 * tb:4 * tb + 4, :]).then_inc(out_stored, 16)
                    sp.wait_ge(out_stored, 16 * TB)

                @block.gpsimd
                def _(pool):
                    def split(n, parity):
                        pool.wait_ge(w_loaded, 32 * n + 32)
                        at_least(pool, down_done, 4 * TB * (n - 1))
                        nc.gpsimd.sem_inc(pool_passed)
                        split_weights(pool, n, parity)

                    split(1, 1)
                    split(2, 0)
                    with nc.gpsimd.Fori(1, E // 2) as u:
                        split(2 * u + 1, 1)
                        split(2 * u + 2, 0)

                @block.tensor
                def _(pe):
                    def gate_up(n, parity, tb, ic):
                        hi, lo = wh[parity], wl[parity]
                        k = TB * n + tb
                        at_least(pe, z_ready, 2 * k - 1 + ic)
                        if tb == 0 and ic == 0:
                            pe.wait_ge(w_split, n + 1)
                        for m in range(2):
                            for c in range(NC):
                                first = ((m * NC) + c) * IC * P + ic * P
                                cols = slice(512 * tb, 512 * tb + 512)
                                for q, (w, v) in enumerate(((hi, xh), (lo, xh), (hi, xl))):
                                    last = nc.tensor.matmul(psum[2 * ic + m][:, :], w[:, first:first + P], v[:, c, cols],
                                                            start=(c == 0 and q == 0), stop=(c == NC - 1 and q == 2))
                        last.then_inc(gu_done, 1)

                    def down(n, parity, tb):
                        hi, lo = wh[parity], wl[parity]
                        k = TB * n + tb
                        pe.wait_ge(z_ready, 2 * k + 2)
                        at_least(pe, acc_done, 4 * k)
                        for tt in range(4):
                            for ic in range(IC):
                                first = GU + ic * N
                                cols = slice(tt * P, tt * P + P)
                                for q, (z, w) in enumerate(((zh, hi), (zh, lo), (zl, hi))):
                                    last = nc.tensor.matmul(psum[4 + tt][:, :], z[:, tb % 2, ic, cols],
                                                            w[:, first:first + N], start=(ic == 0 and q == 0),
                                                            stop=(ic == IC - 1 and q == 2))
                            last.then_inc(down_done, 1)

                    def expert(n, parity, carry):
                        for tb in range(TB):
                            gate_up(n, parity, tb, 0)
                            gate_up(n, parity, tb, 1)
                            if tb:
                                down(n, parity, tb - 1)
                            elif carry:
                                down(n - 1, 1 - parity, TB - 1)

                    all_experts(nc.tensor, expert)
                    down(E, 0, TB - 1)

                @block.scalar
                def _(act):
                    def expert(n, parity, carry):
                        for tb in range(TB):
                            for ic in range(IC):
                                k = TB * n + tb
                                act.wait_ge(gu_done, 2 * k + ic + 1)
                                at_least(act, z_mult, 2 * k + ic - 1)
                                nc.scalar.activation(sg2[:, ic, :], psum[2 * ic][:, :], ACT.Silu).then_inc(silu_done, 1)

                    act.wait_ge(exp_ask, 1)
                    flat_sc = sc[:, :, :].rearrange("p t e -> p (t e)")
                    nc.scalar.activation(flat_sc, flat_sc, ACT.Exp, scale=-1.0).then_inc(exp_ans, 1)
                    all_experts(nc.scalar, expert)

                @block.vector
                def _(dve):
                    V = nc.vector

                    def hidden(n, tb, ic):
                        k = TB * n + tb
                        dve.wait_ge(silu_done, 2 * k + ic + 1)
                        V.tensor_tensor(z32[:, ic, :], sg2[:, ic, :], psum[2 * ic + 1][:, :],
                                        ALU.mult).then_inc(z_mult, 1)
                        dve.wait_ge(z_mult, 2 * k + ic + 1)
                        at_least(dve, down_done, 4 * (k - 1))
                        own.link(V.tensor_copy(zh[:, tb % 2, ic, :], z32[:, ic, :]))
                        V.tensor_tensor(zl[:, tb % 2, ic, :], z32[:, ic, :], zh[:, tb % 2, ic, :].bitcast(f32),
                                        ALU.subtract).then_inc(z_ready, 1)

                    def add(n, tb):
                        for tt in range(4):
                            t = 4 * tb + tt
                            dve.wait_ge(down_done, 4 * (TB * n + tb) + tt + 1)
                            V.scalar_tensor_tensor(out=x_all[:, t, :], in0=psum[4 + tt][:, :],
                                                   scalar=at(cw, n, slice(t, t + 1)), in1=x_all[:, t, :],
                                                   op0=ALU.mult, op1=ALU.add).then_inc(acc_done, 1)

                    def expert(n, parity, carry):
                        for tb in range(TB):
                            hidden(n, tb, 0)
                            hidden(n, tb, 1)
                            if tb:
                                add(n, tb - 1)
                            elif carry:
                                add(n - 1, TB - 1)

                    flat_sc = sc[:, :, :].rearrange("p t e -> p (t e)")
                    V.tensor_copy(tot[:, 0, 0:1], flat_sc[:, 0:1]).then_inc(exp_ask, 1)
                    dve.wait_ge(exp_ans, 1)
                    own.link(V.tensor_scalar(flat_sc, flat_sc, 1.0, None, ALU.add))
                    own.link(V.reciprocal(flat_sc, flat_sc))
                    own.link(V.tensor_tensor(sc[:, :, :], sc[:, :, :],
                                             bias_sb[:, :].unsqueeze(1).broadcast_to([P, T, E]), ALU.add))
                    own.mark(V.memset(padded[:, :, E:E + TOPK], NEVER))
                    own.mark(V.memset(cw[:, :, :], 1.0))
                    own.link(V.tensor_copy(padded[:, :, 0:E], sc[:, :, :]))
                    for t in range(T):
                        own.mark(V.max(out=top[:, t, :], in_=padded[:, t, 0:E]))
                    own.wait()
                    own.link(V.memset(top[:, :, TOPK:8], NEVER))
                    for t in range(T):
                        own.mark(V.match_replace(out=left[:, t, :], in_to_replace=top[:, t, :], in_values=padded[:, t, :],
                                                 imm_value=-NEVER))
                    own.wait()
                    own.link(V.tensor_scalar(left[:, :, 0:E], left[:, :, 0:E], -1.0e38, None, ALU.is_lt))
                    own.link(V.tensor_tensor(left[:, :, 0:E], left[:, :, 0:E], sc[:, :, :], ALU.mult))
                    own.link(V.reduce_sum(tot[:, 0, :], left[:, :, 0:E], axis=AX))
                    own.link(V.tensor_scalar(tot[:, 0, :], tot[:, 0, :], 1e-20, None, ALU.add))
                    own.link(V.reciprocal(tot[:, 1, :], tot[:, 0, :]))
                    own.link(V.tensor_tensor(cw[:, 1:E + 1, :], left[:, :, 0:E].rearrange("p t e -> p e t"),
                                             tot[:, 1, :].unsqueeze(1).broadcast_to([P, E, T]), ALU.mult))
                    own.link(V.tensor_scalar(cw[:, :, :], cw[:, :, :], tanh_g[:, 3:4], None, ALU.mult))

                    all_experts(nc.vector, expert, own, IC * TB)
                    add(E, TB - 1)


def kernel(x, ctx_4096, g_xattn, g_ffn, L0_xattn_Wq, L0_xattn_Wk, L0_xattn_Wv, L0_xattn_Wo, L0_xattn_bo, L0_xattn_g,
           L0_ffn_W_res, L0_ffn_W_pre, L0_ffn_W_post, L0_ffn_H_res_base, L0_ffn_H_pre_base, L0_ffn_H_post_base,
           L0_ffn_gate, L0_ffn_W_branch, L1_ffn_gate_w, L1_ffn_bias, L1_ffn_Wg, L1_ffn_Wu, L1_ffn_Wd,
           L1_ffn_Sg, L1_ffn_Su, L1_ffn_Sd):
    import numpy as np
    import concourse.bacc as bacc
    from concourse.bass_utils import run_bass_kernel_spmd

    def a(v):
        return np.asarray(v)

    def rows(v, n=128):
        return np.broadcast_to(a(v).reshape(1, -1), (n, a(v).size))

    def twice(v):
        return np.concatenate([a(v), a(v)], axis=0)

    B, C, N = x.shape
    H = L1_ffn_Sg.shape[1]
    I = L1_ffn_Sg.shape[0]
    E = L1_ffn_Wg.shape[0]
    P = 128

    def by_partition(w):
        k, m = w.shape
        return w.reshape(k // P, P, m).transpose(1, 0, 2).reshape(P, -1)

    gates_up = [np.stack([by_partition(a(g).T), by_partition(a(u).T)], axis=1)
                for g, u in [(L1_ffn_Sg, L1_ffn_Su)] + list(zip(a(L1_ffn_Wg), a(L1_ffn_Wu)))]
    downs = [by_partition(a(d).T) for d in [L1_ffn_Sd] + list(a(L1_ffn_Wd))]
    consts = np.zeros((P, 2 * P + 2), np.float32)
    consts[:, :P] = np.eye(P)
    consts[:, P:2 * P] = np.kron(np.eye(P // 8), np.ones((8, 8)))
    consts[:, 2 * P:] = np.kron(np.eye(2), np.ones((P // 2, 1)))
    arrays = {
        "x": a(x).reshape(B * C, N),
        "ctx_kv": a(ctx_4096).reshape(B * C, N),
        "wq": twice(a(L0_xattn_Wq).T),
        "wk": twice(a(L0_xattn_Wk).T),
        "wv": a(L0_xattn_Wv),
        "wo": a(L0_xattn_Wo).T,
        "bo": twice(a(L0_xattn_bo).reshape(C, 1)),
        "rms_gain": twice(a(L0_xattn_g).reshape(C, 1)),
        "gates": rows(np.concatenate([a(g_xattn), a(g_ffn)])),
        "w24": np.concatenate([a(L0_ffn_W_res), a(L0_ffn_W_pre), a(L0_ffn_W_post)], axis=0).T,
        "base24": rows(np.concatenate([a(L0_ffn_H_res_base).reshape(-1), a(L0_ffn_H_pre_base), a(L0_ffn_H_post_base)])),
        "sig_gate": rows(L0_ffn_gate),
        "w_branch": a(L0_ffn_W_branch),
        "gate_w": a(L1_ffn_gate_w).T,
        "bias": rows(L1_ffn_bias),
        "wgu": np.stack(gates_up).reshape((E + 1) * P, -1),
        "wd": np.stack(downs).reshape((E + 1) * P, -1),
        "consts": consts,
    }
    arrays = {f"in_{k}": np.ascontiguousarray(v) for k, v in arrays.items()}
    nc = bacc.Bacc("TRN2", target_bir_lowering=False, num_devices=1)
    args = [nc.dram_tensor(k, v.shape, mybir.dt.from_np(v.dtype), kind="ExternalInput").ap() for k, v in arrays.items()]
    out = nc.dram_tensor("out", (B * C, N), mybir.dt.float32, kind="ExternalOutput").ap()
    flamingo_program(nc, *args, out)
    r = run_bass_kernel_spmd(nc, [arrays], core_ids=[0])
    return r.results[0]["out"].reshape(B, C, N)
```
